# Optimizing a Trainium2 kernel written in Bass

```python
import numpy as np
import jax
import jax.numpy as jnp

def _softmax(x, axis=-1):
    return jax.nn.softmax(x, axis=axis)

def _gelu(x):
    return jax.nn.gelu(x, approximate=True)

def _silu(x):
    return jax.nn.silu(x)

def _sigmoid(x):
    return jax.nn.sigmoid(x)

def _layernorm(x, axis=-1, eps=1e-05):
    m = jnp.mean(x, axis=axis, keepdims=True)
    v = jnp.var(x, axis=axis, keepdims=True)
    return (x - m) / jnp.sqrt(v + eps)

def _scatter_add(tgt, idx, src, axis=0):
    return tgt.at[idx].add(src)

def _segment_sum(src, seg, n):
    return jax.ops.segment_sum(src, seg, n)
kernel_name = 'mk_adj_preln_d4_adj_r2_c5be8b'

def setup_inputs(seed: int=0):
    np.random.seed(seed)
    _w = jnp.asarray

    def _rec_inputs():
        import jax
        import jax.numpy as jnp
        _gk = jax.random.key(seed)
        x = -0.0002037 + 1 * jax.random.normal(jax.random.fold_in(_gk, 1), (5000, 128), jnp.float32)
        _a = jax.random.bernoulli(jax.random.fold_in(_gk, 2), 0.0004, (5000, 5000))
        _af = _a.astype(jnp.float32)
        adj = _af
        return (x, adj)
    x, adj = _rec_inputs()

    def _L0_gnn_setup():
        import jax, jax.numpy as jnp
        import numpy as np
        N = 5000
        F = 128
        C = 16
        AL = 0.1
        EPS = 1e-12
        key = jax.random.key(seed)
        k1, k2, k3, k4 = jax.random.split(key, 4)
        A = (jax.random.uniform(k1, (N, N)) > 0.99).astype(jnp.float32)
        x = jax.random.normal(k2, (N, F), dtype=jnp.float32)
        h0 = jax.random.normal(k3, (N, F), dtype=jnp.float32)
        labels = jax.random.randint(k4, (N,), 0, C)
        y = jax.nn.one_hot(labels, C, dtype=jnp.float32)
        return {'input': x, 'A': A, 'h0': h0, 'y': y}
    _L0_gnn_all = _L0_gnn_setup()
    _L0_gnn_in = {k: v for k, v in _L0_gnn_all.items() if k in ('h0', 'y')}
    del _L0_gnn_all

    def _L1_gnn_setup():
        import jax, jax.numpy as jnp
        import numpy as np
        from jax import lax
        D_MODEL = 128
        D_STATE = 16
        D_CONV = 4
        EXPAND = 2
        D_INNER = EXPAND * D_MODEL
        DT_RANK = (D_MODEL + 15) // 16
        N = 2048
        EPS = 1e-05

        def _mamba(h, w_in, conv_w, conv_b, w_xp, w_dt, b_dt, A_log, D_skip, w_out):
            L = h.shape[0]
            xz = h @ w_in
            xc, z = (xz[:, :D_INNER], xz[:, D_INNER:])
            xpad = jnp.pad(xc, ((D_CONV - 1, 0), (0, 0)))
            xconv = sum((xpad[k:k + L] * conv_w[:, k] for k in range(D_CONV))) + conv_b
            u = jax.nn.silu(xconv)
            dbc = u @ w_xp
            dt = jax.nn.softplus(dbc[:, :DT_RANK] @ w_dt + b_dt)
            B = dbc[:, DT_RANK:DT_RANK + D_STATE]
            C = dbc[:, DT_RANK + D_STATE:]
            A = -jnp.exp(A_log)
            dA = jnp.exp(dt[:, :, None] * A[None])
            dBu = dt[:, :, None] * B[:, None, :] * u[:, :, None]

            def step(hst, inp):
                dAt, dBut, Ct = inp
                hst = dAt * hst + dBut
                return (hst, hst @ Ct)
            _, ys = lax.scan(step, jnp.zeros((D_INNER, D_STATE), h.dtype), (dA, dBu, C))
            y = ys + u * D_skip
            y = y * jax.nn.silu(z)
            return y @ w_out
        key = jax.random.key(seed)
        ks = jax.random.split(key, 16)
        x = jax.random.normal(ks[0], (N, D_MODEL), dtype=jnp.float32)
        a = jax.random.uniform(ks[1], (N, N), dtype=jnp.float32)
        adj = a / a.sum(axis=1, keepdims=True)
        s = lambda fi, fo: 1.0 / np.sqrt(fi)
        gcn_w = jax.random.uniform(ks[2], (D_MODEL, D_MODEL), jnp.float32, -s(D_MODEL, 0), s(D_MODEL, 0))
        gcn_b = jnp.zeros((D_MODEL,), jnp.float32)
        ln_g = jnp.ones((D_MODEL,), jnp.float32)
        ln_b = jnp.zeros((D_MODEL,), jnp.float32)
        w_in = jax.random.normal(ks[3], (D_MODEL, 2 * D_INNER), jnp.float32) * s(D_MODEL, 0)
        conv_w = jax.random.normal(ks[4], (D_INNER, D_CONV), jnp.float32) * s(D_CONV, 0)
        conv_b = jnp.zeros((D_INNER,), jnp.float32)
        w_xp = jax.random.normal(ks[5], (D_INNER, DT_RANK + 2 * D_STATE), jnp.float32) * s(D_INNER, 0)
        w_dt = jax.random.normal(ks[6], (DT_RANK, D_INNER), jnp.float32) * s(DT_RANK, 0)
        b_dt = jnp.log(jnp.expm1(jnp.exp(jax.random.uniform(ks[7], (D_INNER,), jnp.float32, np.log(0.001), np.log(0.1)))))
        A_log = jnp.log(jnp.broadcast_to(jnp.arange(1, D_STATE + 1, dtype=jnp.float32), (D_INNER, D_STATE)))
        D_skip = jnp.ones((D_INNER,), jnp.float32)
        w_out = jax.random.normal(ks[8], (D_INNER, D_MODEL), jnp.float32) * s(D_INNER, 0)
        return dict(x=x, adj=adj, gcn_w=gcn_w, gcn_b=gcn_b, ln_g=ln_g, ln_b=ln_b, w_in=w_in, conv_w=conv_w, conv_b=conv_b, w_xp=w_xp, w_dt=w_dt, b_dt=b_dt, A_log=A_log, D_skip=D_skip, w_out=w_out)
    _L1_gnn_all = _L1_gnn_setup()
    _L1_gnn_in = {k: v for k, v in _L1_gnn_all.items() if k in ('gcn_w', 'gcn_b', 'ln_g', 'ln_b', 'w_in', 'conv_w', 'conv_b', 'w_xp', 'w_dt', 'b_dt', 'A_log', 'D_skip', 'w_out')}
    del _L1_gnn_all

    def _L2_gnn_setup():
        import jax, jax.numpy as jnp
        import numpy as np
        MIN_NORM = 1e-15
        BALL_EPS = 1e-05
        C_IN = 1.0
        C_OUT = 1.0

        def _artanh(x):
            x = jnp.clip(x, -1.0 + 1e-07, 1.0 - 1e-07)
            return 0.5 * (jnp.log1p(x) - jnp.log1p(-x))

        def _norm(x):
            return jnp.maximum(jnp.linalg.norm(x, axis=-1, keepdims=True), MIN_NORM)

        def proj(x, c):
            norm = _norm(x)
            maxnorm = (1.0 - BALL_EPS) / jnp.sqrt(c)
            return jnp.where(norm > maxnorm, x / norm * maxnorm, x)

        def expmap0(u, c):
            sc = jnp.sqrt(c)
            un = _norm(u)
            return jnp.tanh(sc * un) * u / (sc * un)

        def logmap0(p, c):
            sc = jnp.sqrt(c)
            pn = _norm(p)
            return _artanh(sc * pn) * p / (sc * pn)

        def mobius_matvec(m, x, c):
            sc = jnp.sqrt(c)
            xn = _norm(x)
            mx = x @ m.T
            mxn = _norm(mx)
            res = jnp.tanh(mxn / xn * _artanh(sc * xn)) * mx / (mxn * sc)
            zero_row = jnp.all(mx == 0, axis=-1, keepdims=True)
            return jnp.where(zero_row, jnp.zeros((), dtype=res.dtype), res)

        def mobius_add(x, y, c):
            x2 = jnp.sum(x * x, axis=-1, keepdims=True)
            y2 = jnp.sum(y * y, axis=-1, keepdims=True)
            xy = jnp.sum(x * y, axis=-1, keepdims=True)
            num = (1.0 + 2.0 * c * xy + c * y2) * x + (1.0 - c * x2) * y
            denom = 1.0 + 2.0 * c * xy + c * c * x2 * y2
            return num / jnp.maximum(denom, MIN_NORM)
        key = jax.random.key(seed)
        k1, k2, k3, k4 = jax.random.split(key, 4)
        N, D_IN, D_OUT = (4096, 128, 128)
        x = proj(0.05 * jax.random.normal(k1, (N, D_IN), dtype=jnp.float32), C_IN)
        adj = jax.random.uniform(k2, (N, N), dtype=jnp.float32)
        adj = adj / jnp.sum(adj, axis=1, keepdims=True)
        bound = np.sqrt(2.0) * np.sqrt(6.0 / (D_IN + D_OUT))
        weight = jax.random.uniform(k3, (D_OUT, D_IN), dtype=jnp.float32, minval=-bound, maxval=bound)
        bias = 0.01 * jax.random.normal(k4, (D_OUT,), dtype=jnp.float32)
        return {'x': x, 'adj': adj, 'weight': weight, 'bias': bias}
    _L2_gnn_all = _L2_gnn_setup()
    _L2_gnn_in = {k: v for k, v in _L2_gnn_all.items() if k in ('weight', 'bias')}
    del _L2_gnn_all

    def _L3_gnn_setup():
        import jax, jax.numpy as jnp
        import numpy as np
        N = 4096
        D = 128
        CUTOFF = 1.0
        MU = 1.0
        SIGMA = 0.5

        def sensitivity(r, mu, sigma):
            return jnp.exp(-(1.0 / r - 1.0 / mu) ** 2 / (2.0 * sigma * sigma))
        key = jax.random.key(seed)
        k_z, k_d, k_w = jax.random.split(key, 3)
        z = jax.random.normal(k_z, (N, D), dtype=jnp.float32)
        dist_matrix = jax.random.uniform(k_d, (N, N), dtype=jnp.float32) * 2.0 + 0.05
        W = jax.random.normal(k_w, (D, D), dtype=jnp.float32)
        B = jnp.zeros((D,), dtype=jnp.float32)
        return {'z': z, 'dist_matrix': dist_matrix, 'W': W, 'B': B}
    _L3_gnn_all = _L3_gnn_setup()
    _L3_gnn_in = {k: v for k, v in _L3_gnn_all.items() if k in ('W', 'B')}
    del _L3_gnn_all
    return {'x': x, 'adj': adj, 'L0_gnn_h0': _L0_gnn_in['h0'], 'L0_gnn_y': _L0_gnn_in['y'], 'L1_gnn_gcn_w': _L1_gnn_in['gcn_w'], 'L1_gnn_gcn_b': _L1_gnn_in['gcn_b'], 'L1_gnn_ln_g': _L1_gnn_in['ln_g'], 'L1_gnn_ln_b': _L1_gnn_in['ln_b'], 'L1_gnn_w_in': _L1_gnn_in['w_in'], 'L1_gnn_conv_w': _L1_gnn_in['conv_w'], 'L1_gnn_conv_b': _L1_gnn_in['conv_b'], 'L1_gnn_w_xp': _L1_gnn_in['w_xp'], 'L1_gnn_w_dt': _L1_gnn_in['w_dt'], 'L1_gnn_b_dt': _L1_gnn_in['b_dt'], 'L1_gnn_A_log': _L1_gnn_in['A_log'], 'L1_gnn_D_skip': _L1_gnn_in['D_skip'], 'L1_gnn_w_out': _L1_gnn_in['w_out'], 'L2_gnn_weight': _L2_gnn_in['weight'], 'L2_gnn_bias': _L2_gnn_in['bias'], 'L3_gnn_W': _L3_gnn_in['W'], 'L3_gnn_B': _L3_gnn_in['B']}

def reference(x, adj, L0_gnn_h0, L0_gnn_y, L1_gnn_gcn_w, L1_gnn_gcn_b, L1_gnn_ln_g, L1_gnn_ln_b, L1_gnn_w_in, L1_gnn_conv_w, L1_gnn_conv_b, L1_gnn_w_xp, L1_gnn_w_dt, L1_gnn_b_dt, L1_gnn_A_log, L1_gnn_D_skip, L1_gnn_w_out, L2_gnn_weight, L2_gnn_bias, L3_gnn_W, L3_gnn_B):
    import jax
    import jax.numpy as jnp

    def _L0_gnn_ref(input, A, h0, y):
        import jax, jax.numpy as jnp
        import numpy as np
        N = 5000
        F = 128
        C = 16
        AL = 0.1
        EPS = 1e-12
        adj = A * (y @ y.T)
        row_l1 = jnp.maximum(jnp.sum(jnp.abs(adj), axis=1, keepdims=True), EPS)
        adj = adj / row_l1
        support = adj @ input
        return (1.0 - AL) * support + AL * h0

    def _L1_gnn_ref(x, adj, gcn_w, gcn_b, ln_g, ln_b, w_in, conv_w, conv_b, w_xp, w_dt, b_dt, A_log, D_skip, w_out):
        import jax, jax.numpy as jnp
        import numpy as np
        from jax import lax
        D_MODEL = 128
        D_STATE = 16
        D_CONV = 4
        EXPAND = 2
        D_INNER = EXPAND * D_MODEL
        DT_RANK = (D_MODEL + 15) // 16
        N = 2048
        EPS = 1e-05

        def _mamba(h, w_in, conv_w, conv_b, w_xp, w_dt, b_dt, A_log, D_skip, w_out):
            L = h.shape[0]
            xz = h @ w_in
            xc, z = (xz[:, :D_INNER], xz[:, D_INNER:])
            xpad = jnp.pad(xc, ((D_CONV - 1, 0), (0, 0)))
            xconv = sum((xpad[k:k + L] * conv_w[:, k] for k in range(D_CONV))) + conv_b
            u = jax.nn.silu(xconv)
            dbc = u @ w_xp
            dt = jax.nn.softplus(dbc[:, :DT_RANK] @ w_dt + b_dt)
            B = dbc[:, DT_RANK:DT_RANK + D_STATE]
            C = dbc[:, DT_RANK + D_STATE:]
            A = -jnp.exp(A_log)
            dA = jnp.exp(dt[:, :, None] * A[None])
            dBu = dt[:, :, None] * B[:, None, :] * u[:, :, None]

            def step(hst, inp):
                dAt, dBut, Ct = inp
                hst = dAt * hst + dBut
                return (hst, hst @ Ct)
            _, ys = lax.scan(step, jnp.zeros((D_INNER, D_STATE), h.dtype), (dA, dBu, C))
            y = ys + u * D_skip
            y = y * jax.nn.silu(z)
            return y @ w_out
        h = jax.nn.relu(adj @ x @ gcn_w + gcn_b)
        mu = h.mean(-1, keepdims=True)
        var = h.var(-1, keepdims=True)
        h = (h - mu) * lax.rsqrt(var + EPS) * ln_g + ln_b
        return _mamba(h, w_in, conv_w, conv_b, w_xp, w_dt, b_dt, A_log, D_skip, w_out)

    def _L2_gnn_ref(x, adj, weight, bias):
        import jax, jax.numpy as jnp
        import numpy as np
        MIN_NORM = 1e-15
        BALL_EPS = 1e-05
        C_IN = 1.0
        C_OUT = 1.0

        def _artanh(x):
            x = jnp.clip(x, -1.0 + 1e-07, 1.0 - 1e-07)
            return 0.5 * (jnp.log1p(x) - jnp.log1p(-x))

        def _norm(x):
            return jnp.maximum(jnp.linalg.norm(x, axis=-1, keepdims=True), MIN_NORM)

        def proj(x, c):
            norm = _norm(x)
            maxnorm = (1.0 - BALL_EPS) / jnp.sqrt(c)
            return jnp.where(norm > maxnorm, x / norm * maxnorm, x)

        def expmap0(u, c):
            sc = jnp.sqrt(c)
            un = _norm(u)
            return jnp.tanh(sc * un) * u / (sc * un)

        def logmap0(p, c):
            sc = jnp.sqrt(c)
            pn = _norm(p)
            return _artanh(sc * pn) * p / (sc * pn)

        def mobius_matvec(m, x, c):
            sc = jnp.sqrt(c)
            xn = _norm(x)
            mx = x @ m.T
            mxn = _norm(mx)
            res = jnp.tanh(mxn / xn * _artanh(sc * xn)) * mx / (mxn * sc)
            zero_row = jnp.all(mx == 0, axis=-1, keepdims=True)
            return jnp.where(zero_row, jnp.zeros((), dtype=res.dtype), res)

        def mobius_add(x, y, c):
            x2 = jnp.sum(x * x, axis=-1, keepdims=True)
            y2 = jnp.sum(y * y, axis=-1, keepdims=True)
            xy = jnp.sum(x * y, axis=-1, keepdims=True)
            num = (1.0 + 2.0 * c * xy + c * y2) * x + (1.0 - c * x2) * y
            denom = 1.0 + 2.0 * c * xy + c * c * x2 * y2
            return num / jnp.maximum(denom, MIN_NORM)
        h = proj(mobius_matvec(weight, x, C_IN), C_IN)
        hyp_bias = proj(expmap0(bias[None, :], C_IN), C_IN)
        h = proj(mobius_add(h, hyp_bias, C_IN), C_IN)
        x_tangent = logmap0(h, C_IN)
        support_t = adj @ x_tangent
        h = proj(expmap0(support_t, C_IN), C_IN)
        xt = jax.nn.relu(logmap0(h, C_IN))
        return proj(expmap0(xt, C_OUT), C_OUT)

    def _L3_gnn_ref(z, dist_matrix, W, B):
        import jax, jax.numpy as jnp
        import numpy as np
        N = 4096
        D = 128
        CUTOFF = 1.0
        MU = 1.0
        SIGMA = 0.5

        def sensitivity(r, mu, sigma):
            return jnp.exp(-(1.0 / r - 1.0 / mu) ** 2 / (2.0 * sigma * sigma))
        msg = z @ W + B
        sens = sensitivity(dist_matrix, MU, SIGMA)
        weights = jnp.where(dist_matrix < CUTOFF, sens, 0.0)
        return weights @ msg
    h = jnp.maximum(_layernorm(x, axis=-1), 0.0)
    x = x + _L0_gnn_ref(h, adj, L0_gnn_h0, L0_gnn_y)
    h = jnp.maximum(_layernorm(x, axis=-1), 0.0)
    x = x + _L1_gnn_ref(h, adj, L1_gnn_gcn_w, L1_gnn_gcn_b, L1_gnn_ln_g, L1_gnn_ln_b, L1_gnn_w_in, L1_gnn_conv_w, L1_gnn_conv_b, L1_gnn_w_xp, L1_gnn_w_dt, L1_gnn_b_dt, L1_gnn_A_log, L1_gnn_D_skip, L1_gnn_w_out)
    h = jnp.maximum(_layernorm(x, axis=-1), 0.0)
    x = x + _L2_gnn_ref(h, adj, L2_gnn_weight, L2_gnn_bias)
    h = jnp.maximum(_layernorm(x, axis=-1), 0.0)
    x = x + _L3_gnn_ref(h, adj, L3_gnn_W, L3_gnn_B)
    return x

_drawn_inputs = setup_inputs


def setup_inputs(seed=0):
    import zlib

    import numpy as np

    out = dict(_drawn_inputs(seed))
    spreads = {'L1_gnn_gcn_b': (0.0, 0.1),
     'L1_gnn_ln_g': (1.0, 0.2),
     'L1_gnn_ln_b': (0.0, 0.1),
     'L1_gnn_conv_b': (0.0, 0.1),
     'L1_gnn_D_skip': (1.0, 0.2),
     'L3_gnn_B': (0.0, 0.1)}
    factors = {}
    for name, (base, spread) in spreads.items():
        noise = np.random.default_rng([zlib.crc32(name.encode()), seed]).standard_normal(out[name].shape)
        drawn = base * np.exp(spread * noise) if base else spread * noise
        out[name] = jnp.asarray(drawn.astype(out[name].dtype))
    for name, factor in factors.items():
        out[name] = (out[name] * factor).astype(out[name].dtype)
    return out
```

```python
from contextlib import ExitStack

import concourse.bass as bass
from concourse import mybir

FP32, BF16, FP16 = mybir.dt.float32, mybir.dt.bfloat16, mybir.dt.float16
FP8, U32, I32 = mybir.dt.float8e4, mybir.dt.uint32, mybir.dt.int32
ALU, ACT, AX = mybir.AluOpType, mybir.ActivationFunctionType, mybir.AxisListType

N = 5000
P = 128
D = 128
CLS = 16
T = -(-N // P)
NP = T * P
W = 512
NB = NP // W
BT = W // P
CH = 4
NCH = T // CH
RING = 5
QT = T // 4
HS = 4096.0
HW = 2 * D + 1
HP = 260
INNER = 256
ST = 16
RANK = 8
TAPS = 4
UN = 2 * ST
LN_EPS = 1e-5
L1_FLOOR = 1e-12
TINY = 1e-30
MAXNORM = 1.0 - 1e-5
ATANH_MAX = 6.10303382275888
DATA = ["x", "adj", "L0_gnn_h0", "L0_gnn_y"]


def chain(eng, sem):
    count = [0]

    def link(ins):
        count[0] += 1
        ins.then_inc(sem, 1)
        eng.wait_ge(sem, count[0])

    return link


class Memory:

    def __init__(self, nc, ctx):
        def sb(name, shape, dt):
            return ctx.enter_context(nc.sbuf_tensor(name, shape, dt))

        self.x = sb("x_cur", [P, T, D], FP32)
        self.agg = sb("agg", [P, T, D], FP32)
        self.hh = sb("h_halves", [P, T, HP], FP16)
        self.rows = sb("row_sum", [P, T], FP32)
        self.cnt1 = sb("count_one", [P, T], FP32)
        self.nz = sb("count_nonzero", [P, NB * NCH], FP32)
        self.ybad = sb("y_bad", [CLS, 1], FP32)
        self.ident = sb("ident", [P, P], FP32)
        self.ones = sb("ones", [P, 1], FP32)
        self.flag = sb("flag", [1, 1], I32)
        self.acc = [ctx.enter_context(nc.psum_tensor(f"ps{k}", [P, 2, W], FP32)) for k in range(4)]
        self.adj8 = nc.dram_tensor("adj_compact", (NB, P, T * W // 2), BF16, kind="Internal").ap()
        self.b_rows = nc.dram_tensor("b_rows", (2, ST * W), FP32, kind="Internal").ap()


def setup(nc, m, a):
    with ExitStack() as ctx:
        sem = lambda name: ctx.enter_context(nc.semaphore(name))
        yt = ctx.enter_context(nc.sbuf_tensor("yt_chk", [CLS, NP], FP32))
        junk = ctx.enter_context(nc.sbuf_tensor("y_junk", [CLS, NP], BF16))
        x_in, y_in, zeroed, made, bad = sem("x_in"), sem("y_in"), sem("zeroed"), sem("made"), sem("bad")
        block = ctx.enter_context(nc.Block())

        @block.sync
        def _(sp):
            sp.dma_start(m.x[:, :, :], a["x"].rearrange("p (t d) -> p t d", d=D)).then_inc(x_in, 16)
            sp.dma_start(yt[:, :], a["L0_gnn_y"]).then_inc(y_in, 16)
            sp.wait_ge(x_in, 16)

        @block.gpsimd
        def _(pool):
            pool.memset(m.ident[:, :], 0.0).then_inc(zeroed, 1)
            pool.wait_ge(zeroed, 1)
            pool.affine_select(out=m.ident[:, :], in_=m.ident[:, :], compare_op=ALU.not_equal, fill=1.0,
                               base=0, pattern=[[-1, P]], channel_multiplier=1).then_inc(made, 1)
            pool.wait_ge(made, 1)

        @block.vector
        def _(dve):
            dve.memset(m.ones[:, :], 1.0)
            dve.memset(m.hh[:, :, 2 * D:HP], 1.0)
            dve.wait_ge(y_in, 16)
            dve.scalar_tensor_tensor(out=junk[:, :], in0=yt[:, :], scalar=1.0, in1=yt[:, :],
                                     op0=ALU.is_equal, op1=ALU.not_equal, accum_out=m.ybad[:, :]).then_inc(bad, 1)
            dve.wait_ge(bad, 1)


def rsqrt_newton(dve, link, out, y0, v, tmp, floor_scale):
    link(dve.tensor_tensor(tmp, y0, y0, ALU.mult))
    link(dve.tensor_tensor(tmp, tmp, v, ALU.mult))
    link(dve.tensor_scalar(tmp, tmp, -0.5 * floor_scale, 1.5 * floor_scale, ALU.mult, ALU.add))
    link(dve.tensor_tensor(out, tmp, y0, ALU.mult))


def layernorm_halves(nc, m, tag):
    with ExitStack() as ctx:
        sem = lambda name: ctx.enter_context(nc.semaphore(f"{name}_{tag}"))
        sq = ctx.enter_context(nc.sbuf_tensor(f"sq_{tag}", [P, T, D], FP32))
        small = lambda name: ctx.enter_context(nc.sbuf_tensor(f"{name}_{tag}", [P, T], FP32))
        tot, mean, ssq, var, lnv, y0, tmp, rstd = (small(s) for s in ("tot", "mean", "ssq", "var", "lnv", "y0", "tmp", "rstd"))
        step, centered, squared, var_ready, y0_ready, normed, split = (
            sem(s) for s in ("step", "centered", "squared", "var_ready", "y0_ready", "normed", "split"))
        block = ctx.enter_context(nc.Block())

        @block.vector
        def _(dve):
            link = chain(dve, step)
            link(dve.reduce_sum(tot[:, :], m.x[:, :, :], axis=AX.X))
            link(dve.tensor_scalar(mean[:, :], tot[:, :], 1.0 / D, None, ALU.mult))
            dve.tensor_tensor(m.agg[:, :, :], m.x[:, :, :], mean[:, :].unsqueeze(2).to_broadcast([P, T, D]),
                              ALU.subtract).then_inc(centered, 1)
            dve.wait_ge(squared, 1)
            link(dve.reduce_sum(ssq[:, :], sq[:, :, :], axis=AX.X))
            dve.tensor_scalar(var[:, :], ssq[:, :], 1.0 / D, LN_EPS, ALU.mult, ALU.add).then_inc(var_ready, 1)
            dve.wait_ge(y0_ready, 1)
            rsqrt_newton(dve, link, rstd[:, :], y0[:, :], var[:, :], tmp[:, :], HS)
            dve.tensor_tensor(sq[:, :, :], m.agg[:, :, :], rstd[:, :].unsqueeze(2).to_broadcast([P, T, D]),
                              ALU.mult).then_inc(normed, 1)
            dve.wait_ge(split, 1)
            link(dve.tensor_scalar(m.agg[:, :, :], sq[:, :, :], 0.0, None, ALU.max))
            link(dve.tensor_tensor(m.hh[:, :, D:2 * D], m.agg[:, :, :], m.hh[:, :, 0:D], ALU.subtract))

        @block.scalar
        def _(act):
            act.wait_ge(centered, 1)
            act.activation(sq[:, :, :], m.agg[:, :, :], ACT.Square).then_inc(squared, 1)
            act.wait_ge(var_ready, 1)
            act.activation(lnv[:, :], var[:, :], ACT.Ln).then_inc(squared, 1)
            act.wait_ge(squared, 2)
            act.activation(y0[:, :], lnv[:, :], ACT.Exp, scale=-0.5).then_inc(y0_ready, 1)
            act.wait_ge(normed, 1)
            act.activation(m.hh[:, :, 0:D], sq[:, :, :], ACT.Relu).then_inc(split, 1)


def aggregate_masked(nc, m, a):
    KC = CH * W
    NPAIR = T // 2
    with ExitStack() as ctx:
        sem = lambda name: ctx.enter_context(nc.semaphore(name))
        sb = lambda name, shape, dt: ctx.enter_context(nc.sbuf_tensor(name, shape, dt))
        adj = sb("adj32", [P, RING, KC], FP32)
        bits = sb("bits", [P, RING, KC], FP8)
        masked = sb("masked", [P, 4, 2, W], BF16)
        low = sb("low_part", [P, 2, 2, D], FP32)
        junk = sb("sign_out", [P, 2, KC], BF16)
        yt = sb("yt32", [CLS, NP], FP32)
        y16 = sb("yt16", [CLS, NP], BF16)
        yb = sb("y_block", [CLS, W], BF16)
        adj_in = [sem(f"adj_in{k}") for k in range(RING)]
        bits_out = [sem(f"bits_out{k}") for k in range(RING)]
        y_in, y16_ready, yb_ready = sem("y0_in"), sem("y16_ready"), sem("yb_ready")
        counted, bits_ready, pair_ready, pair_masked = sem("counted"), sem("bits_ready"), sem("pair_ready"), sem("pair_masked")
        masked_used, low_ready, acc_free = sem("masked_used"), sem("low_ready"), sem("acc_free")
        chunks_of = a["adj"]
        block = ctx.enter_context(nc.Block())
        
        @block.sync
        def _(sp):
            sp.dma_start(yt[:, :], a["L0_gnn_y"]).then_inc(y_in, 16)
            with sp.Fori(0, NB) as ib:
                for k in range(NCH):
                    sp.wait_ge(counted, ib * NCH + k + 1)
                    sp.wait_ge(bits_ready, ib * NCH + k + 1)
                    sp.dma_start(adj[:, k % RING, :],
                                 chunks_of[bass.ds(ib, 1), :, k * KC:(k + 1) * KC].rearrange("b p n -> (b p) n")
                                 ).then_inc(adj_in[k % RING], 16)

        @block.scalar
        def _(act):
            act.sem_inc(counted, RING)
            act.wait_ge(y_in, 16)
            act.activation(y16[:, :], yt[:, :], ACT.Copy).then_inc(y16_ready, 1)
            act.wait_ge(y16_ready, 1)
            with act.Fori(0, NB) as ib:
                act.wait_ge(pair_ready, ib * NPAIR + 1)
                act.activation(yb[:, :], y16[:, bass.ds(ib * W, W)], ACT.Copy).then_inc(yb_ready, 1)
                for k in range(NCH):
                    act.wait_ge(adj_in[k % RING], (ib * (NCH // RING) + k // RING + 1) * 16)
                    act.wait_ge(counted, ib * NCH + (RING + k - 1))
                    act.activation(junk[:, k % 2, :], adj[:, k % RING, :].bitcast(U32), ACT.Sign,
                                   accum_out=m.nz[:, bass.ds(ib * NCH + k, 1)]).then_inc(counted, 1)
                    act.wait_ge(bits_ready, ib * NCH + (RING + k + 1))
                    act.dma_start(m.adj8[bass.ds(ib, 1), :, k * KC // 2:(k + 1) * KC // 2].rearrange("b p n -> (b p) n"),
                                  bits[:, k % RING, :].bitcast(BF16)).then_inc(bits_out[k % RING], 16)
                act.wait_ge(masked_used, ib * NPAIR + (NPAIR + 4))
                for b in range(2):
                    act.activation(low[:, b, :, :], m.acc[b][:, :, D:2 * D], ACT.Copy).then_inc(low_ready, 1)

        @block.vector
        def _(dve):
            dve.sem_inc(bits_ready, RING)
            dve.sem_inc(pair_masked, 3)
            dve.sem_inc(acc_free, 1)
            for k in range(RING):
                dve.sem_inc(bits_out[k], 16)
            with dve.Fori(0, NB) as ib:
                for k in range(NCH):
                    r = k % RING
                    dve.wait_ge(adj_in[r], (ib * (NCH // RING) + k // RING + 1) * 16)
                    dve.wait_ge(bits_out[r], (ib * (NCH // RING) + k // RING + 1) * 16)
                    dve.nop(nofuse=True)
                    dve.tensor_scalar(bits[:, r, :], adj[:, r, :], 1.0, None, ALU.is_equal,
                                      saturate=False).then_inc(bits_ready, 1)
                    dve.wait_ge(bits_ready, ib * NCH + (RING + k + 1))
                    for j in range(CH // 2):
                        q = k * (CH // 2) + j
                        dve.wait_ge(pair_ready, ib * NPAIR + (q + 2))
                        dve.wait_ge(masked_used, ib * NPAIR + (q + 1))
                        dve.nop(nofuse=True)
                        dve.tensor_tensor(masked[:, q % 4, :, :],
                                          bits[:, r, j * 2 * W:(j + 1) * 2 * W].rearrange("p (s n) -> p s n", s=2),
                                          m.acc[2 + q % 2][:, :, :], ALU.mult).then_inc(pair_masked, 1)
                dve.wait_ge(masked_used, ib * NPAIR + (NPAIR + 4))
                for b in range(2):
                    dve.wait_ge(low_ready, ib * 2 + (b + 1))
                    dve.tensor_tensor(m.agg[:, bass.ds(ib * BT + 2 * b, 2), :], m.acc[b][:, :, 0:D],
                                      low[:, b, :, :], ALU.add)
                    last = dve.tensor_copy(m.rows[:, bass.ds(ib * BT + 2 * b, 2)], m.acc[b][:, :, 2 * D])
                last.then_inc(acc_free, 1)

        @block.tensor
        def _(pe):
            pe.sem_inc(masked_used, 4)
            pe.sem_inc(pair_ready, 1)

            def labels(ib, q):
                pe.wait_ge(pair_masked, ib * NPAIR + (q + 2))
                for s in range(2):
                    mm = pe.matmul(m.acc[2 + q % 2][:, s, :], y16[:, (2 * q + s) * P:(2 * q + s + 1) * P], yb[:, :],
                                   start=True, stop=True)
                mm.then_inc(pair_ready, 1)

            def gather(ib, q):
                pe.wait_ge(pair_masked, ib * NPAIR + (q + 4))
                if q == 0:
                    pe.wait_ge(acc_free, ib + 1)
                for s in range(2):
                    for it in range(BT):
                        mm = pe.matmul(m.acc[it // 2][:, it % 2, 0:HW], masked[:, q % 4, s, it * P:(it + 1) * P],
                                       m.hh[:, 2 * q + s, 0:HW], start=(q + s == 0), stop=(q == NPAIR - 1 and s == 1))
                mm.then_inc(masked_used, 1)
                return mm

            with pe.Fori(0, NB) as ib:
                pe.wait_ge(yb_ready, ib + 1)
                for q in range(NPAIR):
                    labels(ib, q)
                    if q:
                        gather(ib, q - 1)
                gather(ib, NPAIR - 1)

        @block.gpsimd
        def _(pool):
            for k in range(RING):
                pool.wait_ge(bits_out[k], 16 * (NB * NCH // RING + 1))


def aggregate_compact(nc, m, counting, tag):
    width = HW if counting else 2 * D
    KQ = QT * W
    with ExitStack() as ctx:
        sem = lambda name: ctx.enter_context(nc.semaphore(f"{name}_{tag}"))
        bits = ctx.enter_context(nc.sbuf_tensor(f"bits_{tag}", [P, 4, KQ], FP8))
        low = ctx.enter_context(nc.sbuf_tensor(f"low_{tag}", [P, 4, 2, D], FP32))
        bits_in = [sem(f"bits_in{k}") for k in range(4)]
        bits_used, acc_full, low_ready, acc_free = sem("bits_used"), sem("acc_full"), sem("low_ready"), sem("acc_free")
        block = ctx.enter_context(nc.Block())

        @block.sync
        def _(sp):
            with sp.Fori(0, NB) as ib:
                for k in range(4):
                    sp.wait_ge(bits_used, ib * 4 + (k + 1))
                    sp.dma_start(bits[:, k, :].bitcast(BF16),
                                 m.adj8[bass.ds(ib, 1), :, k * KQ // 2:(k + 1) * KQ // 2].rearrange("b p n -> (b p) n")
                                 ).then_inc(bits_in[k], 16)

        @block.tensor
        def _(pe):
            pe.sem_inc(bits_used, 4)
            with pe.Fori(0, NB // 2) as pair:
                for par in range(2):
                    ib = pair * 2 + par
                    pe.wait_ge(acc_free, ib + 1)
                    for k in range(4):
                        pe.wait_ge(bits_in[k], ib * 16 + 16)
                        pe.nop(nofuse=True)
                        for j in range(QT):
                            for it in range(BT):
                                mm = pe.matmul(m.acc[2 * par + it // 2][:, it % 2, 0:width],
                                               bits[:, k, j * W + it * P:j * W + (it + 1) * P],
                                               m.hh[:, k * QT + j, 0:width],
                                               start=(k + j == 0), stop=(k == 3 and j == QT - 1))
                        mm.then_inc(bits_used, 1)

        @block.scalar
        def _(act):
            with act.Fori(0, NB // 2) as pair:
                for par in range(2):
                    ib = pair * 2 + par
                    act.wait_ge(bits_used, ib * 4 + 8)
                    act.wait_ge(acc_free, ib + 1)
                    for b in range(2):
                        act.activation(low[:, 2 * par + b, :, :], m.acc[2 * par + b][:, :, D:2 * D], ACT.Copy).then_inc(low_ready, 1)

        @block.vector
        def _(dve):
            dve.sem_inc(acc_free, 2)
            with dve.Fori(0, NB // 2) as pair:
                for par in range(2):
                    ib = pair * 2 + par
                    for b in range(2):
                        dve.wait_ge(low_ready, ib * 2 + (b + 1))
                        last = dve.tensor_tensor(m.agg[:, bass.ds(ib * BT + 2 * b, 2), :],
                                                 m.acc[2 * par + b][:, :, 0:D], low[:, 2 * par + b, :, :], ALU.add)
                        if counting:
                            last = dve.tensor_copy(m.cnt1[:, bass.ds(ib * BT + 2 * b, 2)],
                                                   m.acc[2 * par + b][:, :, 2 * D])
                    last.then_inc(acc_free, 1)


def after_l0(nc, m, a, tag):
    with ExitStack() as ctx:
        sem = lambda name: ctx.enter_context(nc.semaphore(name))
        h0 = ctx.enter_context(nc.sbuf_tensor(f"h0_{tag}", [P, T, D], FP32))
        r = ctx.enter_context(nc.sbuf_tensor(f"l0_r_{tag}", [P, T], FP32))
        h0_in, step = sem("h0_in"), sem("l0_step")
        block = ctx.enter_context(nc.Block())

        @block.sync
        def _(sp):
            sp.dma_start(h0[:, :, :], a["L0_gnn_h0"].rearrange("p (t d) -> p t d", d=D)).then_inc(h0_in, 16)

        @block.vector
        def _(dve):
            link = chain(dve, step)
            link(dve.tensor_scalar(r[:, :], m.rows[:, :], L1_FLOOR, None, ALU.max))
            link(dve.reciprocal(r[:, :], r[:, :]))
            link(dve.tensor_scalar(r[:, :], r[:, :], 0.9 / HS, None, ALU.mult))
            link(dve.tensor_tensor(m.agg[:, :, :], m.agg[:, :, :], r[:, :].unsqueeze(2).to_broadcast([P, T, D]), ALU.mult))
            link(dve.tensor_tensor(m.x[:, :, :], m.x[:, :, :], m.agg[:, :, :], ALU.add))
            dve.wait_ge(h0_in, 16)
            link(dve.scalar_tensor_tensor(out=m.x[:, :, :], in0=h0[:, :, :], scalar=0.1, in1=m.x[:, :, :],
                                          op0=ALU.mult, op1=ALU.add))


def mamba(nc, m, a, agg_scale, tag):
    with ExitStack() as ctx:
        def sem(name):
            return ctx.enter_context(nc.semaphore(f"{name}_{tag}"))

        def sb(name, shape, dt=FP32):
            return ctx.enter_context(nc.sbuf_tensor(f"{name}_{tag}", shape, dt))

        gcn_w, gcn_b = sb("gcn_w", [P, D]), sb("gcn_b", [P, D])
        ln_g, ln_b = sb("ln_g", [P, 1]), sb("ln_b", [P, 1])
        w_in = sb("w_in", [P, 2 * INNER])
        conv_w, conv_b = sb("conv_w", [P, 2 * TAPS]), sb("conv_b", [P, 2])
        w_cb, w_r, w_dt, b_dt = sb("w_cb", [P, 2 * 96]), sb("w_r", [P, 2 * RANK]), sb("w_dt", [RANK, INNER]), sb("b_dt", [P, 2])
        decay, skip, w_out = sb("decay", [P, UN]), sb("skip", [P, 2]), sb("w_out", [P, 2 * D])
        pick = sb("pick", [96, ST * P], BF16)

        s_blk, s_t, g_act, h_t = sb("s_blk", [P, BT, D]), sb("s_t", [P, W]), sb("g_act", [P, BT, D]), sb("h_t", [P, W])
        stats, mv = sb("stats", [P, BT, 6]), sb("mv", [P, BT, 2])
        var, lnv, y0, tmp, rstd, shift = (sb(s, [P, BT]) for s in ("var", "lnv", "y0", "tmp", "rstd", "shift"))
        xc, cv = sb("xc", [P, 2, W + TAPS]), sb("cv", [P, 2, W])
        zs, us, dts, dtu = (sb(s, [P, 2, 2, W]) for s in ("zs", "us", "dts", "dtu"))
        c_parts, c_rest = sb("c_parts", [96, 2, W], BF16), sb("c_rest", [96, W])
        b_row, dtr, soft, lin = sb("b_row", [2 * ST, W]), sb("dtr", [RANK, W]), sb("soft", [P, 2, W]), sb("lin", [P, 2, W])
        bbc = sb("bbc", [P, 2, 4, W])
        bx, hs, ps, yd, yg = sb("bx", [P, 4, W]), sb("hs", [P, 4, W]), sb("ps", [P, 4, W]), sb("yd", [P, W]), sb("yg", [P, 2, W])
        state = sb("state", [P, UN])

        a_bank, c_bank, y_bank, misc = m.acc[0], m.acc[1], m.acc[2][:, 0, :], m.acc[2][:, 1, :]

        consts_in, pick0, pick1, decay_ready, zeroed = sem("consts_in"), sem("pick0"), sem("pick1"), sem("decay_ready"), sem("zeroed")
        a_ready, bx_ready, c_ready, scan_done = sem("a_ready"), sem("bx_ready"), sem("c_ready"), sem("scan_done")
        p_ready, p_used, state_saved, y_read, gated = sem("p_ready"), sem("p_used"), sem("state_saved"), sem("y_read"), sem("gated")
        misc_full, misc_free = sem("misc_full"), sem("misc_free")
        s_ready, var_ready, y0_ready, ln_step, hn_ready = sem("s_ready"), sem("var_ready"), sem("y0_ready"), sem("ln_step"), sem("hn_ready")
        halo, conv_step, u_ready, b_ready, c_step, c_sub = sem("halo"), sem("conv_step"), sem("u_ready"), sem("b_ready"), sem("c_step"), sem("c_sub")
        soft_step, dt_ready, x_added = sem("soft_step"), sem("dt_ready"), sem("x_added")
        b_out, bbc_in = sem("b_out"), [sem(f"bbc_in{k}") for k in range(2)]
        block = ctx.enter_context(nc.Block())

        def front_use(f, j):
            return j + 1 if isinstance(f, int) and f == 0 else 12 * f + j

        def back_use(c):
            return 12 * NB + 1 if isinstance(c, int) and c == NB - 1 else 12 * c + 24

        def chunks(eng, body):
            body(0, 0, True, False)
            with eng.Fori(0, (NB - 2) // 2) as two:
                body(two * 2 + 1, 1, True, True)
                body(two * 2 + 2, 0, True, True)
            body(NB - 1, 1, False, True)

        WEIGHTS = [(gcn_w, "L1_gnn_gcn_w"), (gcn_b, "L1_gnn_gcn_b"), (ln_g, "L1_gnn_ln_g"), (ln_b, "L1_gnn_ln_b"),
                   (w_in, "L1_gnn_w_in"), (conv_w, "L1_gnn_conv_w"), (conv_b, "L1_gnn_conv_b"), (w_cb, "w_cb"),
                   (w_r, "w_r"), (w_dt, "L1_gnn_w_dt"), (b_dt, "L1_gnn_b_dt"), (decay, "L1_gnn_A_log"),
                   (skip, "L1_gnn_D_skip"), (w_out, "L1_gnn_w_out")]
        ALL_IN = 16 * len(WEIGHTS)

        @block.sync
        def _(sp):
            for tile, name in WEIGHTS:
                sp.dma_start(tile[:, :], a[name]).then_inc(consts_in, 16)

            def b_store(f, q):
                sp.wait_ge(b_ready, f + 1)
                sp.dma_start(m.b_rows[q:q + 1, :].rearrange("a (s w) -> (a s) w", w=W),
                             b_row[ST:2 * ST, :]).then_inc(b_out, 16)
                sp.wait_ge(b_out, f * 16 + 16)
                sp.nop(nofuse=True)

            def body(c, q, front, back):
                for g in range(8):
                    sp.wait_ge(bx_ready, c * UN + (4 * g + 4))
                    sp.dma_start(bbc[:, g % 2, :, :],
                                 m.b_rows[q, (g % 4) * 4 * W:(g % 4 + 1) * 4 * W].rearrange("(s w) -> s w", w=W)
                                 .partition_broadcast(P)).then_inc(bbc_in[g % 2], 16)
                if front:
                    b_store(c + 1, 1 - q)

            b_store(0, 0)
            chunks(sp, body)

        @block.gpsimd
        def _(pool):
            pool.sem_inc(bx_ready, 8)
            pool.memset(pick[:, :], 0.0).then_inc(pick0, 1)
            rows = pick[:, :].rearrange("k (n p) -> k n p", p=P)
            for part in range(3):
                pool.wait_ge(pick0, part + 1)
                pool.affine_select(out=rows, in_=rows, compare_op=ALU.not_equal, fill=1.0, base=-32 * part,
                                   pattern=[[-1, ST], [0, P]], channel_multiplier=1).then_inc(pick0, 1)
            pool.memset(state[:, :], 0.0).then_inc(zeroed, 1)
            pool.memset(xc[:, :, 0:TAPS - 1], 0.0).then_inc(zeroed, 1)

            def dt_half(f, q, h):
                pool.wait_ge(soft_step, 6 * f + (3 * h + 3))
                pool.tensor_tensor(dts[:, q, h, :], soft[:, h, :], lin[:, h, :], ALU.add).then_inc(dt_ready, 1)
                pool.wait_ge(dt_ready, 4 * f + (2 * h + 1))
                pool.tensor_tensor(dtu[:, q, h, :], dts[:, q, h, :], us[:, q, h, :], ALU.mult).then_inc(dt_ready, 1)

            def body(c, q, front, back):
                for u in range(UN):
                    if u % 4 == 0:
                        pool.wait_ge(bbc_in[u // 4 % 2], (c * 4 + (u // 8 + 1)) * 16)
                    if u == 0:
                        pool.wait_ge(dt_ready, 4 * c + 4)
                    pool.wait_ge(scan_done, c * UN + (u + 1))
                    pool.tensor_tensor(bx[:, u % 4, :], dtu[:, q, u // ST, :], bbc[:, u // 4 % 2, u % 4, :],
                                       ALU.mult).then_inc(bx_ready, 1)
                    if front and u in (26, 28):
                        if u == 26:
                            pool.wait_ge(scan_done, c * UN + 4)
                        dt_half(c + 1, 1 - q, (u - 26) // 2)

            dt_half(0, 0, 0)
            dt_half(0, 0, 1)
            chunks(pool, body)

        @block.scalar
        def _(act):
            act.wait_ge(consts_in, ALL_IN)
            act.activation(decay[:, :], decay[:, :], ACT.Exp).then_inc(decay_ready, 1)
            act.wait_ge(decay_ready, 1)
            act.activation(decay[:, :], decay[:, :], ACT.Copy, scale=-1.0).then_inc(decay_ready, 1)
            act.wait_ge(decay_ready, 2)

            def take_agg(f):
                act.activation(s_blk[:, :, :], m.agg[:, f * BT:(f + 1) * BT, :] if isinstance(f, int)
                               else m.agg[:, bass.ds(f * BT, BT), :], ACT.Copy, scale=agg_scale).then_inc(s_ready, 1)

            def take_s_t(f):
                act.wait_ge(misc_full, front_use(f, 1))
                act.activation(s_t[:, :], misc, ACT.Copy).then_inc(misc_free, 1)

            def var_root(f):
                act.wait_ge(var_ready, f + 1)
                act.activation(lnv[:, :], var[:, :], ACT.Ln).then_inc(y0_ready, 1)
                act.wait_ge(y0_ready, 2 * f + 1)
                act.activation(y0[:, :], lnv[:, :], ACT.Exp, scale=-0.5).then_inc(y0_ready, 1)

            def take_h_t(f):
                act.wait_ge(misc_full, front_use(f, 3))
                act.activation(h_t[:, :], misc, ACT.Identity, scale=ln_g[:, :], bias=ln_b[:, :]).then_inc(misc_free, 1)
                if isinstance(f, int) and f == 0:
                    act.wait_ge(zeroed, 2)
                    act.sem_inc(halo, 1)
                else:
                    act.wait_ge(conv_step, 8 * f)
                    act.activation(xc[:, :, 0:TAPS - 1], xc[:, :, W:W + TAPS - 1], ACT.Copy).then_inc(halo, 1)

            def take_xc(f, h):
                act.wait_ge(misc_full, front_use(f, 4 + h))
                act.wait_ge(halo, f + 1)
                act.activation(xc[:, h, TAPS - 1:W + TAPS - 1], misc, ACT.Copy).then_inc(misc_free, 1)

            def silus(f, q):
                if not (isinstance(f, int) and f < 2):
                    act.wait_ge(gated, 2 * f - 2)
                for h in range(2):
                    act.wait_ge(misc_full, front_use(f, 6 + h))
                    act.activation(zs[:, q, h, :], misc, ACT.Silu).then_inc(misc_free, 1)
                for h in range(2):
                    act.wait_ge(conv_step, 8 * f + (4 * h + 4))
                    act.activation(us[:, q, h, :], cv[:, h, :], ACT.Silu).then_inc(u_ready, 1)

            def take_bc(f, q):
                act.wait_ge(misc_full, front_use(f, 8))
                if not (isinstance(f, int) and f == 0):
                    act.wait_ge(b_out, f * 16)
                act.activation(b_row[:, :], misc[0:2 * ST, :], ACT.Copy).then_inc(b_ready, 1)
                act.activation(c_parts[:, q, :], misc[0:96, :], ACT.Copy).then_inc(c_step, 1)

            def second_c(f, q):
                act.wait_ge(misc_free, front_use(f, 8))
                act.activation(c_parts[32:64, q, :], c_rest[32:64, :], ACT.Copy)
                act.activation(c_parts[64:96, q, :], c_rest[64:96, :], ACT.Copy).then_inc(c_step, 1)

            def third_c(f, q):
                act.wait_ge(c_sub, f + 1)
                act.activation(c_parts[64:96, q, :], c_rest[64:96, :], ACT.Copy).then_inc(c_step, 1)

            def take_dtr(f):
                act.wait_ge(misc_full, front_use(f, 9))
                act.activation(dtr[:, :], misc[0:RANK, :], ACT.Copy).then_inc(misc_free, 1)

            def softplus(f, h):
                act.wait_ge(misc_full, front_use(f, 10 + h))
                if not (isinstance(f, int) and f == 0):
                    act.wait_ge(dt_ready, 4 * f)
                act.activation(soft[:, h, :], misc, ACT.Abs, bias=b_dt[:, h:h + 1]).then_inc(soft_step, 1)
                act.activation(lin[:, h, :], misc, ACT.Relu, bias=b_dt[:, h:h + 1]).then_inc(misc_free, 1)
                act.wait_ge(soft_step, 6 * f + (3 * h + 1))
                act.activation(soft[:, h, :], soft[:, h, :], ACT.Exp, scale=-1.0).then_inc(soft_step, 1)
                act.wait_ge(soft_step, 6 * f + (3 * h + 2))
                act.activation(soft[:, h, :], soft[:, h, :], ACT.Ln, bias=1.0).then_inc(soft_step, 1)

            def save_state(c, u):
                act.wait_ge(scan_done, c * UN + (u + 5))
                act.activation(state[:, u:u + 1], hs[:, u % 4, W - 1:W], ACT.Copy).then_inc(state_saved, 1)

            def front_step(f, q, u):
                if u == 1:
                    take_agg(f)
                if u == 4:
                    take_s_t(f)
                if u == 7:
                    var_root(f)
                if u == 10:
                    take_h_t(f)
                if u in (12, 14):
                    take_xc(f, (u - 12) // 2)
                if u == 17:
                    silus(f, q)
                if u == 20:
                    take_bc(f, q)
                if u == 22:
                    take_dtr(f)
                    second_c(f, q)
                if u == 24:
                    third_c(f, q)
                    softplus(f, 0)
                if u == 26:
                    softplus(f, 1)

            def body(c, q, front, back):
                for u in range(UN):
                    if u == 0:
                        act.wait_ge(dt_ready, 4 * c + 4)
                    act.wait_ge(scan_done, c * UN + (u + 3))
                    act.activation(a_bank[:, u % 2, :], dts[:, q, u // ST, :], ACT.Exp,
                                   scale=decay[:, u:u + 1]).then_inc(a_ready, 1)
                    if u:
                        save_state(c, u - 1)
                    if front:
                        front_step(c + 1, 1 - q, u)
                save_state(c, UN - 1)

            for u in range(UN):
                front_step(0, 0, u)
            chunks(act, body)

        @block.vector
        def _(dve):
            dve.sem_inc(scan_done, 4)
            dve.sem_inc(state_saved, UN)
            dve.sem_inc(p_ready, 4)
            dve.sem_inc(y_read, 1)
            dve.sem_inc(misc_free, 1)
            dve.wait_ge(consts_in, ALL_IN)
            dve.wait_ge(zeroed, 2)

            def scan(c, u):
                dve.wait_ge(a_ready, c * UN + (u + 1))
                dve.wait_ge(bx_ready, c * UN + (u + 9))
                dve.wait_ge(p_ready, c * UN + (u + 1))
                dve.wait_ge(state_saved, c * UN + (u + 29))
                dve.tensor_tensor_scan(hs[:, u % 4, :], a_bank[:, u % 2, :], bx[:, u % 4, :], state[:, u:u + 1],
                                       ALU.mult, ALU.add).then_inc(scan_done, 1)

            def times_c(c, u):
                dve.wait_ge(c_ready, c * UN + (u + 1))
                dve.wait_ge(p_used, c * UN + (u + 1))
                dve.wait_ge(scan_done, c * UN + (u + 5))
                dve.tensor_tensor(ps[:, u % 4, :], hs[:, u % 4, :], c_bank[:, u % 2, :], ALU.mult).then_inc(p_ready, 1)

            def gate(c, q, h):
                dve.wait_ge(p_used, c * UN + (ST * (h + 1) + 4))
                if not (isinstance(c, int) and c == 0):
                    dve.wait_ge(gated, 2 * c + h)
                    dve.wait_ge(misc_full, 12 * c + 12)
                elif h:
                    dve.wait_ge(gated, 1)
                dve.scalar_tensor_tensor(out=yd[:, :], in0=us[:, q, h, :], scalar=skip[:, h:h + 1], in1=y_bank,
                                         op0=ALU.mult, op1=ALU.add).then_inc(y_read, 1)
                dve.wait_ge(y_read, 2 * c + (h + 2))
                dve.tensor_tensor(yg[:, h, :], yd[:, :], zs[:, q, h, :], ALU.mult).then_inc(gated, 1)

            def add_out(c):
                dve.wait_ge(misc_full, back_use(c))
                at = m.x[:, c * BT:(c + 1) * BT, :] if isinstance(c, int) else m.x[:, bass.ds(c * BT, BT), :]
                dve.tensor_tensor(at, at, misc.rearrange("p (t d) -> p t d", d=D), ALU.add).then_inc(misc_free, 1)

            def gcn_stats(f):
                n = 14 * f
                dve.wait_ge(misc_full, front_use(f, 2))
                if not (isinstance(f, int) and f == 0):
                    dve.wait_ge(hn_ready, f)
                dve.tensor_tensor(g_act[:, :, :], misc.rearrange("p (t d) -> p t d", d=D),
                                  gcn_b[:, :].unsqueeze(1).to_broadcast([P, BT, D]), ALU.add).then_inc(misc_free, 1)
                dve.wait_ge(misc_free, front_use(f, 2))
                dve.tensor_scalar(g_act[:, :, :], g_act[:, :, :], 0.0, None, ALU.max).then_inc(ln_step, 1)
                dve.wait_ge(ln_step, n + 1)
                for t in range(BT):
                    dve.bn_stats(stats[:, t, :], g_act[:, t, :]).then_inc(ln_step, 1)
                dve.wait_ge(ln_step, n + 5)
                dve.nop(nofuse=True)
                for t in range(BT):
                    dve.bn_aggr(mv[:, t, :], stats[:, t, :]).then_inc(ln_step, 1)
                dve.wait_ge(ln_step, n + 9)
                dve.tensor_scalar(var[:, :], mv[:, :, 1], LN_EPS, None, ALU.add).then_inc(var_ready, 1)

            def normalize(f):
                n = 14 * f + 9
                dve.wait_ge(y0_ready, 2 * f + 2)
                dve.tensor_tensor(tmp[:, :], y0[:, :], y0[:, :], ALU.mult).then_inc(ln_step, 1)
                dve.wait_ge(ln_step, n + 1)
                dve.tensor_tensor(tmp[:, :], tmp[:, :], var[:, :], ALU.mult).then_inc(ln_step, 1)
                dve.wait_ge(ln_step, n + 2)
                dve.tensor_scalar(tmp[:, :], tmp[:, :], -0.5, 1.5, ALU.mult, ALU.add).then_inc(ln_step, 1)
                dve.wait_ge(ln_step, n + 3)
                dve.tensor_tensor(rstd[:, :], tmp[:, :], y0[:, :], ALU.mult).then_inc(ln_step, 1)
                dve.wait_ge(ln_step, n + 4)
                dve.scalar_tensor_tensor(out=shift[:, :], in0=mv[:, :, 0], scalar=-1.0, in1=rstd[:, :],
                                         op0=ALU.mult, op1=ALU.mult).then_inc(ln_step, 1)
                dve.wait_ge(ln_step, n + 5)
                for t in range(BT):
                    last = dve.tensor_scalar(g_act[:, t, :], g_act[:, t, :], rstd[:, t:t + 1], shift[:, t:t + 1],
                                             ALU.mult, ALU.add)
                last.then_inc(hn_ready, 1)

            def convolve(f, h, part):
                n = 8 * f + 4 * h
                if part == 0:
                    dve.wait_ge(misc_free, front_use(f, 4 + h))
                    if not (isinstance(f, int) and f == 0):
                        dve.wait_ge(u_ready, 2 * f)
                    dve.tensor_scalar(cv[:, h, :], xc[:, h, 0:W], conv_w[:, TAPS * h:TAPS * h + 1], conv_b[:, h:h + 1],
                                      ALU.mult, ALU.add).then_inc(conv_step, 1)
                for k in ((1,), (2, 3))[part]:
                    dve.wait_ge(conv_step, n + k)
                    dve.scalar_tensor_tensor(out=cv[:, h, :], in0=xc[:, h, k:k + W],
                                             scalar=conv_w[:, TAPS * h + k:TAPS * h + k + 1], in1=cv[:, h, :],
                                             op0=ALU.mult, op1=ALU.add).then_inc(conv_step, 1)

            def c_minus_first(f, q):
                dve.wait_ge(c_step, 3 * f + 1)
                dve.tensor_tensor(c_rest[32:64, :], misc[32:64, :], c_parts[32:64, q, :], ALU.subtract)
                dve.tensor_tensor(c_rest[64:96, :], misc[64:96, :], c_parts[64:96, q, :], ALU.subtract).then_inc(misc_free, 1)

            def c_minus_second(f, q):
                dve.wait_ge(c_step, 3 * f + 2)
                dve.tensor_tensor(c_rest[64:96, :], c_rest[64:96, :], c_parts[64:96, q, :], ALU.subtract).then_inc(c_sub, 1)

            def front_step(f, q, u):
                if u == 6:
                    gcn_stats(f)
                if u == 8:
                    normalize(f)
                if u in (13, 14, 15, 16):
                    convolve(f, (u - 13) // 2, (u - 13) % 2)
                if u == 21:
                    c_minus_first(f, q)
                if u == 23:
                    c_minus_second(f, q)

            def body(c, q, front, back):
                for u in range(UN):
                    scan(c, u)
                    times_c(c, u)
                    if back and u == 0:
                        gate(c - 1, 1 - q, 1)
                    if back and u == 3:
                        add_out(c - 1)
                    if u == ST:
                        gate(c, q, 0)
                    if front:
                        front_step(c + 1, 1 - q, u)

            for u in range(UN):
                front_step(0, 0, u)
            chunks(dve, body)
            gate(NB - 1, 1, 1)
            add_out(NB - 1)

        @block.tensor
        def _(pe):
            pe.sem_inc(misc_full, 1)
            pe.sem_inc(p_used, 4)
            pe.wait_ge(consts_in, ALL_IN)
            pe.wait_ge(pick0, 4)

            def take_misc(use):
                pe.wait_ge(misc_free, use - 1)

            def transposes(f, use, src):
                take_misc(use)
                for t in range(BT):
                    mm = pe.transpose(misc[:, t * P:(t + 1) * P], src[:, t, :], m.ident[:, :])
                mm.then_inc(misc_full, 1)

            def front_step(f, q, u):
                if u == 3:
                    pe.wait_ge(s_ready, f + 1)
                    transposes(f, front_use(f, 1), s_blk)
                if u == 5:
                    take_misc(front_use(f, 2))
                    for t in range(BT):
                        mm = pe.matmul(misc[:, t * P:(t + 1) * P], s_t[:, t * P:(t + 1) * P], gcn_w[:, :], start=True, stop=True)
                    mm.then_inc(misc_full, 1)
                if u == 9:
                    pe.wait_ge(hn_ready, f + 1)
                    transposes(f, front_use(f, 3), g_act)
                if u in (11, 13, 15, 16):
                    j = {11: 0, 13: 1, 15: 2, 16: 3}[u]
                    take_misc(front_use(f, 4 + j))
                    pe.matmul(misc, w_in[:, j * P:(j + 1) * P], h_t[:, :], start=True, stop=True).then_inc(misc_full, 1)
                if u in (19, 21):
                    j, w, k = (8, w_cb, 96) if u == 19 else (9, w_r, RANK)
                    take_misc(front_use(f, j))
                    pe.wait_ge(u_ready, 2 * f + 2)
                    for h in range(2):
                        mm = pe.matmul(misc[0:k, :], w[:, h * k:(h + 1) * k], us[:, q, h, :], start=(h == 0), stop=(h == 1))
                    mm.then_inc(misc_full, 1)
                if u in (23, 25):
                    h = (u - 23) // 2
                    take_misc(front_use(f, 10 + h))
                    pe.matmul(misc, w_dt[:, h * P:(h + 1) * P], dtr[:, :], start=True, stop=True).then_inc(misc_full, 1)

            def spread_c(c, q, u):
                if u == 0:
                    pe.wait_ge(c_step, 3 * c + 3)
                pe.wait_ge(p_ready, c * UN + (u + 3))
                n = u % ST
                pe.matmul(c_bank[:, u % 2, :], pick[:, n * P:(n + 1) * P], c_parts[:, q, :], start=True, stop=True).then_inc(c_ready, 1)

            def add_state(c, u):
                n = u % ST
                pe.wait_ge(p_ready, c * UN + (u + 5))
                if n == 0:
                    pe.wait_ge(y_read, 2 * c + (u // ST + 1))
                pe.matmul(y_bank, m.ident[:, :], ps[:, u % 4, :], start=(n == 0), stop=(n == ST - 1)).then_inc(p_used, 1)

            def output(c):
                take_misc(back_use(c))
                pe.wait_ge(gated, 2 * c + 2)
                for t in range(BT):
                    for h in range(2):
                        mm = pe.matmul(misc[:, t * P:(t + 1) * P], yg[:, h, t * P:(t + 1) * P], w_out[:, h * D:(h + 1) * D],
                                       start=(h == 0), stop=(h == 1))
                mm.then_inc(misc_full, 1)

            def body(c, q, front, back):
                for u in range(UN):
                    spread_c(c, q, u)
                    if u:
                        add_state(c, u - 1)
                    if back and u == 2:
                        output(c - 1)
                    if front:
                        front_step(c + 1, 1 - q, u)
                add_state(c, UN - 1)

            for u in range(UN):
                front_step(0, 0, u)
            chunks(pe, body)
            output(NB - 1)


ROOT_SCALE = 2.0 ** 36


def hyperbolic_in(nc, m, a, tag):
    with ExitStack() as ctx:
        sem = lambda name: ctx.enter_context(nc.semaphore(f"{name}_{tag}"))
        sb = lambda name, shape: ctx.enter_context(nc.sbuf_tensor(f"{name}_{tag}", shape, FP32))
        names = ("xn2", "mn2", "dot", "hn2", "lnv", "y0", "tmp", "rs_x", "n_x", "rs_m", "n_m", "at_x", "at_h", "rs_h",
                 "n_h", "lp", "lm", "sq", "poly", "mask", "arg", "th", "alpha", "x2", "xy", "num_a", "num_b", "den", "c1", "c2", "coef")
        s = {n: sb(f"l2_{n}", [P, T]) for n in names}
        big = sb("l2_big", [P, T, D])
        w_t, bias = sb("l2_w", [P, D]), sb("l2_bias", [P, D])
        b_sq = sb("l2_bsq", [P, D])
        b1 = {n: sb(f"l2b_{n}", [P, 1]) for n in ("n2", "lnv", "y0", "tmp", "rs", "n", "th", "beta", "y2")}
        blk, blk_t = sb("l2_blk", [P, 2, BT * D]), sb("l2_blk_t", [P, 2, W])
        w_in_, step, for_act, for_dve = sem("l2_w_in"), sem("l2_step"), sem("l2_for_act"), sem("l2_for_dve")
        blk_ready, t_full, t_free, mx_full, mx_free = sem("blk_ready"), sem("t_full"), sem("t_free"), sem("mx_full"), sem("mx_free")
        block = ctx.enter_context(nc.Block())
        S = lambda n: s[n][:, :]
        B = lambda n: b1[n][:, :]
        wide = lambda ap: ap.unsqueeze(2).to_broadcast([P, T, D])
        bias_w = bias[:, :].unsqueeze(1).to_broadcast([P, T, D])

        @block.sync
        def _(sp):
            sp.dma_start(w_t[:, :], a["L2_gnn_weight"]).then_inc(w_in_, 16)
            sp.dma_start(bias[:, :], a["L2_gnn_bias"]).then_inc(w_in_, 16)

        @block.tensor
        def _(pe):
            pe.wait_ge(w_in_, 32)
            for ib in range(NB):
                r = ib % 2
                pe.wait_ge(blk_ready, ib + 1)
                for t in range(BT):
                    mm = pe.transpose(m.acc[0][:, r, t * P:(t + 1) * P], blk[:, r, t * D:(t + 1) * D], m.ident[:, :])
                mm.then_inc(t_full, 1)
                pe.wait_ge(t_free, ib + 1)
                if ib >= 2:
                    pe.wait_ge(mx_free, ib - 1)
                for t in range(BT):
                    mm = pe.matmul(m.acc[1][:, r, t * P:(t + 1) * P], blk_t[:, r, t * P:(t + 1) * P], w_t[:, :], start=True, stop=True)
                mm.then_inc(mx_full, 1)

        @block.scalar
        def _(act):
            act.activation(big[:, :, :], m.agg[:, :, :], ACT.Square, scale=1.0 / HS).then_inc(for_dve, 1)
            for ib in range(NB):
                r = ib % 2
                if ib >= 2:
                    act.wait_ge(t_full, ib - 1)
                act.activation(blk[:, r, :], m.agg[:, ib * BT:(ib + 1) * BT, :], ACT.Copy, scale=1.0 / HS).then_inc(blk_ready, 1)
                act.wait_ge(t_full, ib + 1)
                if ib >= 2:
                    act.wait_ge(mx_full, ib - 1)
                act.activation(blk_t[:, r, :], m.acc[0][:, r, :], ACT.Copy).then_inc(t_free, 1)
                act.wait_ge(mx_full, ib + 1)
                act.activation(m.agg[:, ib * BT:(ib + 1) * BT, :], m.acc[1][:, r, :], ACT.Copy).then_inc(mx_free, 1)
            turn = [0]

            def take(n=1):
                turn[0] += n
                act.wait_ge(for_act, turn[0])

            done = [1]

            def give(ins):
                done[0] += 1
                ins.then_inc(for_dve, 1)
                act.wait_ge(for_dve, done[0])

            take()
            act.wait_ge(mx_free, NB)
            give(act.activation(big[:, :, :], m.agg[:, :, :], ACT.Square))
            for v, lnv, y0 in ((S("xn2"), S("lnv"), S("y0")), (S("mn2"), S("lnv"), S("y0")), (B("n2"), B("lnv"), B("y0"))):
                take()
                give(act.activation(lnv, v, ACT.Ln, scale=ROOT_SCALE))
                give(act.activation(y0, lnv, ACT.Exp, scale=-0.5))
            take()
            give(act.activation(S("lp"), S("n_x"), ACT.Ln, bias=1.0))
            give(act.activation(S("lm"), S("n_x"), ACT.Ln, scale=-1.0, bias=1.0))
            take()
            give(act.activation(S("th"), S("arg"), ACT.Tanh))
            give(act.activation(B("th"), B("n"), ACT.Tanh))
            take()
            give(act.activation(big[:, :, :], m.agg[:, :, :], ACT.Square))
            take()
            give(act.activation(S("lnv"), S("hn2"), ACT.Ln, scale=ROOT_SCALE))
            give(act.activation(S("y0"), S("lnv"), ACT.Exp, scale=-0.5))
            take()
            give(act.activation(S("lp"), S("n_h"), ACT.Ln, bias=1.0))
            give(act.activation(S("lm"), S("n_h"), ACT.Ln, scale=-1.0, bias=1.0))
            take()
            give(act.activation(m.hh[:, :, 0:D], m.agg[:, :, :], ACT.Copy))

        @block.vector
        def _(dve):
            link = chain(dve, step)
            got = [0]

            def hand(ins):
                got[0] += 1
                ins.then_inc(for_act, 1)
                dve.wait_ge(for_act, got[0])

            back = [0]

            def take(n=1):
                back[0] += n
                dve.wait_ge(for_dve, back[0])

            tt = lambda out, x, y, op: link(dve.tensor_tensor(out, x, y, op))
            ts = lambda out, x, s1, op0, s2=None, op1=ALU.bypass: link(dve.tensor_scalar(out, x, s1, s2, op0, op1)
                                                                      if s2 is not None else dve.tensor_scalar(out, x, s1, None, op0))

            def root(v, y0, tmp, rs, n):
                hand(dve.tensor_scalar(v, v, TINY, None, ALU.max))
                take(2)
                ts(y0, y0, ROOT_SCALE ** 0.5, ALU.mult)
                rsqrt_newton(dve, link, rs, y0, v, tmp, 1.0)
                tt(n, v, rs, ALU.mult)

            def artanh(n, out):
                take(2)
                tt(out, S("lp"), S("lm"), ALU.subtract)
                ts(out, out, 0.5, ALU.mult)
                tt(S("sq"), n, n, ALU.mult)
                ts(S("poly"), S("sq"), 1 / 15, ALU.mult, 1 / 13, ALU.add)
                for k in (11, 9, 7, 5, 3, 1):
                    tt(S("poly"), S("poly"), S("sq"), ALU.mult)
                    ts(S("poly"), S("poly"), 1 / k, ALU.add)
                tt(S("poly"), S("poly"), n, ALU.mult)
                tt(S("poly"), S("poly"), out, ALU.subtract)
                ts(S("mask"), n, 0.25, ALU.is_lt)
                tt(S("poly"), S("poly"), S("mask"), ALU.mult)
                tt(out, out, S("poly"), ALU.add)

            take()
            hand(dve.reduce_sum(S("xn2"), big[:, :, :], axis=AX.X))
            dve.wait_ge(w_in_, 32)
            take()
            link(dve.reduce_sum(S("mn2"), big[:, :, :], axis=AX.X))
            tt(big[:, :, :], m.agg[:, :, :], bias_w, ALU.mult)
            link(dve.reduce_sum(S("dot"), big[:, :, :], axis=AX.X))
            tt(b_sq[:, :], bias[:, :], bias[:, :], ALU.mult)
            link(dve.reduce_sum(B("n2"), b_sq[:, :], axis=AX.X))
            root(S("xn2"), S("y0"), S("tmp"), S("rs_x"), S("n_x"))
            root(S("mn2"), S("y0"), S("tmp"), S("rs_m"), S("n_m"))
            root(B("n2"), B("y0"), B("tmp"), B("rs"), B("n"))
            hand(dve.tensor_scalar(S("n_x"), S("n_x"), 1.0 - 1e-7, None, ALU.min))
            artanh(S("n_x"), S("at_x"))
            tt(S("arg"), S("n_m"), S("rs_x"), ALU.mult)
            hand(dve.tensor_tensor(S("arg"), S("arg"), S("at_x"), ALU.mult))
            take(2)
            ts(S("alpha"), S("th"), MAXNORM, ALU.min)
            tt(S("alpha"), S("alpha"), S("rs_m"), ALU.mult)
            ts(B("beta"), B("th"), MAXNORM, ALU.min)
            tt(B("beta"), B("beta"), B("rs"), ALU.mult)
            tt(B("y2"), B("beta"), B("beta"), ALU.mult)
            tt(B("y2"), B("y2"), B("n2"), ALU.mult)
            tt(S("x2"), S("alpha"), S("alpha"), ALU.mult)
            tt(S("x2"), S("x2"), S("mn2"), ALU.mult)
            tt(S("xy"), S("alpha"), S("dot"), ALU.mult)
            ts(S("xy"), S("xy"), B("beta"), ALU.mult, 2.0, ALU.mult)
            ts(S("num_a"), S("xy"), B("y2"), ALU.add, 1.0, ALU.add)
            ts(S("num_b"), S("x2"), -1.0, ALU.mult, 1.0, ALU.add)
            ts(S("den"), S("x2"), B("y2"), ALU.mult, 1.0, ALU.add)
            tt(S("den"), S("den"), S("xy"), ALU.add)
            ts(S("den"), S("den"), 1e-15, ALU.max)
            link(dve.reciprocal(S("den"), S("den")))
            tt(S("c1"), S("num_a"), S("alpha"), ALU.mult)
            tt(S("c1"), S("c1"), S("den"), ALU.mult)
            ts(S("c2"), S("num_b"), B("beta"), ALU.mult)
            tt(S("c2"), S("c2"), S("den"), ALU.mult)
            tt(m.agg[:, :, :], m.agg[:, :, :], wide(S("c1")), ALU.mult)
            tt(big[:, :, :], bias_w, wide(S("c2")), ALU.mult)
            hand(dve.tensor_tensor(m.agg[:, :, :], m.agg[:, :, :], big[:, :, :], ALU.add))
            take()
            link(dve.reduce_sum(S("hn2"), big[:, :, :], axis=AX.X))
            root(S("hn2"), S("y0"), S("tmp"), S("rs_h"), S("n_h"))
            hand(dve.tensor_scalar(S("n_h"), S("n_h"), MAXNORM, None, ALU.min))
            artanh(S("n_h"), S("at_h"))
            tt(S("coef"), S("at_h"), S("rs_h"), ALU.mult)
            ts(S("coef"), S("coef"), HS, ALU.mult)
            hand(dve.tensor_tensor(m.agg[:, :, :], m.agg[:, :, :], wide(S("coef")), ALU.mult))
            take()
            link(dve.tensor_tensor(m.hh[:, :, D:2 * D], m.agg[:, :, :], m.hh[:, :, 0:D], ALU.subtract))


def hyperbolic_out(nc, m, scale, tag):
    with ExitStack() as ctx:
        sb = lambda name: ctx.enter_context(nc.sbuf_tensor(f"o_{name}_{tag}", [P, T], FP32))
        sem = lambda name: ctx.enter_context(nc.semaphore(f"{name}_{tag}"))
        v2, r2, lnv, y0, tmp, rs_v, n_v, rs_r, n_r, th = (sb(n) for n in ("v2", "r2", "lnv", "y0", "tmp", "rsv", "nv", "rsr", "nr", "th"))
        big = ctx.enter_context(nc.sbuf_tensor(f"o_big_{tag}", [P, T, D], FP32))
        step, for_act, for_dve = sem("step"), sem("for_act"), sem("for_dve")
        block = ctx.enter_context(nc.Block())

        @block.scalar
        def _(act):
            act.activation(big[:, :, :], m.agg[:, :, :], ACT.Square, scale=scale).then_inc(for_dve, 1)
            act.wait_ge(for_act, 1)
            act.activation(m.agg[:, :, :], m.agg[:, :, :], ACT.Relu, scale=scale).then_inc(for_dve, 1)
            act.wait_ge(for_dve, 2)
            act.activation(big[:, :, :], m.agg[:, :, :], ACT.Square).then_inc(for_dve, 1)
            for k, v in enumerate((v2, r2)):
                act.wait_ge(for_act, 2 + k)
                act.activation(lnv[:, :], v[:, :], ACT.Ln, scale=ROOT_SCALE).then_inc(for_dve, 1)
                act.wait_ge(for_dve, 4 + 2 * k)
                act.activation(y0[:, :], lnv[:, :], ACT.Exp, scale=-0.5).then_inc(for_dve, 1)
            act.wait_ge(for_act, 4)
            act.activation(th[:, :], n_r[:, :], ACT.Tanh).then_inc(for_dve, 1)

        @block.vector
        def _(dve):
            link = chain(dve, step)
            dve.wait_ge(for_dve, 1)
            dve.reduce_sum(v2[:, :], big[:, :, :], axis=AX.X).then_inc(for_act, 1)
            dve.wait_ge(for_dve, 3)
            link(dve.reduce_sum(r2[:, :], big[:, :, :], axis=AX.X))
            for k, (v, rs, n) in enumerate(((v2, rs_v, n_v), (r2, rs_r, n_r))):
                dve.tensor_scalar(v[:, :], v[:, :], TINY, None, ALU.max).then_inc(for_act, 1)
                dve.wait_ge(for_dve, 5 + 2 * k)
                link(dve.tensor_scalar(y0[:, :], y0[:, :], ROOT_SCALE ** 0.5, None, ALU.mult))
                rsqrt_newton(dve, link, rs[:, :], y0[:, :], v[:, :], tmp[:, :], 1.0)
                link(dve.tensor_tensor(n[:, :], v[:, :], rs[:, :], ALU.mult))
            link(dve.tensor_scalar(rs_v[:, :], rs_v[:, :], ATANH_MAX, 1.0, ALU.mult, ALU.min))
            dve.tensor_tensor(n_r[:, :], n_r[:, :], rs_v[:, :], ALU.mult).then_inc(for_act, 1)
            dve.wait_ge(for_dve, 8)
            link(dve.tensor_scalar(th[:, :], th[:, :], MAXNORM, None, ALU.min))
            link(dve.tensor_tensor(th[:, :], th[:, :], rs_r[:, :], ALU.mult))
            link(dve.tensor_tensor(m.agg[:, :, :], m.agg[:, :, :], th[:, :].unsqueeze(2).to_broadcast([P, T, D]), ALU.mult))
            link(dve.tensor_tensor(m.x[:, :, :], m.x[:, :, :], m.agg[:, :, :], ALU.add))


def judge(nc, m):
    with ExitStack() as ctx:
        sb = lambda name, shape: ctx.enter_context(nc.sbuf_tensor(name, shape, FP32))
        sem = lambda name: ctx.enter_context(nc.semaphore(name))
        n1, n0, tot, odd = sb("n_one", [P, NB]), sb("n_nonzero", [P, NB]), sb("tot_row", [1, NB + 1]), sb("odd", [1, 1])
        step, diff_ready, summed = sem("j_step"), sem("diff_ready"), sem("summed")
        block = ctx.enter_context(nc.Block())

        @block.vector
        def _(dve):
            link = chain(dve, step)
            link(dve.reduce_sum(n0[:, :], m.nz[:, :].rearrange("p (b k) -> p b k", k=NCH), axis=AX.X))
            link(dve.reduce_sum(n1[:, :], m.cnt1[:, :].rearrange("p (b k) -> p b k", k=BT), axis=AX.X))
            dve.tensor_tensor(n0[:, :], n0[:, :], n1[:, :], ALU.subtract).then_inc(diff_ready, 1)
            dve.wait_ge(summed, 1)
            link(dve.tensor_copy(tot[:, :], m.acc[0][0:1, 0, 0:NB + 1]))
            link(dve.reduce_sum(odd[:, :], tot[:, :], axis=AX.X))
            link(dve.tensor_scalar(odd[:, :], odd[:, :], 0.5, None, ALU.is_gt))
            link(dve.tensor_copy(m.flag[:, :], odd[:, :]))

        @block.tensor
        def _(pe):
            pe.wait_ge(diff_ready, 1)
            pe.matmul(m.acc[0][0:1, 0, 0:NB], m.ones[:, :], n0[:, :], start=True, stop=True)
            pe.matmul(m.acc[0][0:1, 0, NB:NB + 1], m.ones[0:CLS, :], m.ybad[:, :], start=True, stop=True).then_inc(summed, 1)


def store_x(nc, m, out, tag):
    with ExitStack() as ctx:
        stored = ctx.enter_context(nc.semaphore(f"stored_{tag}"))
        block = ctx.enter_context(nc.Block())

        @block.sync
        def _(sp):
            sp.dma_start(out.rearrange("p (t d) -> p t d", d=D), m.x[:, :, :]).then_inc(stored, 16)
            sp.wait_ge(stored, 16)

MASKED, PLAIN, SENSITIVE = "masked", "plain", "sensitive"


def aggregate_any(nc, m, a, mode, tag):
    KC = CH * W
    with ExitStack() as ctx:
        sem = lambda name: ctx.enter_context(nc.semaphore(f"{name}_{tag}"))
        sb = lambda name, shape: ctx.enter_context(nc.sbuf_tensor(f"{name}_{tag}", shape, FP32))
        src = sb("src", [P, T, D])
        adj = sb("adj_any", [P, 2, KC])
        wts = sb("wts", [P, 2, KC]) if mode != PLAIN else adj
        if mode == MASKED:
            yt, yb, abs_sum, magnitude = (sb("yt_any", [CLS, NP]), sb("yb_any", [CLS, W]), sb("abs_sum", [P, W]),
                                          sb("magnitude", [P, W]))
        if mode == SENSITIVE:
            inv = sb("inv", [P, KC])
        adj_in = [sem(f"adj_in{k}") for k in range(2)]
        y_in, yb_ready, labels_ready, labels_used = sem("y_in"), sem("yb_ready"), sem("labels_ready"), sem("labels_used")
        src_ready, adj_used, wts_ready, wts_used = sem("src_ready"), sem("adj_used"), sem("wts_ready"), sem("wts_used")
        abs_step, acc_free, rows_ready, inv_ready, exp_ready, sens_step = (
            sem("abs_step"), sem("acc_free"), sem("rows_ready"), sem("inv_ready"), sem("exp_ready"), sem("sens_step"))
        block = ctx.enter_context(nc.Block())

        @block.sync
        def _(sp):
            if mode == MASKED:
                sp.dma_start(yt[:, :], a["L0_gnn_y"]).then_inc(y_in, 16)
            with sp.Fori(0, NB) as ib:
                for k in range(NCH):
                    sp.wait_ge(wts_used if mode == PLAIN else adj_used, ib * NCH + (k + 1))
                    sp.dma_start(adj[:, k % 2, :], a["adj"][bass.ds(ib, 1), :, k * KC:(k + 1) * KC]
                                 .rearrange("b p n -> (b p) n")).then_inc(adj_in[k % 2], 16)

        @block.tensor
        def _(pe):
            pe.sem_inc(wts_used, 2)
            pe.wait_ge(src_ready, 1)
            with pe.Fori(0, NB) as ib:
                pe.wait_ge(acc_free, ib + 1)
                for k in range(NCH):
                    if mode == MASKED:
                        if k == 0:
                            pe.wait_ge(yb_ready, ib + 1)
                        for j in range(CH // 2):
                            pe.wait_ge(labels_used, ib * (T // 2) + (k * CH // 2 + j + 1))
                            for s in range(2):
                                t = k * CH + 2 * j + s
                                mm = pe.matmul(m.acc[2 + j][:, s, :], yt[:, t * P:(t + 1) * P], yb[:, :], start=True, stop=True)
                            mm.then_inc(labels_ready, 1)
                    if mode == PLAIN:
                        pe.wait_ge(adj_in[k % 2], (ib * (NCH // 2) + (k // 2 + 1)) * 16)
                    else:
                        pe.wait_ge(wts_ready, ib * NCH + (k + 1))
                    for j in range(CH):
                        for it in range(BT):
                            at = j * W + it * P
                            mm = pe.matmul(m.acc[it // 2][:, it % 2, 0:D], wts[:, k % 2, at:at + P], src[:, k * CH + j, :],
                                           start=(k + j == 0), stop=(k == NCH - 1 and j == CH - 1))
                    mm.then_inc(wts_used, 1)
                if mode == MASKED:
                    pe.wait_ge(labels_used, ib * (T // 2) + (T // 2 + 2))
                    pe.wait_ge(abs_step, ib * (2 * NCH * CH + 1) + (2 * NCH * CH + 1))
                    for it in range(BT):
                        mm = pe.matmul(m.acc[2][:, 0, it:it + 1], abs_sum[:, it * P:(it + 1) * P], m.ones[:, :], start=True, stop=True)
                    mm.then_inc(rows_ready, 1)

        @block.scalar
        def _(act):
            act.activation(src[:, :, :], m.agg[:, :, :], ACT.Copy).then_inc(src_ready, 1)
            if mode == MASKED:
                act.wait_ge(y_in, 16)
                with act.Fori(0, NB) as ib:
                    act.wait_ge(labels_ready, ib * (T // 2) + 1)
                    act.activation(yb[:, :], yt[:, bass.ds(ib * W, W)], ACT.Copy).then_inc(yb_ready, 1)
            if mode == SENSITIVE:
                with act.Fori(0, NB) as ib:
                    for k in range(NCH):
                        act.wait_ge(inv_ready, ib * NCH + (k + 1))
                        act.activation(inv[:, :], inv[:, :], ACT.Square).then_inc(exp_ready, 1)
                        act.wait_ge(exp_ready, ib * 2 * NCH + (2 * k + 1))
                        act.activation(inv[:, :], inv[:, :], ACT.Exp, scale=-2.0).then_inc(exp_ready, 1)

        @block.vector
        def _(dve):
            dve.sem_inc(adj_used, 2)
            dve.sem_inc(labels_used, 2)
            dve.sem_inc(acc_free, 1)
            if mode == MASKED:
                dve.sem_inc(labels_ready, 1)
                dve.wait_ge(y_in, 16)
            dve.wait_ge(src_ready, 1)
            with dve.Fori(0, NB) as ib:
                if mode == MASKED:
                    dve.memset(abs_sum[:, :], 0.0).then_inc(abs_step, 1)
                for k in range(NCH) if mode != PLAIN else ():
                    dve.wait_ge(adj_in[k % 2], (ib * (NCH // 2) + (k // 2 + 1)) * 16)
                    dve.wait_ge(wts_used, ib * NCH + (k + 1))
                    if mode == MASKED:
                        for j in range(CH // 2):
                            dve.wait_ge(labels_ready, ib * (T // 2) + (k * CH // 2 + j + 2))
                            at = slice(2 * j * W, 2 * (j + 1) * W)
                            dve.tensor_tensor(wts[:, k % 2, at].rearrange("p (s n) -> p s n", s=2),
                                              adj[:, k % 2, at].rearrange("p (s n) -> p s n", s=2),
                                              m.acc[2 + j][:, :, :], ALU.mult).then_inc(labels_used, 1)
                        dve.wait_ge(labels_used, ib * (T // 2) + ((k + 1) * CH // 2 + 2))
                        dve.nop(nofuse=True)
                        dve.engine_nop().then_inc(adj_used, 1)
                        dve.engine_nop().then_inc(wts_ready, 1)
                        for j in range(CH):
                            step = 2 * (k * CH + j)
                            part = wts[:, k % 2, j * W:(j + 1) * W]
                            dve.scalar_tensor_tensor(out=magnitude[:, :], in0=part, scalar=-1.0, in1=part,
                                                     op0=ALU.mult, op1=ALU.max).then_inc(abs_step, 1)
                            dve.wait_ge(abs_step, ib * (2 * NCH * CH + 1) + (step + 2))
                            dve.tensor_tensor(abs_sum[:, :], abs_sum[:, :], magnitude[:, :], ALU.add).then_inc(abs_step, 1)
                    else:
                        n = 3 * k
                        dve.tensor_scalar(wts[:, k % 2, :], adj[:, k % 2, :], 0.0, 1e-18, ALU.is_equal, ALU.mult).then_inc(sens_step, 1)
                        dve.wait_ge(sens_step, ib * 3 * NCH + (n + 1))
                        dve.tensor_tensor(wts[:, k % 2, :], wts[:, k % 2, :], adj[:, k % 2, :], ALU.add).then_inc(sens_step, 1)
                        dve.wait_ge(sens_step, ib * 3 * NCH + (n + 2))
                        dve.reciprocal(inv[:, :], wts[:, k % 2, :]).then_inc(sens_step, 1)
                        dve.wait_ge(sens_step, ib * 3 * NCH + (n + 3))
                        dve.tensor_scalar(inv[:, :], inv[:, :], -1.0, None, ALU.add).then_inc(inv_ready, 1)
                        dve.wait_ge(exp_ready, ib * 2 * NCH + (2 * k + 2))
                        dve.scalar_tensor_tensor(out=wts[:, k % 2, :], in0=adj[:, k % 2, :], scalar=1.0, in1=inv[:, :],
                                                 op0=ALU.is_lt, op1=ALU.mult).then_inc(wts_ready, 1)
                        dve.wait_ge(wts_ready, ib * NCH + (k + 1))
                        dve.nop(nofuse=True)
                        dve.engine_nop().then_inc(adj_used, 1)
                dve.wait_ge(wts_used, ib * NCH + (NCH + 2))
                for b in range(2):
                    last = dve.tensor_copy(m.agg[:, bass.ds(ib * BT + 2 * b, 2), :], m.acc[b][:, :, 0:D])
                if mode == MASKED:
                    dve.wait_ge(rows_ready, ib + 1)
                    last = dve.tensor_copy(m.rows[:, bass.ds(ib * BT, BT)], m.acc[2][:, 0, 0:BT])
                last.then_inc(acc_free, 1)


def message(nc, m, a):
    with ExitStack() as ctx:
        sem = lambda name: ctx.enter_context(nc.semaphore(name))
        sb = lambda name, shape: ctx.enter_context(nc.sbuf_tensor(name, shape, FP32))
        w3, b3 = sb("l3_w", [P, D]), sb("l3_b", [P, D])
        blk, blk_t = sb("l3_blk", [P, BT * D]), sb("l3_blk_t", [P, W])
        w3_in, blk_ready, t_full, t_free, mx_full, mx_free = (
            sem("w3_in"), sem("l3_blk_ready"), sem("l3_t_full"), sem("l3_t_free"), sem("l3_mx_full"), sem("l3_mx_free"))
        block = ctx.enter_context(nc.Block())

        @block.sync
        def _(sp):
            sp.dma_start(w3[:, :], a["L3_gnn_W"]).then_inc(w3_in, 16)
            sp.dma_start(b3[:, :], a["L3_gnn_B"]).then_inc(w3_in, 16)

        @block.scalar
        def _(act):
            with act.Fori(0, NB) as ib:
                act.wait_ge(mx_free, ib + 1)
                act.activation(blk[:, :], m.agg[:, bass.ds(ib * BT, BT), :], ACT.Copy, scale=1.0 / HS).then_inc(blk_ready, 1)
                act.wait_ge(t_full, ib + 1)
                act.activation(blk_t[:, :], m.acc[0][:, 0, :], ACT.Copy).then_inc(t_free, 1)

        @block.tensor
        def _(pe):
            pe.wait_ge(w3_in, 32)
            with pe.Fori(0, NB) as ib:
                pe.wait_ge(blk_ready, ib + 1)
                for t in range(BT):
                    mm = pe.transpose(m.acc[0][:, 0, t * P:(t + 1) * P], blk[:, t * D:(t + 1) * D], m.ident[:, :])
                mm.then_inc(t_full, 1)
                pe.wait_ge(t_free, ib + 1)
                for t in range(BT):
                    mm = pe.matmul(m.acc[1][:, 0, t * P:(t + 1) * P], blk_t[:, t * P:(t + 1) * P], w3[:, :], start=True, stop=True)
                mm.then_inc(mx_full, 1)

        @block.vector
        def _(dve):
            dve.sem_inc(mx_free, 1)
            dve.wait_ge(w3_in, 32)
            with dve.Fori(0, NB) as ib:
                dve.wait_ge(mx_full, ib + 1)
                dve.tensor_tensor(m.agg[:, bass.ds(ib * BT, BT), :], m.acc[1][:, 0, :].rearrange("p (t d) -> p t d", d=D),
                                  b3[:, :].unsqueeze(1).to_broadcast([P, BT, D]), ALU.add).then_inc(mx_free, 1)


def add_agg(nc, m):
    with ExitStack() as ctx:
        added = ctx.enter_context(nc.semaphore("added"))
        block = ctx.enter_context(nc.Block())

        @block.vector
        def _(dve):
            dve.tensor_tensor(m.x[:, :, :], m.x[:, :, :], m.agg[:, :, :], ALU.add).then_inc(added, 1)
            dve.wait_ge(added, 1)


def reload_x(nc, m, a):
    with ExitStack() as ctx:
        x_again = ctx.enter_context(nc.semaphore("x_again"))
        block = ctx.enter_context(nc.Block())

        @block.sync
        def _(sp):
            sp.dma_start(m.x[:, :, :], a["x"].rearrange("p (t d) -> p t d", d=D)).then_inc(x_again, 16)
            sp.wait_ge(x_again, 16)

        @block.scalar
        def _(act):
            act.wait_ge(x_again, 16)

        @block.tensor
        def _(pe):
            pe.wait_ge(x_again, 16)

        @block.vector
        def _(dve):
            dve.wait_ge(x_again, 16)

        @block.gpsimd
        def _(pool):
            pool.wait_ge(x_again, 16)


def binary_path(nc, m, a):
    setup(nc, m, a)
    layernorm_halves(nc, m, "l0")
    aggregate_masked(nc, m, a)
    after_l0(nc, m, a, "fast")
    layernorm_halves(nc, m, "l1")
    aggregate_compact(nc, m, True, "l1")
    mamba(nc, m, a, 1.0 / HS, "fast")
    layernorm_halves(nc, m, "l2")
    hyperbolic_in(nc, m, a, "fast")
    aggregate_compact(nc, m, False, "l2")
    hyperbolic_out(nc, m, 1.0 / HS, "fast")


def general_path(nc, m, a):
    reload_x(nc, m, a)
    layernorm_halves(nc, m, "g0")
    aggregate_any(nc, m, a, MASKED, "g0")
    after_l0(nc, m, a, "any")
    layernorm_halves(nc, m, "g1")
    aggregate_any(nc, m, a, PLAIN, "g1")
    mamba(nc, m, a, 1.0 / HS, "any")
    layernorm_halves(nc, m, "g2")
    hyperbolic_in(nc, m, a, "any")
    aggregate_any(nc, m, a, PLAIN, "g2")
    hyperbolic_out(nc, m, 1.0 / HS, "any")
    layernorm_halves(nc, m, "g3")
    message(nc, m, a)
    aggregate_any(nc, m, a, SENSITIVE, "g3")
    add_agg(nc, m)


def program(nc, a, out):
    with ExitStack() as ctx:
        m = Memory(nc, ctx)
        binary_path(nc, m, a)
        judge(nc, m)
        store_x(nc, m, out, "fast")
        other = nc.values_load(m.flag[0:1, 0:1], min_val=0, max_val=1)
        with nc.If(other > 0):
            general_path(nc, m, a)
            store_x(nc, m, out, "any")


def laid_out(x):
    import numpy as np
    rows = np.zeros((NP, x.shape[1]), x.dtype)
    rows[:N] = x
    return np.ascontiguousarray(rows.reshape(T, P, x.shape[1]).transpose(1, 0, 2).reshape(P, -1))


def halves(v):
    import numpy as np
    return np.ascontiguousarray(v.reshape(2, P, -1).transpose(1, 0, 2).reshape(P, -1))


def on_all(v):
    import numpy as np
    return np.ascontiguousarray(np.broadcast_to(v.reshape(1, -1), (P, v.size)))


def kernel(**inputs):
    import numpy as np
    import concourse.bacc as bacc
    from concourse.bass_utils import run_bass_kernel_spmd as run

    g = {k: np.asarray(v) for k, v in inputs.items()}
    adj = np.zeros((NP, NP), g["adj"].dtype)
    adj[:N, :N] = g["adj"]
    adj = np.ascontiguousarray(adj.reshape(NB, W, T, P).transpose(0, 3, 2, 1).reshape(NB, P, T * W))
    y = np.zeros((CLS, NP), g["L0_gnn_y"].dtype)
    y[:, :N] = g["L0_gnn_y"].T
    w_xp = g["L1_gnn_w_xp"]
    dt_cols, b_cols, c_cols = w_xp[:, :RANK], w_xp[:, RANK:RANK + ST], w_xp[:, RANK + ST:]
    arrays = {
        "x": laid_out(g["x"]), "adj": adj, "L0_gnn_h0": laid_out(g["L0_gnn_h0"]), "L0_gnn_y": y,
        "L1_gnn_gcn_w": g["L1_gnn_gcn_w"], "L1_gnn_gcn_b": on_all(g["L1_gnn_gcn_b"]),
        "L1_gnn_ln_g": g["L1_gnn_ln_g"].reshape(P, 1), "L1_gnn_ln_b": g["L1_gnn_ln_b"].reshape(P, 1),
        "L1_gnn_w_in": g["L1_gnn_w_in"], "L1_gnn_conv_w": halves(g["L1_gnn_conv_w"]), "L1_gnn_conv_b": halves(g["L1_gnn_conv_b"]),
        "w_cb": halves(np.concatenate([c_cols, b_cols] * 3, axis=1)), "w_r": halves(dt_cols),
        "L1_gnn_w_dt": g["L1_gnn_w_dt"], "L1_gnn_b_dt": halves(g["L1_gnn_b_dt"]), "L1_gnn_A_log": halves(g["L1_gnn_A_log"]),
        "L1_gnn_D_skip": halves(g["L1_gnn_D_skip"]), "L1_gnn_w_out": halves(g["L1_gnn_w_out"]),
        "L2_gnn_weight": np.ascontiguousarray(g["L2_gnn_weight"].T), "L2_gnn_bias": on_all(g["L2_gnn_bias"]),
        "L3_gnn_W": g["L3_gnn_W"], "L3_gnn_B": on_all(g["L3_gnn_B"]),
    }
    nc = bacc.Bacc("TRN2", target_bir_lowering=False, num_devices=1)
    a = {k: nc.dram_tensor(f"in_{k}", v.shape, mybir.dt.from_np(v.dtype), kind="ExternalInput").ap() for k, v in arrays.items()}
    out = nc.dram_tensor("out_0", (P, T * D), FP32, kind="ExternalOutput").ap()
    program(nc, a, out)
    r = run(nc, [{f"in_{k}": np.ascontiguousarray(v) for k, v in arrays.items()}], core_ids=[0])
    return np.ascontiguousarray(r.results[0]["out_0"].reshape(P, T, D).transpose(1, 0, 2).reshape(NP, D)[:N])
```

```python
from contextlib import ExitStack

import concourse.bass as bass
from concourse import mybir

FP32, BF16, FP16 = mybir.dt.float32, mybir.dt.bfloat16, mybir.dt.float16
FP8, U32, I32 = mybir.dt.float8e4, mybir.dt.uint32, mybir.dt.int32
ALU, ACT, AX = mybir.AluOpType, mybir.ActivationFunctionType, mybir.AxisListType

N = 5000
P = 128
D = 128
CLS = 16
T = -(-N // P)
NP = T * P
W = 512
NB = NP // W
BT = W // P
CH = 4
NCH = T // CH
RING = 5
QT = T // 4
HS = 4096.0
HW = 2 * D + 1
HP = 260
INNER = 256
ST = 16
RANK = 8
TAPS = 4
UN = 2 * ST
LN_EPS = 1e-5
L1_FLOOR = 1e-12
TINY = 1e-30
MAXNORM = 1.0 - 1e-5
ATANH_MAX = 6.10303382275888
DATA = ["x", "adj", "L0_gnn_h0", "L0_gnn_y"]


def chain(eng, sem):
    count = [0]

    def link(ins):
        count[0] += 1
        ins.then_inc(sem, 1)
        eng.wait_ge(sem, count[0])

    return link


ROOT_SCALE = 2.0 ** 36


class Memory:

    def __init__(self, nc, ctx):
        def sb(name, shape, dt):
            return ctx.enter_context(nc.sbuf_tensor(name, shape, dt))

        self.x = sb("x_cur", [P, T, D], FP32)
        self.agg = sb("agg", [P, T, D], FP32)
        self.hh = sb("h_halves", [P, T, HP], FP16)
        self.rows = sb("row_sum", [P, T], FP32)
        self.cnt1 = sb("count_one", [P, T], FP32)
        self.nz = sb("count_nonzero", [P, NB * NCH], FP32)
        self.ybad = sb("y_bad", [CLS, 1], FP32)
        self.ident = sb("ident", [P, P], FP32)
        self.ones = sb("ones", [P, 1], FP32)
        self.flag = sb("flag", [1, 1], I32)
        self.acc = [ctx.enter_context(nc.psum_tensor(f"ps{k}", [P, 2, W], FP32)) for k in range(4)]
        self.adj8 = nc.dram_tensor("adj_compact", (NB, P, T * W // 2), BF16, kind="Internal").ap()
        self.b_rows = nc.dram_tensor("b_rows", (2, ST * W), FP32, kind="Internal").ap()


def setup(nc, m, a):
    with ExitStack() as ctx:
        sem = lambda name: ctx.enter_context(nc.semaphore(name))
        yt = ctx.enter_context(nc.sbuf_tensor("yt_chk", [CLS, NP], FP32))
        junk = ctx.enter_context(nc.sbuf_tensor("y_junk", [CLS, NP], BF16))
        x_in, y_in, zeroed, made, bad = sem("x_in"), sem("y_in"), sem("zeroed"), sem("made"), sem("bad")
        block = ctx.enter_context(nc.Block())

        @block.sync
        def _(sp):
            sp.dma_start(m.x[:, :, :], a["x"].rearrange("p (t d) -> p t d", d=D)).then_inc(x_in, 16)
            sp.dma_start(yt[:, :], a["L0_gnn_y"]).then_inc(y_in, 16)
            sp.wait_ge(x_in, 16)

        @block.gpsimd
        def _(pool):
            pool.memset(m.ident[:, :], 0.0).then_inc(zeroed, 1)
            pool.wait_ge(zeroed, 1)
            pool.affine_select(out=m.ident[:, :], in_=m.ident[:, :], compare_op=ALU.not_equal, fill=1.0,
                               base=0, pattern=[[-1, P]], channel_multiplier=1).then_inc(made, 1)
            pool.wait_ge(made, 1)

        @block.vector
        def _(dve):
            dve.memset(m.ones[:, :], 1.0)
            dve.memset(m.hh[:, :, 2 * D:HP], 1.0)
            dve.wait_ge(y_in, 16)
            dve.scalar_tensor_tensor(out=junk[:, :], in0=yt[:, :], scalar=1.0, in1=yt[:, :],
                                     op0=ALU.is_equal, op1=ALU.not_equal, accum_out=m.ybad[:, :]).then_inc(bad, 1)
            dve.wait_ge(bad, 1)


def rsqrt_newton(dve, link, out, y0, v, tmp, floor_scale):
    link(dve.tensor_tensor(tmp, y0, y0, ALU.mult))
    link(dve.tensor_tensor(tmp, tmp, v, ALU.mult))
    link(dve.tensor_scalar(tmp, tmp, -0.5 * floor_scale, 1.5 * floor_scale, ALU.mult, ALU.add))
    link(dve.tensor_tensor(out, tmp, y0, ALU.mult))


GT = T // 5


def layernorm(nc, ctx, m, tag, halves):
    sem = lambda name: ctx.enter_context(nc.semaphore(f"{name}_{tag}"))
    small = lambda name, *shape: ctx.enter_context(nc.sbuf_tensor(f"{name}_{tag}", [P, T, *shape], FP32))
    stats, mv = small("stats", 6), small("mv", 2)
    var, lnv, y0, tmp, rstd, shift = (small(s) for s in ("var", "lnv", "y0", "tmp", "rstd", "shift"))
    step, ln_done, var_ready, y0_ready, shift_ready, h_ready, high_ready, halves_ready = (
        sem(s) for s in ("step", "ln_done", "var_ready", "y0_ready", "shift_ready", "h_ready", "high_ready", "halves_ready"))

    def on_vector(dve):
        for t in range(T):
            last = dve.bn_stats(stats[:, t, :], m.x[:, t, :])
        link = chain(dve, step)
        link(last)
        for t in range(T):
            last = dve.bn_aggr(mv[:, t, :], stats[:, t, :])
        link(last)
        dve.tensor_scalar(var[:, :], mv[:, :, 1], LN_EPS, None, ALU.add).then_inc(var_ready, 1)
        dve.wait_ge(y0_ready, 1)
        rsqrt_newton(dve, link, rstd[:, :], y0[:, :], var[:, :], tmp[:, :], HS)
        dve.scalar_tensor_tensor(out=shift[:, :], in0=mv[:, :, 0], scalar=-1.0, in1=rstd[:, :],
                                 op0=ALU.mult, op1=ALU.mult).then_inc(shift_ready, 1)
        if halves:
            for g in range(T // GT):
                at = slice(g * GT, (g + 1) * GT)
                dve.wait_ge(h_ready, g + 1)
                dve.tensor_copy(m.hh[:, at, 0:D], m.agg[:, at, :]).then_inc(high_ready, 1)
                dve.wait_ge(high_ready, g + 1)
                dve.tensor_tensor(m.hh[:, at, D:2 * D], m.agg[:, at, :], m.hh[:, at, 0:D],
                                  ALU.subtract).then_inc(halves_ready, 1)
            dve.wait_ge(halves_ready, T // GT)

    def on_scalar(act):
        act.wait_ge(var_ready, 1)
        act.activation(lnv[:, :], var[:, :], ACT.Ln).then_inc(ln_done, 1)
        act.wait_ge(ln_done, 1)
        act.activation(y0[:, :], lnv[:, :], ACT.Exp, scale=-0.5).then_inc(y0_ready, 1)
        act.wait_ge(shift_ready, 1)
        for g in range(T // GT):
            for t in range(g * GT, (g + 1) * GT):
                last = act.activation(m.agg[:, t, :], m.x[:, t, :], ACT.Relu, scale=rstd[:, t:t + 1], bias=shift[:, t:t + 1])
            last.then_inc(h_ready, 1)

    return on_vector, on_scalar, halves_ready


def layernorm_phase(nc, m, tag):
    with ExitStack() as ctx:
        on_vector, on_scalar, _ = layernorm(nc, ctx, m, tag, halves=False)
        block = ctx.enter_context(nc.Block())

        @block.vector
        def _(dve):
            on_vector(dve)

        @block.scalar
        def _(act):
            on_scalar(act)


def aggregate_masked(nc, m, a):
    KC = CH * W
    NPAIR = T // 2
    with ExitStack() as ctx:
        sem = lambda name: ctx.enter_context(nc.semaphore(name))
        sb = lambda name, shape, dt: ctx.enter_context(nc.sbuf_tensor(name, shape, dt))
        adj = sb("adj32", [P, RING, KC], FP32)
        bits = sb("bits", [P, RING, KC], FP8)
        masked = sb("masked", [P, 4, 2, W], BF16)
        low = sb("low_part", [P, 2, 2, D], FP32)
        junk = sb("sign_out", [P, 2, KC], BF16)
        yt = sb("yt32", [CLS, NP], FP32)
        y16 = sb("yt16", [CLS, NP], BF16)
        yb = sb("y_block", [CLS, W], BF16)
        adj_in = [sem(f"adj_in{k}") for k in range(RING)]
        bits_out = [sem(f"bits_out{k}") for k in range(RING)]
        y_in, y16_ready, yb_ready = sem("y0_in"), sem("y16_ready"), sem("yb_ready")
        counted, bits_ready, pair_ready, pair_masked = sem("counted"), sem("bits_ready"), sem("pair_ready"), sem("pair_masked")
        masked_used, low_ready, acc_free = sem("masked_used"), sem("low_ready"), sem("acc_free")
        h0, inv = sb("h0_block", [P, BT, D], FP32), sb("l0_r", [P, BT], FP32)
        h0_in, r_step, x_step = sem("h0_in"), sem("r_step"), sem("x_step")
        norm_on_vector, norm_on_scalar, halves_ready = layernorm(nc, ctx, m, "l0", halves=True)
        chunks_of = a["adj"]
        block = ctx.enter_context(nc.Block())

        @block.sync
        def _(sp):
            sp.dma_start(yt[:, :], a["L0_gnn_y"]).then_inc(y_in, 16)
            with sp.Fori(0, NB) as ib:
                for k in range(NCH):
                    sp.wait_ge(counted, ib * NCH + k + 1)
                    sp.wait_ge(bits_ready, ib * NCH + k + 1)
                    sp.dma_start(adj[:, k % RING, :],
                                 chunks_of[bass.ds(ib, 1), :, k * KC:(k + 1) * KC].rearrange("b p n -> (b p) n")
                                 ).then_inc(adj_in[k % RING], 16)
                sp.wait_ge(x_step, ib * 4 + 4)
                sp.dma_start(h0[:, :, :], a["L0_gnn_h0"].rearrange("p (b t d) -> b p t d", t=BT, d=D)[bass.ds(ib, 1)]
                             .rearrange("b p t d -> (b p) t d")).then_inc(h0_in, 16)

        @block.scalar
        def _(act):
            act.sem_inc(counted, RING)
            act.wait_ge(y_in, 16)
            act.activation(y16[:, :], yt[:, :], ACT.Copy).then_inc(y16_ready, 1)
            norm_on_scalar(act)
            act.wait_ge(y16_ready, 1)
            with act.Fori(0, NB) as ib:
                act.wait_ge(pair_ready, ib * NPAIR + 1)
                act.activation(yb[:, :], y16[:, bass.ds(ib * W, W)], ACT.Copy).then_inc(yb_ready, 1)
                for k in range(NCH):
                    act.wait_ge(adj_in[k % RING], (ib * (NCH // RING) + k // RING + 1) * 16)
                    act.wait_ge(counted, ib * NCH + (RING + k - 1))
                    act.activation(junk[:, k % 2, :], adj[:, k % RING, :].bitcast(U32), ACT.Sign,
                                   accum_out=m.nz[:, bass.ds(ib * NCH + k, 1)]).then_inc(counted, 1)
                    act.wait_ge(bits_ready, ib * NCH + (RING + k + 1))
                    act.dma_start(m.adj8[bass.ds(ib, 1), :, k * KC // 2:(k + 1) * KC // 2].rearrange("b p n -> (b p) n"),
                                  bits[:, k % RING, :].bitcast(BF16)).then_inc(bits_out[k % RING], 16)
                act.wait_ge(masked_used, ib * NPAIR + (NPAIR + 4))
                for b in range(2):
                    act.activation(low[:, b, :, :], m.acc[b][:, :, D:2 * D], ACT.Copy).then_inc(low_ready, 1)

        @block.vector
        def _(dve):
            dve.sem_inc(bits_ready, RING)
            dve.sem_inc(pair_masked, 3)
            dve.sem_inc(acc_free, 1)
            for k in range(RING):
                dve.sem_inc(bits_out[k], 16)
            norm_on_vector(dve)
            with dve.Fori(0, NB) as ib:
                for k in range(NCH):
                    r = k % RING
                    dve.wait_ge(adj_in[r], (ib * (NCH // RING) + k // RING + 1) * 16)
                    dve.wait_ge(bits_out[r], (ib * (NCH // RING) + k // RING + 1) * 16)
                    dve.nop(nofuse=True)
                    dve.tensor_scalar(bits[:, r, :], adj[:, r, :], 1.0, None, ALU.is_equal,
                                      saturate=False).then_inc(bits_ready, 1)
                    dve.wait_ge(bits_ready, ib * NCH + (RING + k + 1))
                    for j in range(CH // 2):
                        q = k * (CH // 2) + j
                        dve.wait_ge(pair_ready, ib * NPAIR + (q + 2))
                        dve.wait_ge(masked_used, ib * NPAIR + (q + 1))
                        dve.nop(nofuse=True)
                        dve.tensor_tensor(masked[:, q % 4, :, :],
                                          bits[:, r, j * 2 * W:(j + 1) * 2 * W].rearrange("p (s n) -> p s n", s=2),
                                          m.acc[2 + q % 2][:, :, :], ALU.mult).then_inc(pair_masked, 1)
                dve.wait_ge(masked_used, ib * NPAIR + (NPAIR + 4))
                dve.wait_ge(x_step, ib * 4 + 4)
                for b in range(2):
                    dve.wait_ge(low_ready, ib * 2 + (b + 1))
                    dve.tensor_tensor(m.agg[:, bass.ds(ib * BT + 2 * b, 2), :], m.acc[b][:, :, 0:D],
                                      low[:, b, :, :], ALU.add)
                    last = dve.tensor_scalar(inv[:, 2 * b:2 * b + 2], m.acc[b][:, :, 2 * D], L1_FLOOR, None, ALU.max)
                last.then_inc(acc_free, 1)
                dve.wait_ge(acc_free, ib + 2)
                dve.reciprocal(inv[:, :], inv[:, :]).then_inc(r_step, 1)
                dve.wait_ge(r_step, ib * 2 + 1)
                dve.tensor_scalar(inv[:, :], inv[:, :], 0.9 / HS, None, ALU.mult).then_inc(r_step, 1)

        @block.tensor
        def _(pe):
            pe.sem_inc(masked_used, 4)
            pe.sem_inc(pair_ready, 1)

            def labels(ib, q):
                pe.wait_ge(pair_masked, ib * NPAIR + (q + 2))
                for s in range(2):
                    mm = pe.matmul(m.acc[2 + q % 2][:, s, :], y16[:, (2 * q + s) * P:(2 * q + s + 1) * P], yb[:, :],
                                   start=True, stop=True)
                mm.then_inc(pair_ready, 1)

            def gather(ib, q):
                pe.wait_ge(pair_masked, ib * NPAIR + (q + 4))
                if q == 0:
                    pe.wait_ge(acc_free, ib + 1)
                if 2 * q % GT == 0:
                    pe.wait_ge(halves_ready, 2 * q // GT + 1)
                for s in range(2):
                    for it in range(BT):
                        mm = pe.matmul(m.acc[it // 2][:, it % 2, 0:HW], masked[:, q % 4, s, it * P:(it + 1) * P],
                                       m.hh[:, 2 * q + s, 0:HW], start=(q + s == 0), stop=(q == NPAIR - 1 and s == 1))
                mm.then_inc(masked_used, 1)
                return mm

            with pe.Fori(0, NB) as ib:
                pe.wait_ge(yb_ready, ib + 1)
                for q in range(NPAIR):
                    labels(ib, q)
                    if q:
                        gather(ib, q - 1)
                gather(ib, NPAIR - 1)

        @block.gpsimd
        def _(pool):
            pool.sem_inc(x_step, 4)
            pool.wait_ge(halves_ready, T // GT)
            with pool.Fori(0, NB) as ib:
                at = bass.ds(ib * BT, BT)
                pool.wait_ge(h0_in, ib * 16 + 16)
                pool.nop(nofuse=True)
                pool.tensor_scalar(h0[:, :, :], h0[:, :, :], 0.1, None, ALU.mult).then_inc(x_step, 1)
                pool.wait_ge(r_step, ib * 2 + 2)
                pool.nop(nofuse=True)
                pool.tensor_tensor(m.agg[:, at, :], m.agg[:, at, :], inv[:, :].unsqueeze(2).to_broadcast([P, BT, D]),
                                   ALU.mult).then_inc(x_step, 1)
                pool.wait_ge(x_step, ib * 4 + 5)
                pool.nop(nofuse=True)
                pool.tensor_tensor(m.x[:, at, :], m.x[:, at, :], h0[:, :, :], ALU.add).then_inc(x_step, 1)
                pool.wait_ge(x_step, ib * 4 + 7)
                pool.nop(nofuse=True)
                pool.tensor_tensor(m.x[:, at, :], m.x[:, at, :], m.agg[:, at, :], ALU.add).then_inc(x_step, 1)
            for k in range(RING):
                pool.wait_ge(bits_out[k], 16 * (NB * NCH // RING + 1))


def aggregate_compact(nc, m, counting, tag):
    width = HW if counting else 2 * D
    KQ = QT * W
    with ExitStack() as ctx:
        sem = lambda name: ctx.enter_context(nc.semaphore(f"{name}_{tag}"))
        bits = ctx.enter_context(nc.sbuf_tensor(f"bits_{tag}", [P, 4, KQ], FP8))
        low = ctx.enter_context(nc.sbuf_tensor(f"low_{tag}", [P, 4, 2, D], FP32))
        bits_in = [sem(f"bits_in{k}") for k in range(4)]
        bits_used, low_ready, acc_free = sem("bits_used"), sem("low_ready"), sem("acc_free")
        if counting:
            norm_on_vector, norm_on_scalar, halves_ready = layernorm(nc, ctx, m, tag, halves=True)
        else:
            sb = lambda name, *shape: ctx.enter_context(nc.sbuf_tensor(f"tail_{name}", [P, *shape], FP32))
            s_blk, relu, squares = sb("s_blk", BT, D), sb("relu", BT, D), sb("squares", 2, BT, D)
            norm2, lnv, y0, tmp, rs, norm = (sb(n, 2, BT) for n in ("norm2", "lnv", "y0", "tmp", "rs", "norm"))
            arg, coef = sb("arg", BT), sb("coef", BT)
            relu_ready, squares_ready, norm2_ready, ln_ready, y0_ready, arg_ready, th_ready, tail_step, x_ready = (
                sem(f"tail_{n}") for n in ("relu_ready", "squares_ready", "norm2_ready", "ln_ready", "y0_ready", "arg_ready",
                                 "th_ready", "tail_step", "x_ready"))
        block = ctx.enter_context(nc.Block())

        def tail_on_scalar(act, ib):
            act.wait_ge(acc_free, ib + 3)
            act.wait_ge(x_ready, ib + 1)
            act.activation(relu[:, :, :], s_blk[:, :, :], ACT.Relu, scale=1.0 / HS).then_inc(relu_ready, 1)
            act.activation(squares[:, 0, :, :], s_blk[:, :, :], ACT.Square, scale=1.0 / HS)
            act.wait_ge(relu_ready, ib + 1)
            act.activation(squares[:, 1, :, :], relu[:, :, :], ACT.Square).then_inc(squares_ready, 1)
            act.wait_ge(norm2_ready, ib + 1)
            act.activation(lnv[:, :, :], norm2[:, :, :], ACT.Ln, scale=ROOT_SCALE).then_inc(ln_ready, 1)
            act.wait_ge(ln_ready, ib + 1)
            act.activation(y0[:, :, :], lnv[:, :, :], ACT.Exp, scale=-0.5).then_inc(y0_ready, 1)
            act.wait_ge(arg_ready, ib + 1)
            act.activation(coef[:, :], arg[:, :], ACT.Tanh).then_inc(th_ready, 1)

        def tail_on_vector(dve, ib):
            TAIL = 11
            count = [0]

            def link(ins):
                count[0] += 1
                ins.then_inc(tail_step, 1)
                dve.wait_ge(tail_step, ib * TAIL + count[0])

            dve.wait_ge(squares_ready, ib + 1)
            link(dve.reduce_sum(norm2[:, :, :], squares[:, :, :, :], axis=AX.X))
            dve.tensor_scalar(norm2[:, :, :], norm2[:, :, :], TINY, None, ALU.max).then_inc(norm2_ready, 1)
            dve.wait_ge(y0_ready, ib + 1)
            link(dve.tensor_scalar(y0[:, :, :], y0[:, :, :], ROOT_SCALE ** 0.5, None, ALU.mult))
            rsqrt_newton(dve, link, rs[:, :, :], y0[:, :, :], norm2[:, :, :], tmp[:, :, :], 1.0)
            link(dve.tensor_tensor(norm[:, :, :], norm2[:, :, :], rs[:, :, :], ALU.mult))
            link(dve.tensor_scalar(tmp[:, 0, :], rs[:, 0, :], ATANH_MAX, 1.0, ALU.mult, ALU.min))
            dve.tensor_tensor(arg[:, :], norm[:, 1, :], tmp[:, 0, :], ALU.mult).then_inc(arg_ready, 1)
            dve.wait_ge(th_ready, ib + 1)
            link(dve.tensor_scalar(coef[:, :], coef[:, :], MAXNORM, None, ALU.min))
            link(dve.tensor_tensor(coef[:, :], coef[:, :], rs[:, 1, :], ALU.mult))
            link(dve.tensor_tensor(relu[:, :, :], relu[:, :, :], coef[:, :].unsqueeze(2).to_broadcast([P, BT, D]), ALU.mult))
            assert count[0] == TAIL
            rows = m.x[:, bass.ds(ib * BT, BT), :]
            dve.tensor_tensor(rows, rows, relu[:, :, :], ALU.add).then_inc(x_ready, 1)

        @block.sync
        def _(sp):
            with sp.Fori(0, NB) as ib:
                for k in range(4):
                    sp.wait_ge(bits_used, ib * 4 + (k + 1))
                    sp.dma_start(bits[:, k, :].bitcast(BF16),
                                 m.adj8[bass.ds(ib, 1), :, k * KQ // 2:(k + 1) * KQ // 2].rearrange("b p n -> (b p) n")
                                 ).then_inc(bits_in[k], 16)

        @block.tensor
        def _(pe):
            pe.sem_inc(bits_used, 4)
            with pe.Fori(0, NB // 2) as pair:
                for par in range(2):
                    ib = pair * 2 + par
                    pe.wait_ge(acc_free, ib + 1)
                    for k in range(4):
                        pe.wait_ge(bits_in[k], ib * 16 + 16)
                        pe.nop(nofuse=True)
                        for j in range(QT):
                            if counting and (k * QT + j) % GT == 0:
                                pe.wait_ge(halves_ready, (k * QT + j) // GT + 1)
                            for it in range(BT):
                                mm = pe.matmul(m.acc[2 * par + it // 2][:, it % 2, 0:width],
                                               bits[:, k, j * W + it * P:j * W + (it + 1) * P],
                                               m.hh[:, k * QT + j, 0:width],
                                               start=(k + j == 0), stop=(k == 3 and j == QT - 1))
                        mm.then_inc(bits_used, 1)

        @block.scalar
        def _(act):
            if counting:
                norm_on_scalar(act)
            with act.Fori(0, NB // 2) as pair:
                for par in range(2):
                    ib = pair * 2 + par
                    act.wait_ge(bits_used, ib * 4 + 8)
                    act.wait_ge(acc_free, ib + 1)
                    for b in range(2):
                        act.activation(low[:, 2 * par + b, :, :], m.acc[2 * par + b][:, :, D:2 * D], ACT.Copy).then_inc(low_ready, 1)
                    if not counting:
                        tail_on_scalar(act, ib)

        @block.vector
        def _(dve):
            dve.sem_inc(acc_free, 2)
            if counting:
                norm_on_vector(dve)
            else:
                dve.sem_inc(x_ready, 1)
            with dve.Fori(0, NB // 2) as pair:
                for par in range(2):
                    ib = pair * 2 + par
                    for b in range(2):
                        dve.wait_ge(low_ready, ib * 2 + (b + 1))
                        to = m.agg[:, bass.ds(ib * BT + 2 * b, 2), :] if counting else s_blk[:, 2 * b:2 * b + 2, :]
                        last = dve.tensor_tensor(to, m.acc[2 * par + b][:, :, 0:D], low[:, 2 * par + b, :, :], ALU.add)
                        if counting:
                            last = dve.tensor_copy(m.cnt1[:, bass.ds(ib * BT + 2 * b, 2)],
                                                   m.acc[2 * par + b][:, :, 2 * D])
                    last.then_inc(acc_free, 1)
                    if not counting:
                        tail_on_vector(dve, ib)


def after_l0(nc, m, a, tag):
    with ExitStack() as ctx:
        sem = lambda name: ctx.enter_context(nc.semaphore(name))
        h0 = ctx.enter_context(nc.sbuf_tensor(f"h0_{tag}", [P, T, D], FP32))
        r = ctx.enter_context(nc.sbuf_tensor(f"l0_r_{tag}", [P, T], FP32))
        h0_in, step = sem("h0_in"), sem("l0_step")
        block = ctx.enter_context(nc.Block())

        @block.sync
        def _(sp):
            sp.dma_start(h0[:, :, :], a["L0_gnn_h0"].rearrange("p (t d) -> p t d", d=D)).then_inc(h0_in, 16)

        @block.vector
        def _(dve):
            link = chain(dve, step)
            link(dve.tensor_scalar(r[:, :], m.rows[:, :], L1_FLOOR, None, ALU.max))
            link(dve.reciprocal(r[:, :], r[:, :]))
            link(dve.tensor_scalar(r[:, :], r[:, :], 0.9 / HS, None, ALU.mult))
            link(dve.tensor_tensor(m.agg[:, :, :], m.agg[:, :, :], r[:, :].unsqueeze(2).to_broadcast([P, T, D]), ALU.mult))
            link(dve.tensor_tensor(m.x[:, :, :], m.x[:, :, :], m.agg[:, :, :], ALU.add))
            dve.wait_ge(h0_in, 16)
            link(dve.scalar_tensor_tensor(out=m.x[:, :, :], in0=h0[:, :, :], scalar=0.1, in1=m.x[:, :, :],
                                          op0=ALU.mult, op1=ALU.add))


RG = 8
PE_LAG = 3


def mamba(nc, m, a, agg_scale, tag):
    with ExitStack() as ctx:
        def sem(name):
            return ctx.enter_context(nc.semaphore(f"{name}_{tag}"))

        def sb(name, shape, dt=FP32):
            return ctx.enter_context(nc.sbuf_tensor(f"{name}_{tag}", shape, dt))

        gcn_w, gcn_b = sb("gcn_w", [P, D]), sb("gcn_b", [P, D])
        ln_g, ln_b = sb("ln_g", [P, 1]), sb("ln_b", [P, 1])
        w_in = sb("w_in", [P, 2 * INNER])
        conv_w, conv_b = sb("conv_w", [P, 2 * TAPS]), sb("conv_b", [P, 2])
        w_cb, w_r, w_dt, b_dt = sb("w_cb", [P, 2 * 96]), sb("w_r", [P, 2 * RANK]), sb("w_dt", [RANK, INNER]), sb("b_dt", [P, 2])
        decay, skip, w_out = sb("decay", [P, UN]), sb("skip", [P, 2]), sb("w_out", [P, 2 * D])
        pick = sb("pick", [96, ST * P], BF16)

        s_blk = g_act = sb("by_node", [P, BT, D])
        s_t = h_t = sb("transposed", [P, W])
        stats, mv = sb("stats", [P, BT, 6]), sb("mv", [P, BT, 2])
        var, lnv, y0, tmp, rstd, shift = (sb(s, [P, BT]) for s in ("var", "lnv", "y0", "tmp", "rstd", "shift"))
        xc, cv = sb("xc", [P, 2, W + TAPS]), sb("cv", [P, 2, W])
        zs, us, dts, dtu = (sb(s, [P, 2, 2, W]) for s in ("zs", "us", "dts", "dtu"))
        c_parts, bc = sb("c_parts", [96, 2, W], BF16), sb("bc", [96, W])
        dtr, soft, lin = sb("dtr", [RANK, W]), sb("soft", [P, 2, W]), sb("lin", [P, 2, W])
        bbc = sb("bbc", [P, 4, 2, W])
        da, bx, hs, ps = sb("da", [P, RG, W]), sb("bx", [P, RG, W]), sb("hs", [P, RG, W]), sb("ps", [P, 4, W])
        yg = sb("yg", [P, 2, W])
        state = sb("state", [P, UN])

        c_bank, y_bank, misc, out_bank = m.acc[0:2], m.acc[2], m.acc[3][:, 0, :], m.acc[3][:, 1, :]

        consts_in, pick0, decay_ready, zeroed = sem("consts_in"), sem("pick0"), sem("decay_ready"), sem("zeroed")
        a_ready, bx_ready, c_ready, scan_done = sem("a_ready"), sem("bx_ready"), sem("c_ready"), sem("scan_done")
        p_ready, p_used, state_saved, y_read, gated = sem("p_ready"), sem("p_used"), sem("state_saved"), sem("y_read"), sem("gated")
        misc_full, misc_free = sem("misc_full"), sem("misc_free")
        s_ready, var_ready, y0_ready, ln_step, hn_ready = sem("s_ready"), sem("var_ready"), sem("y0_ready"), sem("ln_step"), sem("hn_ready")
        halo, conv_step, u_ready, b_ready, c_step, c_sub = sem("halo"), sem("conv_step"), sem("u_ready"), sem("b_ready"), sem("c_step"), sem("c_sub")
        soft_step, dt_ready, out_full, out_free = sem("soft_step"), sem("dt_ready"), sem("out_full"), sem("out_free")
        b_out, bbc_in = sem("b_out"), [sem(f"bbc_in{k}") for k in range(4)]
        block = ctx.enter_context(nc.Block())

        def front_use(f, j):
            return 11 * f + (j + 1)

        def chunks(eng, body):
            body(0, 0, True, False)
            with eng.Fori(0, (NB - 2) // 2) as two:
                body(two * 2 + 1, 1, True, True)
                body(two * 2 + 2, 0, True, True)
            body(NB - 1, 1, False, True)

        WEIGHTS = [(gcn_w, "L1_gnn_gcn_w"), (gcn_b, "L1_gnn_gcn_b"), (ln_g, "L1_gnn_ln_g"), (ln_b, "L1_gnn_ln_b"),
                   (w_in, "L1_gnn_w_in"), (conv_w, "L1_gnn_conv_w"), (conv_b, "L1_gnn_conv_b"), (w_cb, "w_cb"),
                   (w_r, "w_r"), (w_dt, "L1_gnn_w_dt"), (b_dt, "L1_gnn_b_dt"), (decay, "L1_gnn_A_log"),
                   (skip, "L1_gnn_D_skip"), (w_out, "L1_gnn_w_out")]
        ALL_IN = 16 * len(WEIGHTS)

        @block.sync
        def _(sp):
            for tile, name in WEIGHTS:
                sp.dma_start(tile[:, :], a[name]).then_inc(consts_in, 16)

            def b_store(f, q):
                sp.wait_ge(b_ready, f + 1)
                sp.dma_start(m.b_rows[q:q + 1, :].rearrange("a (s w) -> (a s) w", w=W),
                             bc[ST:2 * ST, :]).then_inc(b_out, 16)
                sp.wait_ge(b_out, f * 16 + 16)
                sp.nop(nofuse=True)

            def body(c, q, front, back):
                for g in range(UN // 2):
                    sp.wait_ge(bx_ready, c * UN + (2 * g + 2))
                    sp.dma_start(bbc[:, g % 4, :, :],
                                 m.b_rows[q, (g % 8) * 2 * W:(g % 8 + 1) * 2 * W].rearrange("(s w) -> s w", w=W)
                                 .partition_broadcast(P)).then_inc(bbc_in[g % 4], 16)
                if front:
                    b_store(c + 1, 1 - q)

            b_store(0, 0)
            chunks(sp, body)

        @block.gpsimd
        def _(pool):
            pool.sem_inc(bx_ready, 8)
            pool.memset(pick[:, :], 0.0).then_inc(pick0, 1)
            rows = pick[:, :].rearrange("k (n p) -> k n p", p=P)
            for part in range(3):
                pool.wait_ge(pick0, part + 1)
                pool.affine_select(out=rows, in_=rows, compare_op=ALU.not_equal, fill=1.0, base=-32 * part,
                                   pattern=[[-1, ST], [0, P]], channel_multiplier=1).then_inc(pick0, 1)
            pool.memset(state[:, :], 0.0).then_inc(zeroed, 1)
            pool.memset(xc[:, :, 0:TAPS - 1], 0.0).then_inc(zeroed, 1)

            def dt_half(f, q, h):
                pool.wait_ge(soft_step, 5 * f + 5)
                pool.tensor_tensor(dts[:, q, h, :], soft[:, h, :], lin[:, h, :], ALU.add).then_inc(dt_ready, 1)
                pool.wait_ge(dt_ready, 4 * f + (2 * h + 1))
                pool.tensor_tensor(dtu[:, q, h, :], dts[:, q, h, :], us[:, q, h, :], ALU.mult).then_inc(dt_ready, 1)

            def body(c, q, front, back):
                for u in range(UN):
                    if u % 2 == 0:
                        pool.wait_ge(bbc_in[u // 2 % 4], (c * 4 + (u // 8 + 1)) * 16)
                    if u % ST == 0:
                        pool.wait_ge(dt_ready, 4 * c + (2 * (u // ST) + 2))
                    pool.wait_ge(scan_done, c * UN + (u + 1))
                    pool.tensor_tensor(bx[:, u % RG, :], dtu[:, q, u // ST, :], bbc[:, u // 2 % 4, u % 2, :],
                                       ALU.mult).then_inc(bx_ready, 1)
                    if u == 4:
                        dt_half(c, q, 1)
                    if front and u == 30:
                        pool.wait_ge(scan_done, c * UN + 8)
                        dt_half(c + 1, 1 - q, 0)

            dt_half(0, 0, 0)
            chunks(pool, body)

        @block.scalar
        def _(act):
            act.wait_ge(consts_in, ALL_IN)
            act.activation(decay[:, :], decay[:, :], ACT.Exp).then_inc(decay_ready, 1)
            act.wait_ge(decay_ready, 1)
            act.activation(decay[:, :], decay[:, :], ACT.Copy, scale=-1.0).then_inc(decay_ready, 1)
            act.wait_ge(decay_ready, 2)

            def take_agg(f):
                act.activation(s_blk[:, :, :], m.agg[:, f * BT:(f + 1) * BT, :] if isinstance(f, int)
                               else m.agg[:, bass.ds(f * BT, BT), :], ACT.Copy, scale=agg_scale).then_inc(s_ready, 1)

            def take_s_t(f):
                act.wait_ge(misc_full, front_use(f, 1))
                act.activation(s_t[:, :], misc, ACT.Copy).then_inc(misc_free, 1)

            def var_root(f):
                act.wait_ge(var_ready, f + 1)
                act.activation(lnv[:, :], var[:, :], ACT.Ln).then_inc(y0_ready, 1)
                act.wait_ge(y0_ready, 2 * f + 1)
                act.activation(y0[:, :], lnv[:, :], ACT.Exp, scale=-0.5).then_inc(y0_ready, 1)

            def take_h_t(f):
                act.wait_ge(misc_full, front_use(f, 3))
                act.activation(h_t[:, :], misc, ACT.Identity, scale=ln_g[:, :], bias=ln_b[:, :]).then_inc(misc_free, 1)
                if isinstance(f, int) and f == 0:
                    act.wait_ge(zeroed, 2)
                    act.sem_inc(halo, 1)
                else:
                    act.wait_ge(conv_step, 8 * f)
                    act.activation(xc[:, :, 0:TAPS - 1], xc[:, :, W:W + TAPS - 1], ACT.Copy).then_inc(halo, 1)

            def take_xc(f, h):
                act.wait_ge(misc_full, front_use(f, 4 + h))
                act.wait_ge(halo, f + 1)
                act.activation(xc[:, h, TAPS - 1:W + TAPS - 1], misc, ACT.Copy).then_inc(misc_free, 1)

            def take_z(f, q, h):
                if not (isinstance(f, int) and f < 2):
                    act.wait_ge(gated, 2 * f - 2)
                act.wait_ge(misc_full, front_use(f, 6 + h))
                act.activation(zs[:, q, h, :], misc, ACT.Copy).then_inc(misc_free, 1)

            def silus(f, q):
                act.wait_ge(misc_free, front_use(f, 7))
                act.activation(zs[:, q, :, :], zs[:, q, :, :], ACT.Silu)
                act.wait_ge(conv_step, 8 * f + 8)
                act.activation(us[:, q, :, :], cv[:, :, :], ACT.Silu).then_inc(u_ready, 1)

            def take_bc(f, q):
                act.wait_ge(misc_full, front_use(f, 8))
                if not (isinstance(f, int) and f == 0):
                    act.wait_ge(b_out, f * 16)
                act.activation(bc[:, :], misc[0:96, :], ACT.Copy).then_inc(b_ready, 1)
                act.activation(c_parts[:, q, :], misc[0:96, :], ACT.Copy).then_inc(c_step, 1)
                act.wait_ge(c_step, 3 * f + 1)
                act.sem_inc(misc_free, 1)

            def second_c(f, q):
                act.wait_ge(c_sub, 2 * f + 1)
                act.activation(c_parts[32:64, q, :], bc[32:64, :], ACT.Copy)
                act.activation(c_parts[64:96, q, :], bc[64:96, :], ACT.Copy).then_inc(c_step, 1)

            def third_c(f, q):
                act.wait_ge(c_sub, 2 * f + 2)
                act.activation(c_parts[64:96, q, :], bc[64:96, :], ACT.Copy).then_inc(c_step, 1)

            def take_dtr(f):
                act.wait_ge(misc_full, front_use(f, 9))
                act.activation(dtr[:, :], misc[0:RANK, :], ACT.Copy).then_inc(misc_free, 1)

            def softplus(f, h):
                act.wait_ge(misc_full, front_use(f, 10 + h))
                if not (isinstance(f, int) and f == 0):
                    act.wait_ge(dt_ready, 4 * f)
                act.activation(soft[:, h, :], misc, ACT.Abs, bias=b_dt[:, h:h + 1]).then_inc(soft_step, 1)
                act.activation(lin[:, h, :], misc, ACT.Relu, bias=b_dt[:, h:h + 1]).then_inc(misc_free, 1)
                act.wait_ge(soft_step, 5 * f + (2 * h + 1))
                act.activation(soft[:, h, :], soft[:, h, :], ACT.Exp, scale=-1.0).then_inc(soft_step, 1)
                if h == 1:
                    act.wait_ge(soft_step, 5 * f + 4)
                    act.activation(soft[:, :, :], soft[:, :, :], ACT.Ln, bias=1.0).then_inc(soft_step, 1)

            def front_step(f, q, u):
                if u == 0:
                    take_agg(f)
                if u == 2:
                    take_s_t(f)
                if u == 7:
                    var_root(f)
                if u == 10:
                    take_h_t(f)
                if u in (11, 13):
                    take_xc(f, (u - 11) // 2)
                if u in (15, 17):
                    take_z(f, q, (u - 15) // 2)
                if u == 17:
                    silus(f, q)
                if u == 20:
                    take_bc(f, q)
                if u == 21:
                    take_dtr(f)
                if u == 23:
                    second_c(f, q)
                if u in (23, 25):
                    softplus(f, (u - 23) // 2)
                if u == 26:
                    third_c(f, q)

            def body(c, q, front, back):
                for u in range(UN):
                    if u % ST == 0:
                        act.wait_ge(dt_ready, 4 * c + (2 * (u // ST) + 2))
                    act.wait_ge(scan_done, c * UN + (u + 1))
                    act.activation(da[:, u % RG, :], dts[:, q, u // ST, :], ACT.Exp,
                                   scale=decay[:, u:u + 1]).then_inc(a_ready, 1)
                    if front:
                        front_step(c + 1, 1 - q, u)

            for u in range(UN):
                front_step(0, 0, u)
            chunks(act, body)

        @block.vector
        def _(dve):
            dve.sem_inc(scan_done, 8)
            dve.sem_inc(state_saved, UN // 4)
            dve.sem_inc(p_ready, 8)
            dve.sem_inc(y_read, 2)
            dve.sem_inc(out_free, 1)
            dve.sem_inc(misc_free, 1)
            dve.wait_ge(consts_in, ALL_IN)
            dve.wait_ge(zeroed, 2)

            def scan(c, u):
                dve.wait_ge(a_ready, c * UN + (u + 1))
                dve.wait_ge(bx_ready, c * UN + (u + 9))
                dve.wait_ge(p_ready, c * UN + (u + 1))
                dve.wait_ge(state_saved, c * (UN // 4) + (u // 4 + 7))
                dve.tensor_tensor_scan(hs[:, u % RG, :], da[:, u % RG, :], bx[:, u % RG, :], state[:, u:u + 1],
                                       ALU.mult, ALU.add).then_inc(scan_done, 1)

            def save_states(c, g):
                dve.wait_ge(scan_done, c * UN + (4 * g + 12))
                at = 4 * g % RG
                dve.tensor_copy(state[:, 4 * g:4 * g + 4], hs[:, at:at + 4, W - 1]).then_inc(state_saved, 1)

            def times_c(c, u):
                dve.wait_ge(c_ready, c * UN + (u + 1))
                dve.wait_ge(p_used, c * UN + (u + 1))
                dve.wait_ge(scan_done, c * UN + (u + 9))
                dve.tensor_tensor(ps[:, u % 4, :], hs[:, u % RG, :], c_bank[u // 2 % 2][:, u % 2, :], ALU.mult).then_inc(p_ready, 1)

            def gate(c, q, h):
                dve.wait_ge(p_used, c * UN + (ST * (h + 1) + 4))
                if h == 0 and not (isinstance(c, int) and c == 0):
                    dve.wait_ge(out_full, c)
                dve.scalar_tensor_tensor(out=yg[:, h, :], in0=us[:, q, h, :], scalar=skip[:, h:h + 1], in1=y_bank[:, h, :],
                                         op0=ALU.mult, op1=ALU.add).then_inc(y_read, 1)
                dve.wait_ge(y_read, 2 * c + (h + 3))
                dve.tensor_tensor(yg[:, h, :], yg[:, h, :], zs[:, q, h, :], ALU.mult).then_inc(gated, 1)

            def add_out(c):
                dve.wait_ge(out_full, c + 1)
                at = m.x[:, c * BT:(c + 1) * BT, :] if isinstance(c, int) else m.x[:, bass.ds(c * BT, BT), :]
                dve.tensor_tensor(at, at, out_bank.rearrange("p (t d) -> p t d", d=D), ALU.add).then_inc(out_free, 1)

            def gcn_stats(f):
                n = 14 * f
                dve.wait_ge(misc_full, front_use(f, 2))
                if not (isinstance(f, int) and f == 0):
                    dve.wait_ge(hn_ready, f)
                dve.tensor_tensor(g_act[:, :, :], misc.rearrange("p (t d) -> p t d", d=D),
                                  gcn_b[:, :].unsqueeze(1).to_broadcast([P, BT, D]), ALU.add).then_inc(misc_free, 1)
                dve.wait_ge(misc_free, front_use(f, 2))
                dve.tensor_scalar(g_act[:, :, :], g_act[:, :, :], 0.0, None, ALU.max).then_inc(ln_step, 1)
                dve.wait_ge(ln_step, n + 1)
                for t in range(BT):
                    dve.bn_stats(stats[:, t, :], g_act[:, t, :]).then_inc(ln_step, 1)
                dve.wait_ge(ln_step, n + 5)
                dve.nop(nofuse=True)
                for t in range(BT):
                    dve.bn_aggr(mv[:, t, :], stats[:, t, :]).then_inc(ln_step, 1)
                dve.wait_ge(ln_step, n + 9)
                dve.tensor_scalar(var[:, :], mv[:, :, 1], LN_EPS, None, ALU.add).then_inc(var_ready, 1)

            def normalize(f):
                n = 14 * f + 9
                dve.wait_ge(y0_ready, 2 * f + 2)
                dve.tensor_tensor(tmp[:, :], y0[:, :], y0[:, :], ALU.mult).then_inc(ln_step, 1)
                dve.wait_ge(ln_step, n + 1)
                dve.tensor_tensor(tmp[:, :], tmp[:, :], var[:, :], ALU.mult).then_inc(ln_step, 1)
                dve.wait_ge(ln_step, n + 2)
                dve.tensor_scalar(tmp[:, :], tmp[:, :], -0.5, 1.5, ALU.mult, ALU.add).then_inc(ln_step, 1)
                dve.wait_ge(ln_step, n + 3)
                dve.tensor_tensor(rstd[:, :], tmp[:, :], y0[:, :], ALU.mult).then_inc(ln_step, 1)
                dve.wait_ge(ln_step, n + 4)
                dve.scalar_tensor_tensor(out=shift[:, :], in0=mv[:, :, 0], scalar=-1.0, in1=rstd[:, :],
                                         op0=ALU.mult, op1=ALU.mult).then_inc(ln_step, 1)
                dve.wait_ge(ln_step, n + 5)
                for t in range(BT):
                    last = dve.tensor_scalar(g_act[:, t, :], g_act[:, t, :], rstd[:, t:t + 1], shift[:, t:t + 1],
                                             ALU.mult, ALU.add)
                last.then_inc(hn_ready, 1)

            def convolve(f, h, part):
                n = 8 * f + 4 * h
                if part == 0:
                    dve.wait_ge(misc_free, front_use(f, 4 + h))
                    if not (isinstance(f, int) and f == 0):
                        dve.wait_ge(u_ready, f)
                    dve.tensor_scalar(cv[:, h, :], xc[:, h, 0:W], conv_w[:, TAPS * h:TAPS * h + 1], conv_b[:, h:h + 1],
                                      ALU.mult, ALU.add).then_inc(conv_step, 1)
                for k in ((1,), (2, 3))[part]:
                    dve.wait_ge(conv_step, n + k)
                    dve.scalar_tensor_tensor(out=cv[:, h, :], in0=xc[:, h, k:k + W],
                                             scalar=conv_w[:, TAPS * h + k:TAPS * h + k + 1], in1=cv[:, h, :],
                                             op0=ALU.mult, op1=ALU.add).then_inc(conv_step, 1)

            def c_minus_first(f, q):
                dve.wait_ge(c_step, 3 * f + 1)
                dve.tensor_tensor(bc[32:64, :], bc[32:64, :], c_parts[32:64, q, :], ALU.subtract)
                dve.tensor_tensor(bc[64:96, :], bc[64:96, :], c_parts[64:96, q, :], ALU.subtract).then_inc(c_sub, 1)

            def c_minus_second(f, q):
                dve.wait_ge(c_step, 3 * f + 2)
                dve.tensor_tensor(bc[64:96, :], bc[64:96, :], c_parts[64:96, q, :], ALU.subtract).then_inc(c_sub, 1)

            def front_step(f, q, u):
                if u == 2:
                    gcn_stats(f)
                if u == 4:
                    normalize(f)
                if u in (9, 10, 11, 12):
                    convolve(f, (u - 9) // 2, (u - 9) % 2)
                if u == 18:
                    c_minus_first(f, q)
                if u == 21:
                    c_minus_second(f, q)

            def body(c, q, front, back):
                for u in range(UN):
                    scan(c, u)
                    if u:
                        times_c(c, u - 1)
                    if u % 4 == 0 and u:
                        save_states(c, u // 4 - 1)
                    if back and u == 4:
                        gate(c - 1, 1 - q, 1)
                    if back and u == 9:
                        add_out(c - 1)
                    if u == ST + 4:
                        gate(c, q, 0)
                    if front:
                        front_step(c + 1, 1 - q, u)
                times_c(c, UN - 1)
                save_states(c, UN // 4 - 1)

            for u in range(UN):
                front_step(0, 0, u)
            chunks(dve, body)
            gate(NB - 1, 1, 1)
            add_out(NB - 1)

        @block.tensor
        def _(pe):
            pe.sem_inc(misc_full, 1)
            pe.sem_inc(p_used, 4)
            pe.wait_ge(consts_in, ALL_IN)
            pe.wait_ge(pick0, 4)

            def take_misc(use):
                pe.wait_ge(misc_free, use - 1)

            def transposes(f, use, src):
                take_misc(use)
                for t in range(BT):
                    mm = pe.transpose(misc[:, t * P:(t + 1) * P], src[:, t, :], m.ident[:, :])
                mm.then_inc(misc_full, 1)

            def front_step(f, q, u):
                if u == 1:
                    pe.wait_ge(s_ready, f + 1)
                    transposes(f, front_use(f, 1), s_blk)
                if u == 3:
                    take_misc(front_use(f, 2))
                    for t in range(BT):
                        mm = pe.matmul(misc[:, t * P:(t + 1) * P], s_t[:, t * P:(t + 1) * P], gcn_w[:, :], start=True, stop=True)
                    mm.then_inc(misc_full, 1)
                if u == 7:
                    pe.wait_ge(hn_ready, f + 1)
                    transposes(f, front_use(f, 3), g_act)
                if u in (8, 10, 12, 14):
                    j = (u - 8) // 2
                    take_misc(front_use(f, 4 + j))
                    pe.matmul(misc, w_in[:, j * P:(j + 1) * P], h_t[:, :], start=True, stop=True).then_inc(misc_full, 1)
                if u in (17, 18):
                    j, w, k = (8, w_cb, 96) if u == 17 else (9, w_r, RANK)
                    take_misc(front_use(f, j))
                    pe.wait_ge(u_ready, f + 1)
                    for h in range(2):
                        mm = pe.matmul(misc[0:k, :], w[:, h * k:(h + 1) * k], us[:, q, h, :], start=(h == 0), stop=(h == 1))
                    mm.then_inc(misc_full, 1)
                if u in (20, 22):
                    h = (u - 20) // 2
                    take_misc(front_use(f, 10 + h))
                    pe.matmul(misc, w_dt[:, h * P:(h + 1) * P], dtr[:, :], start=True, stop=True).then_inc(misc_full, 1)

            def spread_c(c, q, u):
                if u == 0:
                    pe.wait_ge(c_step, 3 * c + 3)
                pe.wait_ge(p_ready, c * UN + (u + 5))
                n = u % ST
                pe.matmul(c_bank[u // 2 % 2][:, u % 2, :], pick[:, n * P:(n + 1) * P], c_parts[:, q, :],
                          start=True, stop=True).then_inc(c_ready, 1)

            def add_state(c, u):
                n, h = u % ST, u // ST
                pe.wait_ge(p_ready, c * UN + (u + 9))
                if n == 0:
                    pe.wait_ge(y_read, 2 * c + (h + 1))
                pe.matmul(y_bank[:, h, :], m.ident[:, :], ps[:, u % 4, :], start=(n == 0), stop=(n == ST - 1)).then_inc(p_used, 1)

            def output(c):
                pe.wait_ge(out_free, c + 1)
                pe.wait_ge(gated, 2 * c + 2)
                for t in range(BT):
                    for h in range(2):
                        mm = pe.matmul(out_bank[:, t * P:(t + 1) * P], yg[:, h, t * P:(t + 1) * P], w_out[:, h * D:(h + 1) * D],
                                       start=(h == 0), stop=(h == 1))
                mm.then_inc(out_full, 1)

            def body(c, q, front, back):
                for u in range(UN):
                    spread_c(c, q, u)
                    if u >= PE_LAG:
                        add_state(c, u - PE_LAG)
                    elif back:
                        add_state(c - 1, UN + u - PE_LAG)
                    if back and u == 9:
                        output(c - 1)
                    if front:
                        front_step(c + 1, 1 - q, u)

            for u in range(UN):
                front_step(0, 0, u)
            chunks(pe, body)
            for u in range(UN - PE_LAG, UN):
                add_state(NB - 1, u)
            output(NB - 1)



def hyperbolic_in(nc, m, a, tag):
    with ExitStack() as ctx:
        sem = lambda name: ctx.enter_context(nc.semaphore(f"{name}_{tag}"))
        sb = lambda name, shape: ctx.enter_context(nc.sbuf_tensor(f"{name}_{tag}", shape, FP32))
        names = ("xn2", "mn2", "dot", "hn2", "lnv", "y0", "tmp", "rs_x", "n_x", "rs_m", "n_m", "at_x", "at_h", "rs_h",
                 "n_h", "lp", "lm", "sq", "poly", "mask", "arg", "th", "alpha", "x2", "xy", "num_a", "num_b", "den", "c1", "c2", "coef")
        s = {n: sb(f"l2_{n}", [P, T]) for n in names}
        big = sb("l2_big", [P, T, D])
        w_t, bias = sb("l2_w", [P, D]), sb("l2_bias", [P, D])
        b_sq = sb("l2_bsq", [P, D])
        b1 = {n: sb(f"l2b_{n}", [P, 1]) for n in ("n2", "lnv", "y0", "tmp", "rs", "n", "th", "beta", "y2")}
        blk_t = sb("l2_blk_t", [P, 2, W])
        w_in_, step, for_act, for_dve = sem("l2_w_in"), sem("l2_step"), sem("l2_for_act"), sem("l2_for_dve")
        t_full, t_free, mx_full, mx_free = sem("t_full"), sem("t_free"), sem("mx_full"), sem("mx_free")
        block = ctx.enter_context(nc.Block())
        S = lambda n: s[n][:, :]
        B = lambda n: b1[n][:, :]
        wide = lambda ap: ap.unsqueeze(2).to_broadcast([P, T, D])
        bias_w = bias[:, :].unsqueeze(1).to_broadcast([P, T, D])

        @block.sync
        def _(sp):
            sp.dma_start(w_t[:, :], a["L2_gnn_weight"]).then_inc(w_in_, 16)
            sp.dma_start(bias[:, :], a["L2_gnn_bias"]).then_inc(w_in_, 16)

        @block.tensor
        def _(pe):
            pe.wait_ge(w_in_, 32)

            def transposes(ib):
                if ib >= 2:
                    pe.wait_ge(t_free, ib - 1)
                for t in range(BT):
                    mm = pe.transpose(m.acc[0][:, ib % 2, t * P:(t + 1) * P], m.agg[:, ib * BT + t, :], m.ident[:, :])
                mm.then_inc(t_full, 1)

            transposes(0)
            for ib in range(NB):
                r = ib % 2
                if ib + 1 < NB:
                    transposes(ib + 1)
                pe.wait_ge(t_free, ib + 1)
                if ib >= 2:
                    pe.wait_ge(mx_free, ib - 1)
                for t in range(BT):
                    mm = pe.matmul(m.acc[1][:, r, t * P:(t + 1) * P], blk_t[:, r, t * P:(t + 1) * P], w_t[:, :], start=True, stop=True)
                mm.then_inc(mx_full, 1)

        @block.scalar
        def _(act):
            act.activation(big[:, :, :], m.agg[:, :, :], ACT.Square, scale=1.0 / HS).then_inc(for_dve, 1)
            for ib in range(NB):
                act.wait_ge(t_full, ib + 1)
                if ib >= 2:
                    act.wait_ge(mx_full, ib - 1)
                act.activation(blk_t[:, ib % 2, :], m.acc[0][:, ib % 2, :], ACT.Copy, scale=1.0 / HS).then_inc(t_free, 1)
            turn = [0]

            def take(n=1):
                turn[0] += n
                act.wait_ge(for_act, turn[0])

            done = [1]

            def give(ins):
                done[0] += 1
                ins.then_inc(for_dve, 1)
                act.wait_ge(for_dve, done[0])

            take()
            act.wait_ge(mx_free, NB)
            give(act.activation(big[:, :, :], m.agg[:, :, :], ACT.Square))
            for v, lnv, y0 in ((S("xn2"), S("lnv"), S("y0")), (S("mn2"), S("lnv"), S("y0")), (B("n2"), B("lnv"), B("y0"))):
                take()
                give(act.activation(lnv, v, ACT.Ln, scale=ROOT_SCALE))
                give(act.activation(y0, lnv, ACT.Exp, scale=-0.5))
            take()
            give(act.activation(S("lp"), S("n_x"), ACT.Ln, bias=1.0))
            give(act.activation(S("lm"), S("n_x"), ACT.Ln, scale=-1.0, bias=1.0))
            take()
            give(act.activation(S("th"), S("arg"), ACT.Tanh))
            give(act.activation(B("th"), B("n"), ACT.Tanh))
            take()
            give(act.activation(big[:, :, :], m.agg[:, :, :], ACT.Square))
            take()
            give(act.activation(S("lnv"), S("hn2"), ACT.Ln, scale=ROOT_SCALE))
            give(act.activation(S("y0"), S("lnv"), ACT.Exp, scale=-0.5))
            take()
            give(act.activation(S("lp"), S("n_h"), ACT.Ln, bias=1.0))
            give(act.activation(S("lm"), S("n_h"), ACT.Ln, scale=-1.0, bias=1.0))
            take()
            give(act.activation(m.hh[:, :, 0:D], m.agg[:, :, :], ACT.Copy))

        @block.vector
        def _(dve):
            link = chain(dve, step)
            got = [0]

            def hand(ins):
                got[0] += 1
                ins.then_inc(for_act, 1)
                dve.wait_ge(for_act, got[0])

            back = [0]

            def take(n=1):
                back[0] += n
                dve.wait_ge(for_dve, back[0])

            tt = lambda out, x, y, op: link(dve.tensor_tensor(out, x, y, op))
            ts = lambda out, x, s1, op0, s2=None, op1=ALU.bypass: link(dve.tensor_scalar(out, x, s1, s2, op0, op1)
                                                                      if s2 is not None else dve.tensor_scalar(out, x, s1, None, op0))

            def root(v, y0, tmp, rs, n):
                hand(dve.tensor_scalar(v, v, TINY, None, ALU.max))
                take(2)
                ts(y0, y0, ROOT_SCALE ** 0.5, ALU.mult)
                rsqrt_newton(dve, link, rs, y0, v, tmp, 1.0)
                tt(n, v, rs, ALU.mult)

            def artanh(n, out):
                take(2)
                tt(out, S("lp"), S("lm"), ALU.subtract)
                ts(out, out, 0.5, ALU.mult)
                tt(S("sq"), n, n, ALU.mult)
                ts(S("poly"), S("sq"), 1 / 15, ALU.mult, 1 / 13, ALU.add)
                for k in (11, 9, 7, 5, 3, 1):
                    tt(S("poly"), S("poly"), S("sq"), ALU.mult)
                    ts(S("poly"), S("poly"), 1 / k, ALU.add)
                tt(S("poly"), S("poly"), n, ALU.mult)
                tt(S("poly"), S("poly"), out, ALU.subtract)
                ts(S("mask"), n, 0.25, ALU.is_lt)
                tt(S("poly"), S("poly"), S("mask"), ALU.mult)
                tt(out, out, S("poly"), ALU.add)

            take()
            for ib in range(NB):
                dve.wait_ge(mx_full, ib + 1)
                dve.tensor_copy(m.agg[:, ib * BT:(ib + 1) * BT, :],
                                m.acc[1][:, ib % 2, :].rearrange("p (t d) -> p t d", d=D)).then_inc(mx_free, 1)
            hand(dve.reduce_sum(S("xn2"), big[:, :, :], axis=AX.X))
            dve.wait_ge(w_in_, 32)
            take()
            link(dve.reduce_sum(S("mn2"), big[:, :, :], axis=AX.X))
            tt(big[:, :, :], m.agg[:, :, :], bias_w, ALU.mult)
            link(dve.reduce_sum(S("dot"), big[:, :, :], axis=AX.X))
            tt(b_sq[:, :], bias[:, :], bias[:, :], ALU.mult)
            link(dve.reduce_sum(B("n2"), b_sq[:, :], axis=AX.X))
            root(S("xn2"), S("y0"), S("tmp"), S("rs_x"), S("n_x"))
            root(S("mn2"), S("y0"), S("tmp"), S("rs_m"), S("n_m"))
            root(B("n2"), B("y0"), B("tmp"), B("rs"), B("n"))
            hand(dve.tensor_scalar(S("n_x"), S("n_x"), 1.0 - 1e-7, None, ALU.min))
            artanh(S("n_x"), S("at_x"))
            tt(S("arg"), S("n_m"), S("rs_x"), ALU.mult)
            hand(dve.tensor_tensor(S("arg"), S("arg"), S("at_x"), ALU.mult))
            take(2)
            ts(S("alpha"), S("th"), MAXNORM, ALU.min)
            tt(S("alpha"), S("alpha"), S("rs_m"), ALU.mult)
            ts(B("beta"), B("th"), MAXNORM, ALU.min)
            tt(B("beta"), B("beta"), B("rs"), ALU.mult)
            tt(B("y2"), B("beta"), B("beta"), ALU.mult)
            tt(B("y2"), B("y2"), B("n2"), ALU.mult)
            tt(S("x2"), S("alpha"), S("alpha"), ALU.mult)
            tt(S("x2"), S("x2"), S("mn2"), ALU.mult)
            tt(S("xy"), S("alpha"), S("dot"), ALU.mult)
            ts(S("xy"), S("xy"), B("beta"), ALU.mult, 2.0, ALU.mult)
            ts(S("num_a"), S("xy"), B("y2"), ALU.add, 1.0, ALU.add)
            ts(S("num_b"), S("x2"), -1.0, ALU.mult, 1.0, ALU.add)
            ts(S("den"), S("x2"), B("y2"), ALU.mult, 1.0, ALU.add)
            tt(S("den"), S("den"), S("xy"), ALU.add)
            ts(S("den"), S("den"), 1e-15, ALU.max)
            link(dve.reciprocal(S("den"), S("den")))
            tt(S("c1"), S("num_a"), S("alpha"), ALU.mult)
            tt(S("c1"), S("c1"), S("den"), ALU.mult)
            ts(S("c2"), S("num_b"), B("beta"), ALU.mult)
            tt(S("c2"), S("c2"), S("den"), ALU.mult)
            tt(m.agg[:, :, :], m.agg[:, :, :], wide(S("c1")), ALU.mult)
            tt(big[:, :, :], bias_w, wide(S("c2")), ALU.mult)
            hand(dve.tensor_tensor(m.agg[:, :, :], m.agg[:, :, :], big[:, :, :], ALU.add))
            take()
            link(dve.reduce_sum(S("hn2"), big[:, :, :], axis=AX.X))
            root(S("hn2"), S("y0"), S("tmp"), S("rs_h"), S("n_h"))
            hand(dve.tensor_scalar(S("n_h"), S("n_h"), MAXNORM, None, ALU.min))
            artanh(S("n_h"), S("at_h"))
            tt(S("coef"), S("at_h"), S("rs_h"), ALU.mult)
            ts(S("coef"), S("coef"), HS, ALU.mult)
            hand(dve.tensor_tensor(m.agg[:, :, :], m.agg[:, :, :], wide(S("coef")), ALU.mult))
            take()
            link(dve.tensor_tensor(m.hh[:, :, D:2 * D], m.agg[:, :, :], m.hh[:, :, 0:D], ALU.subtract))


def hyperbolic_out(nc, m, scale, tag):
    with ExitStack() as ctx:
        sb = lambda name: ctx.enter_context(nc.sbuf_tensor(f"o_{name}_{tag}", [P, T], FP32))
        sem = lambda name: ctx.enter_context(nc.semaphore(f"{name}_{tag}"))
        v2, r2, lnv, y0, tmp, rs_v, n_v, rs_r, n_r, th = (sb(n) for n in ("v2", "r2", "lnv", "y0", "tmp", "rsv", "nv", "rsr", "nr", "th"))
        big = ctx.enter_context(nc.sbuf_tensor(f"o_big_{tag}", [P, T, D], FP32))
        step, for_act, for_dve = sem("step"), sem("for_act"), sem("for_dve")
        block = ctx.enter_context(nc.Block())

        @block.scalar
        def _(act):
            act.activation(big[:, :, :], m.agg[:, :, :], ACT.Square, scale=scale).then_inc(for_dve, 1)
            act.wait_ge(for_act, 1)
            act.activation(m.agg[:, :, :], m.agg[:, :, :], ACT.Relu, scale=scale).then_inc(for_dve, 1)
            act.wait_ge(for_dve, 2)
            act.activation(big[:, :, :], m.agg[:, :, :], ACT.Square).then_inc(for_dve, 1)
            for k, v in enumerate((v2, r2)):
                act.wait_ge(for_act, 2 + k)
                act.activation(lnv[:, :], v[:, :], ACT.Ln, scale=ROOT_SCALE).then_inc(for_dve, 1)
                act.wait_ge(for_dve, 4 + 2 * k)
                act.activation(y0[:, :], lnv[:, :], ACT.Exp, scale=-0.5).then_inc(for_dve, 1)
            act.wait_ge(for_act, 4)
            act.activation(th[:, :], n_r[:, :], ACT.Tanh).then_inc(for_dve, 1)

        @block.vector
        def _(dve):
            link = chain(dve, step)
            dve.wait_ge(for_dve, 1)
            dve.reduce_sum(v2[:, :], big[:, :, :], axis=AX.X).then_inc(for_act, 1)
            dve.wait_ge(for_dve, 3)
            link(dve.reduce_sum(r2[:, :], big[:, :, :], axis=AX.X))
            for k, (v, rs, n) in enumerate(((v2, rs_v, n_v), (r2, rs_r, n_r))):
                dve.tensor_scalar(v[:, :], v[:, :], TINY, None, ALU.max).then_inc(for_act, 1)
                dve.wait_ge(for_dve, 5 + 2 * k)
                link(dve.tensor_scalar(y0[:, :], y0[:, :], ROOT_SCALE ** 0.5, None, ALU.mult))
                rsqrt_newton(dve, link, rs[:, :], y0[:, :], v[:, :], tmp[:, :], 1.0)
                link(dve.tensor_tensor(n[:, :], v[:, :], rs[:, :], ALU.mult))
            link(dve.tensor_scalar(rs_v[:, :], rs_v[:, :], ATANH_MAX, 1.0, ALU.mult, ALU.min))
            dve.tensor_tensor(n_r[:, :], n_r[:, :], rs_v[:, :], ALU.mult).then_inc(for_act, 1)
            dve.wait_ge(for_dve, 8)
            link(dve.tensor_scalar(th[:, :], th[:, :], MAXNORM, None, ALU.min))
            link(dve.tensor_tensor(th[:, :], th[:, :], rs_r[:, :], ALU.mult))
            link(dve.tensor_tensor(m.agg[:, :, :], m.agg[:, :, :], th[:, :].unsqueeze(2).to_broadcast([P, T, D]), ALU.mult))
            link(dve.tensor_tensor(m.x[:, :, :], m.x[:, :, :], m.agg[:, :, :], ALU.add))


def judge(nc, m):
    with ExitStack() as ctx:
        sb = lambda name, shape: ctx.enter_context(nc.sbuf_tensor(name, shape, FP32))
        sem = lambda name: ctx.enter_context(nc.semaphore(name))
        n1, n0, tot, odd = sb("n_one", [P, NB]), sb("n_nonzero", [P, NB]), sb("tot_row", [1, NB + 1]), sb("odd", [1, 1])
        step, diff_ready, summed = sem("j_step"), sem("diff_ready"), sem("summed")
        block = ctx.enter_context(nc.Block())

        @block.vector
        def _(dve):
            link = chain(dve, step)
            link(dve.reduce_sum(n0[:, :], m.nz[:, :].rearrange("p (b k) -> p b k", k=NCH), axis=AX.X))
            link(dve.reduce_sum(n1[:, :], m.cnt1[:, :].rearrange("p (b k) -> p b k", k=BT), axis=AX.X))
            dve.tensor_tensor(n0[:, :], n0[:, :], n1[:, :], ALU.subtract).then_inc(diff_ready, 1)
            dve.wait_ge(summed, 1)
            link(dve.tensor_copy(tot[:, :], m.acc[0][0:1, 0, 0:NB + 1]))
            link(dve.reduce_sum(odd[:, :], tot[:, :], axis=AX.X))
            link(dve.tensor_scalar(odd[:, :], odd[:, :], 0.5, None, ALU.is_gt))
            link(dve.tensor_copy(m.flag[:, :], odd[:, :]))

        @block.tensor
        def _(pe):
            pe.wait_ge(diff_ready, 1)
            pe.matmul(m.acc[0][0:1, 0, 0:NB], m.ones[:, :], n0[:, :], start=True, stop=True)
            pe.matmul(m.acc[0][0:1, 0, NB:NB + 1], m.ones[0:CLS, :], m.ybad[:, :], start=True, stop=True).then_inc(summed, 1)


def store_x(nc, m, out, tag):
    with ExitStack() as ctx:
        stored = ctx.enter_context(nc.semaphore(f"stored_{tag}"))
        block = ctx.enter_context(nc.Block())

        @block.sync
        def _(sp):
            sp.dma_start(out.rearrange("p (t d) -> p t d", d=D), m.x[:, :, :]).then_inc(stored, 16)
            sp.wait_ge(stored, 16)

MASKED, PLAIN, SENSITIVE = "masked", "plain", "sensitive"


def aggregate_any(nc, m, a, mode, tag):
    KC = CH * W
    with ExitStack() as ctx:
        sem = lambda name: ctx.enter_context(nc.semaphore(f"{name}_{tag}"))
        sb = lambda name, shape: ctx.enter_context(nc.sbuf_tensor(f"{name}_{tag}", shape, FP32))
        src = sb("src", [P, T, D])
        adj = sb("adj_any", [P, 2, KC])
        wts = sb("wts", [P, 2, KC]) if mode != PLAIN else adj
        if mode == MASKED:
            yt, yb, abs_sum, magnitude = (sb("yt_any", [CLS, NP]), sb("yb_any", [CLS, W]), sb("abs_sum", [P, W]),
                                          sb("magnitude", [P, W]))
        if mode == SENSITIVE:
            inv = sb("inv", [P, KC])
        adj_in = [sem(f"adj_in{k}") for k in range(2)]
        y_in, yb_ready, labels_ready, labels_used = sem("y_in"), sem("yb_ready"), sem("labels_ready"), sem("labels_used")
        src_ready, adj_used, wts_ready, wts_used = sem("src_ready"), sem("adj_used"), sem("wts_ready"), sem("wts_used")
        abs_step, acc_free, rows_ready, inv_ready, exp_ready, sens_step = (
            sem("abs_step"), sem("acc_free"), sem("rows_ready"), sem("inv_ready"), sem("exp_ready"), sem("sens_step"))
        block = ctx.enter_context(nc.Block())

        @block.sync
        def _(sp):
            if mode == MASKED:
                sp.dma_start(yt[:, :], a["L0_gnn_y"]).then_inc(y_in, 16)
            with sp.Fori(0, NB) as ib:
                for k in range(NCH):
                    sp.wait_ge(wts_used if mode == PLAIN else adj_used, ib * NCH + (k + 1))
                    sp.dma_start(adj[:, k % 2, :], a["adj"][bass.ds(ib, 1), :, k * KC:(k + 1) * KC]
                                 .rearrange("b p n -> (b p) n")).then_inc(adj_in[k % 2], 16)

        @block.tensor
        def _(pe):
            pe.sem_inc(wts_used, 2)
            pe.wait_ge(src_ready, 1)
            with pe.Fori(0, NB) as ib:
                pe.wait_ge(acc_free, ib + 1)
                for k in range(NCH):
                    if mode == MASKED:
                        if k == 0:
                            pe.wait_ge(yb_ready, ib + 1)
                        for j in range(CH // 2):
                            pe.wait_ge(labels_used, ib * (T // 2) + (k * CH // 2 + j + 1))
                            for s in range(2):
                                t = k * CH + 2 * j + s
                                mm = pe.matmul(m.acc[2 + j][:, s, :], yt[:, t * P:(t + 1) * P], yb[:, :], start=True, stop=True)
                            mm.then_inc(labels_ready, 1)
                    if mode == PLAIN:
                        pe.wait_ge(adj_in[k % 2], (ib * (NCH // 2) + (k // 2 + 1)) * 16)
                    else:
                        pe.wait_ge(wts_ready, ib * NCH + (k + 1))
                    for j in range(CH):
                        for it in range(BT):
                            at = j * W + it * P
                            mm = pe.matmul(m.acc[it // 2][:, it % 2, 0:D], wts[:, k % 2, at:at + P], src[:, k * CH + j, :],
                                           start=(k + j == 0), stop=(k == NCH - 1 and j == CH - 1))
                    mm.then_inc(wts_used, 1)
                if mode == MASKED:
                    pe.wait_ge(labels_used, ib * (T // 2) + (T // 2 + 2))
                    pe.wait_ge(abs_step, ib * (2 * NCH * CH + 1) + (2 * NCH * CH + 1))
                    for it in range(BT):
                        mm = pe.matmul(m.acc[2][:, 0, it:it + 1], abs_sum[:, it * P:(it + 1) * P], m.ones[:, :], start=True, stop=True)
                    mm.then_inc(rows_ready, 1)

        @block.scalar
        def _(act):
            act.activation(src[:, :, :], m.agg[:, :, :], ACT.Copy).then_inc(src_ready, 1)
            if mode == MASKED:
                act.wait_ge(y_in, 16)
                with act.Fori(0, NB) as ib:
                    act.wait_ge(labels_ready, ib * (T // 2) + 1)
                    act.activation(yb[:, :], yt[:, bass.ds(ib * W, W)], ACT.Copy).then_inc(yb_ready, 1)
            if mode == SENSITIVE:
                with act.Fori(0, NB) as ib:
                    for k in range(NCH):
                        act.wait_ge(inv_ready, ib * NCH + (k + 1))
                        act.activation(inv[:, :], inv[:, :], ACT.Square).then_inc(exp_ready, 1)
                        act.wait_ge(exp_ready, ib * 2 * NCH + (2 * k + 1))
                        act.activation(inv[:, :], inv[:, :], ACT.Exp, scale=-2.0).then_inc(exp_ready, 1)

        @block.vector
        def _(dve):
            dve.sem_inc(adj_used, 2)
            dve.sem_inc(labels_used, 2)
            dve.sem_inc(acc_free, 1)
            if mode == MASKED:
                dve.sem_inc(labels_ready, 1)
                dve.wait_ge(y_in, 16)
            dve.wait_ge(src_ready, 1)
            with dve.Fori(0, NB) as ib:
                if mode == MASKED:
                    dve.memset(abs_sum[:, :], 0.0).then_inc(abs_step, 1)
                for k in range(NCH) if mode != PLAIN else ():
                    dve.wait_ge(adj_in[k % 2], (ib * (NCH // 2) + (k // 2 + 1)) * 16)
                    dve.wait_ge(wts_used, ib * NCH + (k + 1))
                    if mode == MASKED:
                        for j in range(CH // 2):
                            dve.wait_ge(labels_ready, ib * (T // 2) + (k * CH // 2 + j + 2))
                            at = slice(2 * j * W, 2 * (j + 1) * W)
                            dve.tensor_tensor(wts[:, k % 2, at].rearrange("p (s n) -> p s n", s=2),
                                              adj[:, k % 2, at].rearrange("p (s n) -> p s n", s=2),
                                              m.acc[2 + j][:, :, :], ALU.mult).then_inc(labels_used, 1)
                        dve.wait_ge(labels_used, ib * (T // 2) + ((k + 1) * CH // 2 + 2))
                        dve.nop(nofuse=True)
                        dve.engine_nop().then_inc(adj_used, 1)
                        dve.engine_nop().then_inc(wts_ready, 1)
                        for j in range(CH):
                            step = 2 * (k * CH + j)
                            dve.wait_ge(abs_step, ib * (2 * NCH * CH + 1) + (step + 1))
                            part = wts[:, k % 2, j * W:(j + 1) * W]
                            dve.scalar_tensor_tensor(out=magnitude[:, :], in0=part, scalar=-1.0, in1=part,
                                                     op0=ALU.mult, op1=ALU.max).then_inc(abs_step, 1)
                            dve.wait_ge(abs_step, ib * (2 * NCH * CH + 1) + (step + 2))
                            dve.tensor_tensor(abs_sum[:, :], abs_sum[:, :], magnitude[:, :], ALU.add).then_inc(abs_step, 1)
                    else:
                        n = 3 * k
                        dve.tensor_scalar(wts[:, k % 2, :], adj[:, k % 2, :], 0.0, 1e-18, ALU.is_equal, ALU.mult).then_inc(sens_step, 1)
                        dve.wait_ge(sens_step, ib * 3 * NCH + (n + 1))
                        dve.tensor_tensor(wts[:, k % 2, :], wts[:, k % 2, :], adj[:, k % 2, :], ALU.add).then_inc(sens_step, 1)
                        dve.wait_ge(sens_step, ib * 3 * NCH + (n + 2))
                        dve.reciprocal(inv[:, :], wts[:, k % 2, :]).then_inc(sens_step, 1)
                        dve.wait_ge(sens_step, ib * 3 * NCH + (n + 3))
                        dve.tensor_scalar(inv[:, :], inv[:, :], -1.0, None, ALU.add).then_inc(inv_ready, 1)
                        dve.wait_ge(exp_ready, ib * 2 * NCH + (2 * k + 2))
                        dve.scalar_tensor_tensor(out=wts[:, k % 2, :], in0=adj[:, k % 2, :], scalar=1.0, in1=inv[:, :],
                                                 op0=ALU.is_lt, op1=ALU.mult).then_inc(wts_ready, 1)
                        dve.wait_ge(wts_ready, ib * NCH + (k + 1))
                        dve.nop(nofuse=True)
                        dve.engine_nop().then_inc(adj_used, 1)
                dve.wait_ge(wts_used, ib * NCH + (NCH + 2))
                for b in range(2):
                    last = dve.tensor_copy(m.agg[:, bass.ds(ib * BT + 2 * b, 2), :], m.acc[b][:, :, 0:D])
                if mode == MASKED:
                    dve.wait_ge(rows_ready, ib + 1)
                    last = dve.tensor_copy(m.rows[:, bass.ds(ib * BT, BT)], m.acc[2][:, 0, 0:BT])
                last.then_inc(acc_free, 1)


def message(nc, m, a):
    with ExitStack() as ctx:
        sem = lambda name: ctx.enter_context(nc.semaphore(name))
        sb = lambda name, shape: ctx.enter_context(nc.sbuf_tensor(name, shape, FP32))
        w3, b3 = sb("l3_w", [P, D]), sb("l3_b", [P, D])
        blk, blk_t = sb("l3_blk", [P, BT * D]), sb("l3_blk_t", [P, W])
        w3_in, blk_ready, t_full, t_free, mx_full, mx_free = (
            sem("w3_in"), sem("l3_blk_ready"), sem("l3_t_full"), sem("l3_t_free"), sem("l3_mx_full"), sem("l3_mx_free"))
        block = ctx.enter_context(nc.Block())

        @block.sync
        def _(sp):
            sp.dma_start(w3[:, :], a["L3_gnn_W"]).then_inc(w3_in, 16)
            sp.dma_start(b3[:, :], a["L3_gnn_B"]).then_inc(w3_in, 16)

        @block.scalar
        def _(act):
            with act.Fori(0, NB) as ib:
                act.wait_ge(mx_free, ib + 1)
                act.activation(blk[:, :], m.agg[:, bass.ds(ib * BT, BT), :], ACT.Copy, scale=1.0 / HS).then_inc(blk_ready, 1)
                act.wait_ge(t_full, ib + 1)
                act.activation(blk_t[:, :], m.acc[0][:, 0, :], ACT.Copy).then_inc(t_free, 1)

        @block.tensor
        def _(pe):
            pe.wait_ge(w3_in, 32)
            with pe.Fori(0, NB) as ib:
                pe.wait_ge(blk_ready, ib + 1)
                for t in range(BT):
                    mm = pe.transpose(m.acc[0][:, 0, t * P:(t + 1) * P], blk[:, t * D:(t + 1) * D], m.ident[:, :])
                mm.then_inc(t_full, 1)
                pe.wait_ge(t_free, ib + 1)
                for t in range(BT):
                    mm = pe.matmul(m.acc[1][:, 0, t * P:(t + 1) * P], blk_t[:, t * P:(t + 1) * P], w3[:, :], start=True, stop=True)
                mm.then_inc(mx_full, 1)

        @block.vector
        def _(dve):
            dve.sem_inc(mx_free, 1)
            dve.wait_ge(w3_in, 32)
            with dve.Fori(0, NB) as ib:
                dve.wait_ge(mx_full, ib + 1)
                dve.tensor_tensor(m.agg[:, bass.ds(ib * BT, BT), :], m.acc[1][:, 0, :].rearrange("p (t d) -> p t d", d=D),
                                  b3[:, :].unsqueeze(1).to_broadcast([P, BT, D]), ALU.add).then_inc(mx_free, 1)


def add_agg(nc, m):
    with ExitStack() as ctx:
        added = ctx.enter_context(nc.semaphore("added"))
        block = ctx.enter_context(nc.Block())

        @block.vector
        def _(dve):
            dve.tensor_tensor(m.x[:, :, :], m.x[:, :, :], m.agg[:, :, :], ALU.add).then_inc(added, 1)
            dve.wait_ge(added, 1)


def clear_semaphores(nc):
    used = sorted(nc.released_uncleared_semaphores)
    block = nc.Block()
    with block:
        @block.gpsimd
        def _(pool):
            pool.sem_clear(range(used[0], used[-1] + 1))

        @block.scalar
        def _(act):
            act.nop()

        @block.tensor
        def _(pe):
            pe.nop()

        @block.vector
        def _(dve):
            dve.nop()

        @block.sync
        def _(sp):
            sp.nop()


def reload_x(nc, m, a):
    with ExitStack() as ctx:
        x_again = ctx.enter_context(nc.semaphore("x_again"))
        block = ctx.enter_context(nc.Block())

        @block.sync
        def _(sp):
            sp.dma_start(m.x[:, :, :], a["x"].rearrange("p (t d) -> p t d", d=D)).then_inc(x_again, 16)
            sp.wait_ge(x_again, 16)


def binary_path(nc, m, a):
    setup(nc, m, a)
    aggregate_masked(nc, m, a)
    aggregate_compact(nc, m, True, "l1")
    mamba(nc, m, a, 1.0 / HS, "fast")
    layernorm_phase(nc, m, "l2")
    hyperbolic_in(nc, m, a, "fast")
    aggregate_compact(nc, m, False, "l2")


def general_path(nc, m, a):
    clear_semaphores(nc)
    reload_x(nc, m, a)
    layernorm_phase(nc, m, "g0")
    aggregate_any(nc, m, a, MASKED, "g0")
    after_l0(nc, m, a, "any")
    layernorm_phase(nc, m, "g1")
    aggregate_any(nc, m, a, PLAIN, "g1")
    mamba(nc, m, a, 1.0 / HS, "any")
    layernorm_phase(nc, m, "g2")
    hyperbolic_in(nc, m, a, "any")
    aggregate_any(nc, m, a, PLAIN, "g2")
    hyperbolic_out(nc, m, 1.0 / HS, "any")
    layernorm_phase(nc, m, "g3")
    message(nc, m, a)
    aggregate_any(nc, m, a, SENSITIVE, "g3")
    add_agg(nc, m)


def program(nc, a, out):
    with ExitStack() as ctx:
        m = Memory(nc, ctx)
        binary_path(nc, m, a)
        judge(nc, m)
        store_x(nc, m, out, "fast")
        other = nc.values_load(m.flag[0:1, 0:1], min_val=0, max_val=1)
        with nc.If(other > 0):
            general_path(nc, m, a)
            store_x(nc, m, out, "any")


def laid_out(x):
    import numpy as np
    rows = np.zeros((NP, x.shape[1]), x.dtype)
    rows[:N] = x
    return np.ascontiguousarray(rows.reshape(T, P, x.shape[1]).transpose(1, 0, 2).reshape(P, -1))


def halves(v):
    import numpy as np
    return np.ascontiguousarray(v.reshape(2, P, -1).transpose(1, 0, 2).reshape(P, -1))


def on_all(v):
    import numpy as np
    return np.ascontiguousarray(np.broadcast_to(v.reshape(1, -1), (P, v.size)))


def kernel(**inputs):
    import numpy as np
    import concourse.bacc as bacc
    from concourse.bass_utils import run_bass_kernel_spmd as run

    g = {k: np.asarray(v) for k, v in inputs.items()}
    adj = np.zeros((NP, NP), g["adj"].dtype)
    adj[:N, :N] = g["adj"]
    adj = np.ascontiguousarray(adj.reshape(NB, W, T, P).transpose(0, 3, 2, 1).reshape(NB, P, T * W))
    y = np.zeros((CLS, NP), g["L0_gnn_y"].dtype)
    y[:, :N] = g["L0_gnn_y"].T
    w_xp = g["L1_gnn_w_xp"]
    dt_cols, b_cols, c_cols = w_xp[:, :RANK], w_xp[:, RANK:RANK + ST], w_xp[:, RANK + ST:]
    arrays = {
        "x": laid_out(g["x"]), "adj": adj, "L0_gnn_h0": laid_out(g["L0_gnn_h0"]), "L0_gnn_y": y,
        "L1_gnn_gcn_w": g["L1_gnn_gcn_w"], "L1_gnn_gcn_b": on_all(g["L1_gnn_gcn_b"]),
        "L1_gnn_ln_g": g["L1_gnn_ln_g"].reshape(P, 1), "L1_gnn_ln_b": g["L1_gnn_ln_b"].reshape(P, 1),
        "L1_gnn_w_in": g["L1_gnn_w_in"], "L1_gnn_conv_w": halves(g["L1_gnn_conv_w"]), "L1_gnn_conv_b": halves(g["L1_gnn_conv_b"]),
        "w_cb": halves(np.concatenate([c_cols, b_cols] * 3, axis=1)), "w_r": halves(dt_cols),
        "L1_gnn_w_dt": g["L1_gnn_w_dt"], "L1_gnn_b_dt": halves(g["L1_gnn_b_dt"]), "L1_gnn_A_log": halves(g["L1_gnn_A_log"]),
        "L1_gnn_D_skip": halves(g["L1_gnn_D_skip"]), "L1_gnn_w_out": halves(g["L1_gnn_w_out"]),
        "L2_gnn_weight": np.ascontiguousarray(g["L2_gnn_weight"].T), "L2_gnn_bias": on_all(g["L2_gnn_bias"]),
        "L3_gnn_W": g["L3_gnn_W"], "L3_gnn_B": on_all(g["L3_gnn_B"]),
    }
    nc = bacc.Bacc("TRN2", target_bir_lowering=False, num_devices=1)
    a = {k: nc.dram_tensor(f"in_{k}", v.shape, mybir.dt.from_np(v.dtype), kind="ExternalInput").ap() for k, v in arrays.items()}
    out = nc.dram_tensor("out_0", (P, T * D), FP32, kind="ExternalOutput").ap()
    program(nc, a, out)
    r = run(nc, [{f"in_{k}": np.ascontiguousarray(v) for k, v in arrays.items()}], core_ids=[0])
    return np.ascontiguousarray(r.results[0]["out_0"].reshape(P, T, D).transpose(1, 0, 2).reshape(NP, D)[:N])
```

```python
from contextlib import ExitStack

import concourse.bass as bass
from concourse import mybir

FP32, BF16, FP16 = mybir.dt.float32, mybir.dt.bfloat16, mybir.dt.float16
FP8, U32, I32 = mybir.dt.float8e4, mybir.dt.uint32, mybir.dt.int32
ALU, ACT, AX = mybir.AluOpType, mybir.ActivationFunctionType, mybir.AxisListType

N = 5000
P = 128
D = 128
CLS = 16
T = -(-N // P)
NP = T * P
W = 512
NB = NP // W
BT = W // P
CH = 4
NCH = T // CH
RING = 5
QT = T // 4
HS = 4096.0
HW = 2 * D + 1
HP = 260
INNER = 256
ST = 16
RANK = 8
TAPS = 4
UN = 2 * ST
LN_EPS = 1e-5
L1_FLOOR = 1e-12
TINY = 1e-30
MAXNORM = 1.0 - 1e-5
ATANH_MAX = 6.10303382275888


def chain(eng, sem):
    count = [0]

    def link(ins):
        count[0] += 1
        ins.then_inc(sem, 1)
        eng.wait_ge(sem, count[0])

    return link


ROOT_SCALE = 2.0 ** 36


class Memory:

    def __init__(self, nc, ctx):
        def sb(name, shape, dt):
            return ctx.enter_context(nc.sbuf_tensor(name, shape, dt))

        self.x = sb("x_cur", [P, T, D], FP32)
        self.agg = sb("agg", [P, T, D], FP32)
        self.hh = sb("h_halves", [P, T, HP], FP16)
        self.rows = sb("row_sum", [P, T], FP32)
        self.cnt1 = sb("count_one", [P, T], FP32)
        self.nz = sb("count_nonzero", [P, NB * NCH], FP32)
        self.ybad = sb("y_bad", [CLS, 1], FP32)
        self.ident = sb("ident", [P, P], FP32)
        self.ones = sb("ones", [P, 1], FP32)
        self.flag = sb("flag", [1, 1], I32)
        self.acc = [ctx.enter_context(nc.psum_tensor(f"ps{k}", [P, 2, W], FP32)) for k in range(4)]
        self.adj8 = nc.dram_tensor("adj_compact", (NB, P, T * W // 2), BF16, kind="Internal").ap()
        self.b_rows = nc.dram_tensor("b_rows", (2, ST * W), FP32, kind="Internal").ap()


def setup(nc, m, a):
    with ExitStack() as ctx:
        sem = lambda name: ctx.enter_context(nc.semaphore(name))
        yt = ctx.enter_context(nc.sbuf_tensor("yt_chk", [CLS, NP], FP32))
        junk = ctx.enter_context(nc.sbuf_tensor("y_junk", [CLS, NP], BF16))
        x_in, y_in, zeroed, made, bad = sem("x_in"), sem("y_in"), sem("zeroed"), sem("made"), sem("bad")
        block = ctx.enter_context(nc.Block())

        @block.sync
        def _(sp):
            sp.dma_start(yt[:, :], a["L0_gnn_y"]).then_inc(y_in, 16)
            sp.dma_start(m.x[:, :, :], a["x"].rearrange("p (t d) -> p t d", d=D)).then_inc(x_in, 16)
            sp.wait_ge(x_in, 16)

        @block.gpsimd
        def _(pool):
            pool.memset(m.ident[:, :], 0.0).then_inc(zeroed, 1)
            pool.wait_ge(zeroed, 1)
            pool.affine_select(out=m.ident[:, :], in_=m.ident[:, :], compare_op=ALU.not_equal, fill=1.0,
                               base=0, pattern=[[-1, P]], channel_multiplier=1).then_inc(made, 1)
            pool.wait_ge(made, 1)

        @block.vector
        def _(dve):
            dve.memset(m.ones[:, :], 1.0)
            dve.memset(m.hh[:, :, 2 * D:HP], 1.0)
            dve.wait_ge(y_in, 16)
            dve.scalar_tensor_tensor(out=junk[:, :], in0=yt[:, :], scalar=1.0, in1=yt[:, :],
                                     op0=ALU.is_equal, op1=ALU.not_equal, accum_out=m.ybad[:, :]).then_inc(bad, 1)
            dve.wait_ge(bad, 1)


def rsqrt_newton(dve, link, out, y0, v, tmp, floor_scale):
    link(dve.tensor_tensor(tmp, y0, y0, ALU.mult))
    link(dve.tensor_tensor(tmp, tmp, v, ALU.mult))
    link(dve.tensor_scalar(tmp, tmp, -0.5 * floor_scale, 1.5 * floor_scale, ALU.mult, ALU.add))
    link(dve.tensor_tensor(out, tmp, y0, ALU.mult))


GT = T // 5


def layernorm(nc, ctx, m, tag, halves):
    sem = lambda name: ctx.enter_context(nc.semaphore(f"{name}_{tag}"))
    small = lambda name, *shape: ctx.enter_context(nc.sbuf_tensor(f"{name}_{tag}", [P, T, *shape], FP32))
    stats, mv = small("stats", 6), small("mv", 2)
    var, lnv, y0, tmp, rstd, shift = (small(s) for s in ("var", "lnv", "y0", "tmp", "rstd", "shift"))
    step, ln_done, var_ready, y0_ready, shift_ready, h_ready, high_ready, halves_ready = (
        sem(s) for s in ("step", "ln_done", "var_ready", "y0_ready", "shift_ready", "h_ready", "high_ready", "halves_ready"))

    def on_vector(dve):
        for t in range(T):
            last = dve.bn_stats(stats[:, t, :], m.x[:, t, :])
        link = chain(dve, step)
        link(last)
        for t in range(T):
            last = dve.bn_aggr(mv[:, t, :], stats[:, t, :])
        link(last)
        dve.tensor_scalar(var[:, :], mv[:, :, 1], LN_EPS, None, ALU.add).then_inc(var_ready, 1)
        dve.wait_ge(y0_ready, 1)
        rsqrt_newton(dve, link, rstd[:, :], y0[:, :], var[:, :], tmp[:, :], HS)
        dve.scalar_tensor_tensor(out=shift[:, :], in0=mv[:, :, 0], scalar=-1.0, in1=rstd[:, :],
                                 op0=ALU.mult, op1=ALU.mult).then_inc(shift_ready, 1)
        if halves:
            for g in range(T // GT):
                at = slice(g * GT, (g + 1) * GT)
                dve.wait_ge(h_ready, g + 1)
                dve.tensor_copy(m.hh[:, at, 0:D], m.agg[:, at, :]).then_inc(high_ready, 1)
                dve.wait_ge(high_ready, g + 1)
                dve.tensor_tensor(m.hh[:, at, D:2 * D], m.agg[:, at, :], m.hh[:, at, 0:D],
                                  ALU.subtract).then_inc(halves_ready, 1)
            dve.wait_ge(halves_ready, T // GT)

    def on_scalar(act, after_group=None):
        act.wait_ge(var_ready, 1)
        act.activation(lnv[:, :], var[:, :], ACT.Ln).then_inc(ln_done, 1)
        act.wait_ge(ln_done, 1)
        act.activation(y0[:, :], lnv[:, :], ACT.Exp, scale=-0.5).then_inc(y0_ready, 1)
        act.wait_ge(shift_ready, 1)
        for g in range(T // GT):
            for t in range(g * GT, (g + 1) * GT):
                last = act.activation(m.agg[:, t, :], m.x[:, t, :], ACT.Relu, scale=rstd[:, t:t + 1], bias=shift[:, t:t + 1])
            last.then_inc(h_ready, 1)
            if after_group:
                after_group(g)

    return on_vector, on_scalar, (halves_ready if halves else h_ready)


def layernorm_phase(nc, m, tag):
    with ExitStack() as ctx:
        on_vector, on_scalar, _ = layernorm(nc, ctx, m, tag, halves=False)
        block = ctx.enter_context(nc.Block())

        @block.vector
        def _(dve):
            on_vector(dve)

        @block.scalar
        def _(act):
            on_scalar(act)


def aggregate_masked(nc, m, a):
    KC = CH * W
    NPAIR = T // 2
    with ExitStack() as ctx:
        sem = lambda name: ctx.enter_context(nc.semaphore(name))
        sb = lambda name, shape, dt: ctx.enter_context(nc.sbuf_tensor(name, shape, dt))
        adj = sb("adj32", [P, RING, KC], FP32)
        bits = sb("bits", [P, RING, KC], FP8)
        masked = sb("masked", [P, 4, 2, W], BF16)
        low = sb("low_part", [P, 2, 2, D], FP32)
        junk = sb("sign_out", [P, 2, KC], BF16)
        yt = sb("yt32", [CLS, NP], FP32)
        y16 = sb("yt16", [CLS, NP], BF16)
        yb = sb("y_block", [CLS, W], BF16)
        adj_in = [sem(f"adj_in{k}") for k in range(RING)]
        bits_out = [sem(f"bits_out{k}") for k in range(RING)]
        y_in, y16_ready, yb_ready = sem("y0_in"), sem("y16_ready"), sem("yb_ready")
        counted, bits_ready, pair_ready, pair_masked = sem("counted"), sem("bits_ready"), sem("pair_ready"), sem("pair_masked")
        masked_used, low_ready, acc_free = sem("masked_used"), sem("low_ready"), sem("acc_free")
        h0, inv = sb("h0_block", [P, BT, D], FP32), sb("l0_r", [P, BT], FP32)
        h0_in, r_step, x_step = sem("h0_in"), sem("r_step"), sem("x_step")
        norm_on_vector, norm_on_scalar, halves_ready = layernorm(nc, ctx, m, "l0", halves=True)
        chunks_of = a["adj"]
        block = ctx.enter_context(nc.Block())

        @block.sync
        def _(sp):
            sp.dma_start(yt[:, :], a["L0_gnn_y"]).then_inc(y_in, 16)
            with sp.Fori(0, NB) as ib:
                for k in range(NCH):
                    sp.wait_ge(counted, ib * NCH + k + 1)
                    sp.wait_ge(bits_ready, ib * NCH + k + 1)
                    sp.dma_start(adj[:, k % RING, :],
                                 chunks_of[bass.ds(ib, 1), :, k * KC:(k + 1) * KC].rearrange("b p n -> (b p) n")
                                 ).then_inc(adj_in[k % RING], 16)
                sp.wait_ge(x_step, ib * 4 + 4)
                sp.dma_start(h0[:, :, :], a["L0_gnn_h0"].rearrange("p (b t d) -> b p t d", t=BT, d=D)[bass.ds(ib, 1)]
                             .rearrange("b p t d -> (b p) t d")).then_inc(h0_in, 16)

        @block.scalar
        def _(act):
            act.sem_inc(counted, RING)
            act.wait_ge(y_in, 16)
            act.activation(y16[:, :], yt[:, :], ACT.Copy).then_inc(y16_ready, 1)
            norm_on_scalar(act)
            act.wait_ge(y16_ready, 1)
            with act.Fori(0, NB) as ib:
                act.wait_ge(pair_ready, ib * NPAIR + 1)
                act.activation(yb[:, :], y16[:, bass.ds(ib * W, W)], ACT.Copy).then_inc(yb_ready, 1)
                for k in range(NCH):
                    act.wait_ge(adj_in[k % RING], (ib * (NCH // RING) + k // RING + 1) * 16)
                    act.wait_ge(counted, ib * NCH + (RING + k - 1))
                    act.activation(junk[:, k % 2, :], adj[:, k % RING, :].bitcast(U32), ACT.Sign,
                                   accum_out=m.nz[:, bass.ds(ib * NCH + k, 1)]).then_inc(counted, 1)
                    act.wait_ge(bits_ready, ib * NCH + (RING + k + 1))
                    act.dma_start(m.adj8[bass.ds(ib, 1), :, k * KC // 2:(k + 1) * KC // 2].rearrange("b p n -> (b p) n"),
                                  bits[:, k % RING, :].bitcast(BF16)).then_inc(bits_out[k % RING], 16)
                act.wait_ge(masked_used, ib * NPAIR + (NPAIR + 4))
                for b in range(2):
                    act.activation(low[:, b, :, :], m.acc[b][:, :, D:2 * D], ACT.Copy).then_inc(low_ready, 1)

        @block.vector
        def _(dve):
            dve.sem_inc(bits_ready, RING)
            dve.sem_inc(pair_masked, 3)
            dve.sem_inc(acc_free, 1)
            for k in range(RING):
                dve.sem_inc(bits_out[k], 16)
            norm_on_vector(dve)
            with dve.Fori(0, NB) as ib:
                for k in range(NCH):
                    r = k % RING
                    dve.wait_ge(adj_in[r], (ib * (NCH // RING) + k // RING + 1) * 16)
                    dve.wait_ge(bits_out[r], (ib * (NCH // RING) + k // RING + 1) * 16)
                    dve.nop(nofuse=True)
                    dve.tensor_scalar(bits[:, r, :], adj[:, r, :], 1.0, None, ALU.is_equal,
                                      saturate=False).then_inc(bits_ready, 1)
                    dve.wait_ge(bits_ready, ib * NCH + (RING + k + 1))
                    for j in range(CH // 2):
                        q = k * (CH // 2) + j
                        dve.wait_ge(pair_ready, ib * NPAIR + (q + 2))
                        dve.wait_ge(masked_used, ib * NPAIR + (q + 1))
                        dve.nop(nofuse=True)
                        dve.tensor_tensor(masked[:, q % 4, :, :],
                                          bits[:, r, j * 2 * W:(j + 1) * 2 * W].rearrange("p (s n) -> p s n", s=2),
                                          m.acc[2 + q % 2][:, :, :], ALU.mult).then_inc(pair_masked, 1)
                dve.wait_ge(masked_used, ib * NPAIR + (NPAIR + 4))
                dve.wait_ge(x_step, ib * 4 + 4)
                for b in range(2):
                    dve.wait_ge(low_ready, ib * 2 + (b + 1))
                    dve.tensor_tensor(m.agg[:, bass.ds(ib * BT + 2 * b, 2), :], m.acc[b][:, :, 0:D],
                                      low[:, b, :, :], ALU.add)
                    last = dve.tensor_scalar(inv[:, 2 * b:2 * b + 2], m.acc[b][:, :, 2 * D], L1_FLOOR, None, ALU.max)
                last.then_inc(acc_free, 1)
                dve.wait_ge(acc_free, ib + 2)
                dve.reciprocal(inv[:, :], inv[:, :]).then_inc(r_step, 1)
                dve.wait_ge(r_step, ib * 2 + 1)
                dve.tensor_scalar(inv[:, :], inv[:, :], 0.9 / HS, None, ALU.mult).then_inc(r_step, 1)

        @block.tensor
        def _(pe):
            pe.sem_inc(masked_used, 4)
            pe.sem_inc(pair_ready, 1)

            def labels(ib, q):
                pe.wait_ge(pair_masked, ib * NPAIR + (q + 2))
                for s in range(2):
                    mm = pe.matmul(m.acc[2 + q % 2][:, s, :], y16[:, (2 * q + s) * P:(2 * q + s + 1) * P], yb[:, :],
                                   start=True, stop=True)
                mm.then_inc(pair_ready, 1)

            def gather(ib, q):
                pe.wait_ge(pair_masked, ib * NPAIR + (q + 4))
                if q == 0:
                    pe.wait_ge(acc_free, ib + 1)
                if 2 * q % GT == 0:
                    pe.wait_ge(halves_ready, 2 * q // GT + 1)
                for s in range(2):
                    for it in range(BT):
                        mm = pe.matmul(m.acc[it // 2][:, it % 2, 0:HW], masked[:, q % 4, s, it * P:(it + 1) * P],
                                       m.hh[:, 2 * q + s, 0:HW], start=(q + s == 0), stop=(q == NPAIR - 1 and s == 1))
                mm.then_inc(masked_used, 1)
                return mm

            with pe.Fori(0, NB) as ib:
                pe.wait_ge(yb_ready, ib + 1)
                for q in range(NPAIR):
                    labels(ib, q)
                    if q >= 2:
                        gather(ib, q - 2)
                for q in (NPAIR - 2, NPAIR - 1):
                    gather(ib, q)

        @block.gpsimd
        def _(pool):
            pool.sem_inc(x_step, 4)
            pool.wait_ge(halves_ready, T // GT)
            with pool.Fori(0, NB) as ib:
                at = bass.ds(ib * BT, BT)
                pool.wait_ge(h0_in, ib * 16 + 16)
                pool.nop(nofuse=True)
                pool.tensor_scalar(h0[:, :, :], h0[:, :, :], 0.1, None, ALU.mult).then_inc(x_step, 1)
                pool.wait_ge(r_step, ib * 2 + 2)
                pool.nop(nofuse=True)
                pool.tensor_tensor(m.agg[:, at, :], m.agg[:, at, :], inv[:, :].unsqueeze(2).to_broadcast([P, BT, D]),
                                   ALU.mult).then_inc(x_step, 1)
                pool.wait_ge(x_step, ib * 4 + 5)
                pool.nop(nofuse=True)
                pool.tensor_tensor(m.x[:, at, :], m.x[:, at, :], h0[:, :, :], ALU.add).then_inc(x_step, 1)
                pool.wait_ge(x_step, ib * 4 + 7)
                pool.nop(nofuse=True)
                pool.tensor_tensor(m.x[:, at, :], m.x[:, at, :], m.agg[:, at, :], ALU.add).then_inc(x_step, 1)
            for k in range(RING):
                pool.wait_ge(bits_out[k], 16 * (NB * NCH // RING + 1))


def aggregate_compact(nc, m, a, counting, tag, weights=None, out=None):
    width = HW if counting else 2 * D
    KQ = QT * W
    with ExitStack() as ctx:
        sem = lambda name: ctx.enter_context(nc.semaphore(f"{name}_{tag}"))
        bits = ctx.enter_context(nc.sbuf_tensor(f"bits_{tag}", [P, 4, KQ], FP8))
        low = ctx.enter_context(nc.sbuf_tensor(f"low_{tag}", [P, 4, 2, D], FP32))
        bits_in = [sem(f"bits_in{k}") for k in range(4)]
        bits_used, low_ready, acc_free = sem("bits_used"), sem("low_ready"), sem("acc_free")
        if counting:
            norm_on_vector, norm_on_scalar, halves_ready = layernorm(nc, ctx, m, tag, halves=True)
        else:
            sb = lambda name, *shape: ctx.enter_context(nc.sbuf_tensor(f"tail_{name}", [P, *shape], FP32))
            s_blk, relu, squares = sb("s_blk", BT, D), sb("relu", BT, D), sb("squares", 2, BT, D)
            norm2, lnv, y0, tmp, rs, norm = (sb(n, 2, BT) for n in ("norm2", "lnv", "y0", "tmp", "rs", "norm"))
            arg, coef = sb("arg", BT), sb("coef", BT)
            stored = sem("stored")
            judge_on_vector, judge_on_tensor = judge(nc, ctx, m)
            relu_ready, squares_ready, norm2_ready, ln_ready, y0_ready, arg_ready, th_ready, tail_step, x_ready = (
                sem(f"tail_{n}") for n in ("relu_ready", "squares_ready", "norm2_ready", "ln_ready", "y0_ready", "arg_ready",
                                 "th_ready", "tail_step", "x_ready"))
        block = ctx.enter_context(nc.Block())

        def tail_on_scalar(act, ib):
            act.wait_ge(acc_free, ib + 3)
            act.wait_ge(x_ready, ib + 1)
            act.activation(relu[:, :, :], s_blk[:, :, :], ACT.Relu, scale=1.0 / HS).then_inc(relu_ready, 1)
            act.activation(squares[:, 0, :, :], s_blk[:, :, :], ACT.Square, scale=1.0 / HS)
            act.wait_ge(relu_ready, ib + 1)
            act.activation(squares[:, 1, :, :], relu[:, :, :], ACT.Square).then_inc(squares_ready, 1)
            act.wait_ge(norm2_ready, ib + 1)
            act.activation(lnv[:, :, :], norm2[:, :, :], ACT.Ln, scale=ROOT_SCALE).then_inc(ln_ready, 1)
            act.wait_ge(ln_ready, ib + 1)
            act.activation(y0[:, :, :], lnv[:, :, :], ACT.Exp, scale=-0.5).then_inc(y0_ready, 1)
            act.wait_ge(arg_ready, ib + 1)
            act.activation(coef[:, :], arg[:, :], ACT.Tanh).then_inc(th_ready, 1)
            act.wait_ge(x_ready, ib + 2)
            act.dma_start(out.rearrange("p (b t d) -> b p t d", t=BT, d=D)[bass.ds(ib, 1)].rearrange("b p t d -> (b p) t d"),
                          m.x[:, bass.ds(ib * BT, BT), :]).then_inc(stored, 16)

        def tail_on_vector(dve, ib):
            TAIL = 11
            count = [0]

            def link(ins):
                count[0] += 1
                ins.then_inc(tail_step, 1)
                dve.wait_ge(tail_step, ib * TAIL + count[0])

            dve.wait_ge(squares_ready, ib + 1)
            link(dve.reduce_sum(norm2[:, :, :], squares[:, :, :, :], axis=AX.X))
            dve.tensor_scalar(norm2[:, :, :], norm2[:, :, :], TINY, None, ALU.max).then_inc(norm2_ready, 1)
            dve.wait_ge(y0_ready, ib + 1)
            link(dve.tensor_scalar(y0[:, :, :], y0[:, :, :], ROOT_SCALE ** 0.5, None, ALU.mult))
            rsqrt_newton(dve, link, rs[:, :, :], y0[:, :, :], norm2[:, :, :], tmp[:, :, :], 1.0)
            link(dve.tensor_tensor(norm[:, :, :], norm2[:, :, :], rs[:, :, :], ALU.mult))
            link(dve.tensor_scalar(tmp[:, 0, :], rs[:, 0, :], ATANH_MAX, 1.0, ALU.mult, ALU.min))
            dve.tensor_tensor(arg[:, :], norm[:, 1, :], tmp[:, 0, :], ALU.mult).then_inc(arg_ready, 1)
            dve.wait_ge(th_ready, ib + 1)
            link(dve.tensor_scalar(coef[:, :], coef[:, :], MAXNORM, None, ALU.min))
            link(dve.tensor_tensor(coef[:, :], coef[:, :], rs[:, 1, :], ALU.mult))
            link(dve.tensor_tensor(relu[:, :, :], relu[:, :, :], coef[:, :].unsqueeze(2).to_broadcast([P, BT, D]), ALU.mult))
            assert count[0] == TAIL
            rows = m.x[:, bass.ds(ib * BT, BT), :]
            dve.tensor_tensor(rows, rows, relu[:, :, :], ALU.add).then_inc(x_ready, 1)

        @block.sync
        def _(sp):
            with sp.Fori(0, NB) as ib:
                for k in range(4):
                    sp.wait_ge(bits_used, ib * 4 + (k + 1))
                    sp.dma_start(bits[:, k, :].bitcast(BF16),
                                 m.adj8[bass.ds(ib, 1), :, k * KQ // 2:(k + 1) * KQ // 2].rearrange("b p n -> (b p) n")
                                 ).then_inc(bits_in[k], 16)
            if counting:
                weights.load(sp, a)

        @block.tensor
        def _(pe):
            pe.sem_inc(bits_used, 4)
            if not counting:
                judge_on_tensor(pe)
            with pe.Fori(0, NB // 2) as pair:
                for par in range(2):
                    ib = pair * 2 + par
                    pe.wait_ge(acc_free, ib + 1)
                    for k in range(4):
                        pe.wait_ge(bits_in[k], ib * 16 + 16)
                        pe.nop(nofuse=True)
                        for j in range(QT):
                            if counting and (k * QT + j) % GT == 0:
                                pe.wait_ge(halves_ready, (k * QT + j) // GT + 1)
                            for it in range(BT):
                                mm = pe.matmul(m.acc[2 * par + it // 2][:, it % 2, 0:width],
                                               bits[:, k, j * W + it * P:j * W + (it + 1) * P],
                                               m.hh[:, k * QT + j, 0:width],
                                               start=(k + j == 0), stop=(k == 3 and j == QT - 1))
                        mm.then_inc(bits_used, 1)

        @block.scalar
        def _(act):
            if counting:
                norm_on_scalar(act)
            with act.Fori(0, NB // 2) as pair:
                for par in range(2):
                    ib = pair * 2 + par
                    act.wait_ge(bits_used, ib * 4 + 8)
                    act.wait_ge(acc_free, ib + 1)
                    for b in range(2):
                        act.activation(low[:, 2 * par + b, :, :], m.acc[2 * par + b][:, :, D:2 * D], ACT.Copy).then_inc(low_ready, 1)
                    if not counting:
                        tail_on_scalar(act, ib)

        @block.vector
        def _(dve):
            if counting:
                norm_on_vector(dve)
            else:
                judge_on_vector(dve)
                dve.sem_inc(x_ready, 1)
            dve.sem_inc(acc_free, 2)
            with dve.Fori(0, NB // 2) as pair:
                for par in range(2):
                    ib = pair * 2 + par
                    for b in range(2):
                        dve.wait_ge(low_ready, ib * 2 + (b + 1))
                        to = m.agg[:, bass.ds(ib * BT + 2 * b, 2), :] if counting else s_blk[:, 2 * b:2 * b + 2, :]
                        last = dve.tensor_tensor(to, m.acc[2 * par + b][:, :, 0:D], low[:, 2 * par + b, :, :], ALU.add)
                        if counting:
                            last = dve.tensor_copy(m.cnt1[:, bass.ds(ib * BT + 2 * b, 2)],
                                                   m.acc[2 * par + b][:, :, 2 * D])
                    last.then_inc(acc_free, 1)
                    if not counting:
                        tail_on_vector(dve, ib)

        if not counting:
            @block.gpsimd
            def _(pool):
                pool.wait_ge(stored, NB * 16)


def after_l0(nc, m, a):
    with ExitStack() as ctx:
        sem = lambda name: ctx.enter_context(nc.semaphore(name))
        h0 = ctx.enter_context(nc.sbuf_tensor("h0_any", [P, T, D], FP32))
        r = ctx.enter_context(nc.sbuf_tensor("l0_r_any", [P, T], FP32))
        h0_in, step = sem("h0_in_any"), sem("l0_step_any")
        block = ctx.enter_context(nc.Block())

        @block.sync
        def _(sp):
            sp.dma_start(h0[:, :, :], a["L0_gnn_h0"].rearrange("p (t d) -> p t d", d=D)).then_inc(h0_in, 16)

        @block.vector
        def _(dve):
            link = chain(dve, step)
            link(dve.tensor_scalar(r[:, :], m.rows[:, :], L1_FLOOR, None, ALU.max))
            link(dve.reciprocal(r[:, :], r[:, :]))
            link(dve.tensor_scalar(r[:, :], r[:, :], 0.9 / HS, None, ALU.mult))
            link(dve.tensor_tensor(m.agg[:, :, :], m.agg[:, :, :], r[:, :].unsqueeze(2).to_broadcast([P, T, D]), ALU.mult))
            link(dve.tensor_tensor(m.x[:, :, :], m.x[:, :, :], m.agg[:, :, :], ALU.add))
            dve.wait_ge(h0_in, 16)
            link(dve.scalar_tensor_tensor(out=m.x[:, :, :], in0=h0[:, :, :], scalar=0.1, in1=m.x[:, :, :],
                                          op0=ALU.mult, op1=ALU.add))


RG = 8
PE_LAG = 3


class MambaWeights:

    def __init__(self, nc, ctx, tag):
        def sb(name, *shape):
            return ctx.enter_context(nc.sbuf_tensor(f"{name}_{tag}", list(shape), FP32))

        self.gcn_w, self.gcn_b = sb("gcn_w", P, D), sb("gcn_b", P, D)
        self.ln_g, self.ln_b = sb("ln_g", P, 1), sb("ln_b", P, 1)
        self.w_in, self.w_out = sb("w_in", P, 2 * INNER), sb("w_out", P, 2 * D)
        self.conv_w, self.conv_b = sb("conv_w", P, 2 * TAPS), sb("conv_b", P, 2)
        self.w_cb, self.w_r, self.w_dt, self.b_dt = sb("w_cb", P, 2 * 96), sb("w_r", P, 2 * RANK), sb("w_dt", RANK, INNER), sb("b_dt", P, 2)
        self.decay, self.skip = sb("decay", P, UN), sb("skip", P, 2)
        self.consts_in = ctx.enter_context(nc.semaphore(f"consts_in_{tag}"))
        self.loads = [(self.gcn_w, "L1_gnn_gcn_w"), (self.gcn_b, "L1_gnn_gcn_b"), (self.ln_g, "L1_gnn_ln_g"),
                      (self.ln_b, "L1_gnn_ln_b"), (self.w_in, "L1_gnn_w_in"), (self.conv_w, "L1_gnn_conv_w"),
                      (self.conv_b, "L1_gnn_conv_b"), (self.w_cb, "w_cb"), (self.w_r, "w_r"), (self.w_dt, "L1_gnn_w_dt"),
                      (self.b_dt, "L1_gnn_b_dt"), (self.decay, "L1_gnn_A_log"), (self.skip, "L1_gnn_D_skip"),
                      (self.w_out, "L1_gnn_w_out")]
        self.ALL_IN = 16 * len(self.loads)

    def load(self, eng, a):
        for tile, name in self.loads:
            eng.dma_start(tile[:, :], a[name]).then_inc(self.consts_in, 16)


def mamba(nc, m, a, weights, agg_scale, tag):
    with ExitStack() as ctx:
        def sem(name):
            return ctx.enter_context(nc.semaphore(f"{name}_{tag}"))

        def sb(name, shape, dt=FP32):
            return ctx.enter_context(nc.sbuf_tensor(f"{name}_{tag}", shape, dt))

        w = weights
        gcn_w, gcn_b, ln_g, ln_b, w_in, w_out = w.gcn_w, w.gcn_b, w.ln_g, w.ln_b, w.w_in, w.w_out
        conv_w, conv_b, w_cb, w_r, w_dt, b_dt, decay, skip = w.conv_w, w.conv_b, w.w_cb, w.w_r, w.w_dt, w.b_dt, w.decay, w.skip
        consts_in, ALL_IN = w.consts_in, w.ALL_IN
        pick = sb("pick", [96, ST * P], BF16)

        s_blk = g_act = sb("by_node", [P, BT, D])
        s_t = h_t = sb("transposed", [P, W])
        stats, mv = sb("stats", [P, BT, 6]), sb("mv", [P, BT, 2])
        var, lnv, y0, tmp, rstd, shift = (sb(s, [P, BT]) for s in ("var", "lnv", "y0", "tmp", "rstd", "shift"))
        xc, cv = sb("xc", [P, 2, W + TAPS]), sb("cv", [P, 2, W])
        zs, us, dts, dtu = (sb(s, [P, 2, 2, W]) for s in ("zs", "us", "dts", "dtu"))
        c_parts, bc = sb("c_parts", [96, 2, W], BF16), sb("bc", [96, W])
        dtr, soft, lin = sb("dtr", [RANK, W]), sb("soft", [P, 2, W]), sb("lin", [P, 2, W])
        bbc = sb("bbc", [P, 4, 2, W])
        da, bx, hs, ps = sb("da", [P, RG, W]), sb("bx", [P, RG, W]), sb("hs", [P, RG, W]), sb("ps", [P, 4, W])
        yg = sb("yg", [P, 2, W])
        state = sb("state", [P, UN])

        c_bank, y_bank, misc, out_bank = m.acc[0:2], m.acc[2], m.acc[3][:, 0, :], m.acc[3][:, 1, :]

        pick0, decay_ready, zeroed = sem("pick0"), sem("decay_ready"), sem("zeroed")
        a_ready, bx_ready, c_ready, scan_done = sem("a_ready"), sem("bx_ready"), sem("c_ready"), sem("scan_done")
        p_ready, p_used, state_saved, y_read, gated = sem("p_ready"), sem("p_used"), sem("state_saved"), sem("y_read"), sem("gated")
        misc_full, misc_free = sem("misc_full"), sem("misc_free")
        s_ready, var_ready, y0_ready, ln_step, hn_ready = sem("s_ready"), sem("var_ready"), sem("y0_ready"), sem("ln_step"), sem("hn_ready")
        halo, conv_step, u_ready, b_ready, c_step, c_sub = sem("halo"), sem("conv_step"), sem("u_ready"), sem("b_ready"), sem("c_step"), sem("c_sub")
        soft_step, dt_ready, out_full, out_free = sem("soft_step"), sem("dt_ready"), sem("out_full"), sem("out_free")
        b_out, bbc_in = sem("b_out"), [sem(f"bbc_in{k}") for k in range(4)]
        block = ctx.enter_context(nc.Block())

        def front_use(f, j):
            return 11 * f + (j + 1)

        def chunks(eng, body):
            body(0, 0, True, False)
            with eng.Fori(0, (NB - 2) // 2) as two:
                body(two * 2 + 1, 1, True, True)
                body(two * 2 + 2, 0, True, True)
            body(NB - 1, 1, False, True)

        @block.sync
        def _(sp):
            def b_store(f, q):
                sp.wait_ge(b_ready, f + 1)
                sp.dma_start(m.b_rows[q:q + 1, :].rearrange("a (s w) -> (a s) w", w=W),
                             bc[ST:2 * ST, :]).then_inc(b_out, 16)
                sp.wait_ge(b_out, f * 16 + 16)
                sp.nop(nofuse=True)

            def body(c, q, front, back):
                for g in range(UN // 2):
                    sp.wait_ge(bx_ready, c * UN + (2 * g + 2))
                    sp.dma_start(bbc[:, g % 4, :, :],
                                 m.b_rows[q, (g % 8) * 2 * W:(g % 8 + 1) * 2 * W].rearrange("(s w) -> s w", w=W)
                                 .partition_broadcast(P)).then_inc(bbc_in[g % 4], 16)
                if front:
                    b_store(c + 1, 1 - q)

            b_store(0, 0)
            chunks(sp, body)

        @block.gpsimd
        def _(pool):
            pool.sem_inc(bx_ready, 8)
            pool.memset(pick[:, :], 0.0).then_inc(pick0, 1)
            rows = pick[:, :].rearrange("k (n p) -> k n p", p=P)
            for part in range(3):
                pool.wait_ge(pick0, part + 1)
                pool.affine_select(out=rows, in_=rows, compare_op=ALU.not_equal, fill=1.0, base=-32 * part,
                                   pattern=[[-1, ST], [0, P]], channel_multiplier=1).then_inc(pick0, 1)
            pool.memset(state[:, :], 0.0).then_inc(zeroed, 1)
            pool.memset(xc[:, :, 0:TAPS - 1], 0.0).then_inc(zeroed, 1)

            def dt_half(f, q, h):
                pool.wait_ge(soft_step, 5 * f + 5)
                pool.tensor_tensor(dts[:, q, h, :], soft[:, h, :], lin[:, h, :], ALU.add).then_inc(dt_ready, 1)
                pool.wait_ge(dt_ready, 4 * f + (2 * h + 1))
                pool.tensor_tensor(dtu[:, q, h, :], dts[:, q, h, :], us[:, q, h, :], ALU.mult).then_inc(dt_ready, 1)

            def body(c, q, front, back):
                for u in range(UN):
                    if u % 2 == 0:
                        pool.wait_ge(bbc_in[u // 2 % 4], (c * 4 + (u // 8 + 1)) * 16)
                    if u % ST == 0:
                        pool.wait_ge(dt_ready, 4 * c + (2 * (u // ST) + 2))
                    pool.wait_ge(scan_done, c * UN + (u + 1))
                    pool.tensor_tensor(bx[:, u % RG, :], dtu[:, q, u // ST, :], bbc[:, u // 2 % 4, u % 2, :],
                                       ALU.mult).then_inc(bx_ready, 1)
                    if u == 4:
                        dt_half(c, q, 1)
                    if front and u == 30:
                        pool.wait_ge(scan_done, c * UN + 8)
                        dt_half(c + 1, 1 - q, 0)

            dt_half(0, 0, 0)
            chunks(pool, body)

        @block.scalar
        def _(act):
            act.wait_ge(consts_in, ALL_IN)
            act.activation(decay[:, :], decay[:, :], ACT.Exp).then_inc(decay_ready, 1)
            act.wait_ge(decay_ready, 1)
            act.activation(decay[:, :], decay[:, :], ACT.Copy, scale=-1.0).then_inc(decay_ready, 1)
            act.wait_ge(decay_ready, 2)

            def take_agg(f):
                act.activation(s_blk[:, :, :], m.agg[:, f * BT:(f + 1) * BT, :] if isinstance(f, int)
                               else m.agg[:, bass.ds(f * BT, BT), :], ACT.Copy, scale=agg_scale).then_inc(s_ready, 1)

            def take_s_t(f):
                act.wait_ge(misc_full, front_use(f, 1))
                act.activation(s_t[:, :], misc, ACT.Copy).then_inc(misc_free, 1)

            def var_root(f):
                act.wait_ge(var_ready, f + 1)
                act.activation(lnv[:, :], var[:, :], ACT.Ln).then_inc(y0_ready, 1)
                act.wait_ge(y0_ready, 2 * f + 1)
                act.activation(y0[:, :], lnv[:, :], ACT.Exp, scale=-0.5).then_inc(y0_ready, 1)

            def take_h_t(f):
                act.wait_ge(misc_full, front_use(f, 3))
                act.activation(h_t[:, :], misc, ACT.Identity, scale=ln_g[:, :], bias=ln_b[:, :]).then_inc(misc_free, 1)
                if isinstance(f, int) and f == 0:
                    act.wait_ge(zeroed, 2)
                    act.sem_inc(halo, 1)
                else:
                    act.wait_ge(conv_step, 8 * f)
                    act.activation(xc[:, :, 0:TAPS - 1], xc[:, :, W:W + TAPS - 1], ACT.Copy).then_inc(halo, 1)

            def take_xc(f, h):
                act.wait_ge(misc_full, front_use(f, 4 + h))
                act.wait_ge(halo, f + 1)
                act.activation(xc[:, h, TAPS - 1:W + TAPS - 1], misc, ACT.Copy).then_inc(misc_free, 1)

            def take_z(f, q, h):
                if not (isinstance(f, int) and f < 2):
                    act.wait_ge(gated, 2 * f - 2)
                act.wait_ge(misc_full, front_use(f, 6 + h))
                act.activation(zs[:, q, h, :], misc, ACT.Copy).then_inc(misc_free, 1)

            def silus(f, q):
                act.wait_ge(misc_free, front_use(f, 7))
                act.activation(zs[:, q, :, :], zs[:, q, :, :], ACT.Silu)
                act.wait_ge(conv_step, 8 * f + 8)
                act.activation(us[:, q, :, :], cv[:, :, :], ACT.Silu).then_inc(u_ready, 1)

            def take_bc(f, q):
                act.wait_ge(misc_full, front_use(f, 8))
                if not (isinstance(f, int) and f == 0):
                    act.wait_ge(b_out, f * 16)
                act.activation(bc[:, :], misc[0:96, :], ACT.Copy).then_inc(b_ready, 1)
                act.activation(c_parts[:, q, :], misc[0:96, :], ACT.Copy).then_inc(c_step, 1)
                act.wait_ge(c_step, 3 * f + 1)
                act.sem_inc(misc_free, 1)

            def second_c(f, q):
                act.wait_ge(c_sub, 2 * f + 1)
                act.activation(c_parts[32:64, q, :], bc[32:64, :], ACT.Copy)
                act.activation(c_parts[64:96, q, :], bc[64:96, :], ACT.Copy).then_inc(c_step, 1)

            def third_c(f, q):
                act.wait_ge(c_sub, 2 * f + 2)
                act.activation(c_parts[64:96, q, :], bc[64:96, :], ACT.Copy).then_inc(c_step, 1)

            def take_dtr(f):
                act.wait_ge(misc_full, front_use(f, 9))
                act.activation(dtr[:, :], misc[0:RANK, :], ACT.Copy).then_inc(misc_free, 1)

            def softplus(f, h):
                act.wait_ge(misc_full, front_use(f, 10 + h))
                if not (isinstance(f, int) and f == 0):
                    act.wait_ge(dt_ready, 4 * f)
                act.activation(soft[:, h, :], misc, ACT.Abs, bias=b_dt[:, h:h + 1]).then_inc(soft_step, 1)
                act.activation(lin[:, h, :], misc, ACT.Relu, bias=b_dt[:, h:h + 1]).then_inc(misc_free, 1)
                act.wait_ge(soft_step, 5 * f + (2 * h + 1))
                act.activation(soft[:, h, :], soft[:, h, :], ACT.Exp, scale=-1.0).then_inc(soft_step, 1)
                if h == 1:
                    act.wait_ge(soft_step, 5 * f + 4)
                    act.activation(soft[:, :, :], soft[:, :, :], ACT.Ln, bias=1.0).then_inc(soft_step, 1)

            def front_step(f, q, u):
                if u == 0:
                    take_agg(f)
                if u == 2:
                    take_s_t(f)
                if u == 5:
                    var_root(f)
                if u == 9:
                    take_h_t(f)
                if u in (10, 12):
                    take_xc(f, (u - 10) // 2)
                if u in (14, 16):
                    take_z(f, q, (u - 14) // 2)
                if u == 16:
                    silus(f, q)
                if u == 19:
                    take_bc(f, q)
                if u == 20:
                    take_dtr(f)
                if u == 22:
                    second_c(f, q)
                if u in (22, 24):
                    softplus(f, (u - 22) // 2)
                if u == 25:
                    third_c(f, q)

            def body(c, q, front, back):
                for u in range(UN):
                    if u % ST == 0:
                        act.wait_ge(dt_ready, 4 * c + (2 * (u // ST) + 2))
                    act.wait_ge(scan_done, c * UN + (u + 1))
                    act.activation(da[:, u % RG, :], dts[:, q, u // ST, :], ACT.Exp,
                                   scale=decay[:, u:u + 1]).then_inc(a_ready, 1)
                    if front:
                        front_step(c + 1, 1 - q, u)

            for u in range(UN):
                front_step(0, 0, u)
            chunks(act, body)

        @block.vector
        def _(dve):
            dve.sem_inc(scan_done, 8)
            dve.sem_inc(state_saved, UN // 4)
            dve.sem_inc(p_ready, 8)
            dve.sem_inc(y_read, 2)
            dve.sem_inc(out_free, 1)
            dve.sem_inc(misc_free, 1)
            dve.wait_ge(consts_in, ALL_IN)
            dve.wait_ge(zeroed, 2)

            def scan(c, u):
                dve.wait_ge(a_ready, c * UN + (u + 1))
                dve.wait_ge(bx_ready, c * UN + (u + 9))
                dve.wait_ge(p_ready, c * UN + (u + 1))
                dve.wait_ge(state_saved, c * (UN // 4) + (u // 4 + 7))
                dve.tensor_tensor_scan(hs[:, u % RG, :], da[:, u % RG, :], bx[:, u % RG, :], state[:, u:u + 1],
                                       ALU.mult, ALU.add).then_inc(scan_done, 1)

            def save_states(c, g):
                dve.wait_ge(scan_done, c * UN + (4 * g + 12))
                at = 4 * g % RG
                dve.tensor_copy(state[:, 4 * g:4 * g + 4], hs[:, at:at + 4, W - 1]).then_inc(state_saved, 1)

            def times_c(c, u):
                dve.wait_ge(c_ready, c * UN + (u + 1))
                dve.wait_ge(p_used, c * UN + (u + 1))
                dve.wait_ge(scan_done, c * UN + (u + 9))
                dve.tensor_tensor(ps[:, u % 4, :], hs[:, u % RG, :], c_bank[u // 2 % 2][:, u % 2, :], ALU.mult).then_inc(p_ready, 1)

            def gate(c, q, h):
                dve.wait_ge(p_used, c * UN + (ST * (h + 1) + 4))
                if h == 0 and not (isinstance(c, int) and c == 0):
                    dve.wait_ge(out_full, c)
                dve.scalar_tensor_tensor(out=yg[:, h, :], in0=us[:, q, h, :], scalar=skip[:, h:h + 1], in1=y_bank[:, h, :],
                                         op0=ALU.mult, op1=ALU.add).then_inc(y_read, 1)
                dve.wait_ge(y_read, 2 * c + (h + 3))
                dve.tensor_tensor(yg[:, h, :], yg[:, h, :], zs[:, q, h, :], ALU.mult).then_inc(gated, 1)

            def add_out(c):
                dve.wait_ge(out_full, c + 1)
                at = m.x[:, c * BT:(c + 1) * BT, :] if isinstance(c, int) else m.x[:, bass.ds(c * BT, BT), :]
                dve.tensor_tensor(at, at, out_bank.rearrange("p (t d) -> p t d", d=D), ALU.add).then_inc(out_free, 1)

            def gcn_stats(f):
                n = 14 * f
                dve.wait_ge(misc_full, front_use(f, 2))
                if not (isinstance(f, int) and f == 0):
                    dve.wait_ge(hn_ready, f)
                dve.tensor_tensor(g_act[:, :, :], misc.rearrange("p (t d) -> p t d", d=D),
                                  gcn_b[:, :].unsqueeze(1).to_broadcast([P, BT, D]), ALU.add).then_inc(misc_free, 1)
                dve.wait_ge(misc_free, front_use(f, 2))
                dve.tensor_scalar(g_act[:, :, :], g_act[:, :, :], 0.0, None, ALU.max).then_inc(ln_step, 1)
                dve.wait_ge(ln_step, n + 1)
                for t in range(BT):
                    dve.bn_stats(stats[:, t, :], g_act[:, t, :]).then_inc(ln_step, 1)
                dve.wait_ge(ln_step, n + 5)
                dve.nop(nofuse=True)
                for t in range(BT):
                    dve.bn_aggr(mv[:, t, :], stats[:, t, :]).then_inc(ln_step, 1)
                dve.wait_ge(ln_step, n + 9)
                dve.tensor_scalar(var[:, :], mv[:, :, 1], LN_EPS, None, ALU.add).then_inc(var_ready, 1)

            def normalize(f):
                n = 14 * f + 9
                dve.wait_ge(y0_ready, 2 * f + 2)
                dve.tensor_tensor(tmp[:, :], y0[:, :], y0[:, :], ALU.mult).then_inc(ln_step, 1)
                dve.wait_ge(ln_step, n + 1)
                dve.tensor_tensor(tmp[:, :], tmp[:, :], var[:, :], ALU.mult).then_inc(ln_step, 1)
                dve.wait_ge(ln_step, n + 2)
                dve.tensor_scalar(tmp[:, :], tmp[:, :], -0.5, 1.5, ALU.mult, ALU.add).then_inc(ln_step, 1)
                dve.wait_ge(ln_step, n + 3)
                dve.tensor_tensor(rstd[:, :], tmp[:, :], y0[:, :], ALU.mult).then_inc(ln_step, 1)
                dve.wait_ge(ln_step, n + 4)
                dve.scalar_tensor_tensor(out=shift[:, :], in0=mv[:, :, 0], scalar=-1.0, in1=rstd[:, :],
                                         op0=ALU.mult, op1=ALU.mult).then_inc(ln_step, 1)
                dve.wait_ge(ln_step, n + 5)
                for t in range(BT):
                    last = dve.tensor_scalar(g_act[:, t, :], g_act[:, t, :], rstd[:, t:t + 1], shift[:, t:t + 1],
                                             ALU.mult, ALU.add)
                last.then_inc(hn_ready, 1)

            def convolve(f, h, part):
                n = 8 * f + 4 * h
                if part == 0:
                    dve.wait_ge(misc_free, front_use(f, 4 + h))
                    if not (isinstance(f, int) and f == 0):
                        dve.wait_ge(u_ready, f)
                    dve.tensor_scalar(cv[:, h, :], xc[:, h, 0:W], conv_w[:, TAPS * h:TAPS * h + 1], conv_b[:, h:h + 1],
                                      ALU.mult, ALU.add).then_inc(conv_step, 1)
                for k in ((1,), (2, 3))[part]:
                    dve.wait_ge(conv_step, n + k)
                    dve.scalar_tensor_tensor(out=cv[:, h, :], in0=xc[:, h, k:k + W],
                                             scalar=conv_w[:, TAPS * h + k:TAPS * h + k + 1], in1=cv[:, h, :],
                                             op0=ALU.mult, op1=ALU.add).then_inc(conv_step, 1)

            def c_minus_first(f, q):
                dve.wait_ge(c_step, 3 * f + 1)
                dve.tensor_tensor(bc[32:64, :], bc[32:64, :], c_parts[32:64, q, :], ALU.subtract)
                dve.tensor_tensor(bc[64:96, :], bc[64:96, :], c_parts[64:96, q, :], ALU.subtract).then_inc(c_sub, 1)

            def c_minus_second(f, q):
                dve.wait_ge(c_step, 3 * f + 2)
                dve.tensor_tensor(bc[64:96, :], bc[64:96, :], c_parts[64:96, q, :], ALU.subtract).then_inc(c_sub, 1)

            def front_step(f, q, u):
                if u == 1:
                    gcn_stats(f)
                if u == 3:
                    normalize(f)
                if u in (8, 9, 10, 11):
                    convolve(f, (u - 8) // 2, (u - 8) % 2)
                if u == 17:
                    c_minus_first(f, q)
                if u == 20:
                    c_minus_second(f, q)

            def body(c, q, front, back):
                for u in range(UN):
                    scan(c, u)
                    if u:
                        times_c(c, u - 1)
                    if u % 4 == 0 and u:
                        save_states(c, u // 4 - 1)
                    if back and u == 4:
                        gate(c - 1, 1 - q, 1)
                    if back and u == 9:
                        add_out(c - 1)
                    if u == ST + 4:
                        gate(c, q, 0)
                    if front:
                        front_step(c + 1, 1 - q, u)
                times_c(c, UN - 1)
                save_states(c, UN // 4 - 1)

            for u in range(UN):
                front_step(0, 0, u)
            chunks(dve, body)
            gate(NB - 1, 1, 1)
            add_out(NB - 1)

        @block.tensor
        def _(pe):
            pe.sem_inc(misc_full, 1)
            pe.sem_inc(p_used, 4)
            pe.wait_ge(consts_in, ALL_IN)
            pe.wait_ge(pick0, 4)

            def take_misc(use):
                pe.wait_ge(misc_free, use - 1)

            def transposes(f, use, src):
                take_misc(use)
                for t in range(BT):
                    mm = pe.transpose(misc[:, t * P:(t + 1) * P], src[:, t, :], m.ident[:, :])
                mm.then_inc(misc_full, 1)

            def front_step(f, q, u):
                if u == 1:
                    pe.wait_ge(s_ready, f + 1)
                    transposes(f, front_use(f, 1), s_blk)
                if u == 3:
                    take_misc(front_use(f, 2))
                    for t in range(BT):
                        mm = pe.matmul(misc[:, t * P:(t + 1) * P], s_t[:, t * P:(t + 1) * P], gcn_w[:, :], start=True, stop=True)
                    mm.then_inc(misc_full, 1)
                if u == 6:
                    pe.wait_ge(hn_ready, f + 1)
                    transposes(f, front_use(f, 3), g_act)
                if u in (7, 9, 11, 13):
                    j = (u - 7) // 2
                    take_misc(front_use(f, 4 + j))
                    pe.matmul(misc, w_in[:, j * P:(j + 1) * P], h_t[:, :], start=True, stop=True).then_inc(misc_full, 1)
                if u in (16, 17):
                    j, w, k = (8, w_cb, 96) if u == 16 else (9, w_r, RANK)
                    take_misc(front_use(f, j))
                    pe.wait_ge(u_ready, f + 1)
                    for h in range(2):
                        mm = pe.matmul(misc[0:k, :], w[:, h * k:(h + 1) * k], us[:, q, h, :], start=(h == 0), stop=(h == 1))
                    mm.then_inc(misc_full, 1)
                if u in (19, 21):
                    h = (u - 19) // 2
                    take_misc(front_use(f, 10 + h))
                    pe.matmul(misc, w_dt[:, h * P:(h + 1) * P], dtr[:, :], start=True, stop=True).then_inc(misc_full, 1)

            def spread_c(c, q, u):
                if u == 0:
                    pe.wait_ge(c_step, 3 * c + 3)
                pe.wait_ge(p_ready, c * UN + (u + 5))
                n = u % ST
                pe.matmul(c_bank[u // 2 % 2][:, u % 2, :], pick[:, n * P:(n + 1) * P], c_parts[:, q, :],
                          start=True, stop=True).then_inc(c_ready, 1)

            def add_state(c, u):
                n, h = u % ST, u // ST
                pe.wait_ge(p_ready, c * UN + (u + 9))
                if n == 0:
                    pe.wait_ge(y_read, 2 * c + (h + 1))
                pe.matmul(y_bank[:, h, :], m.ident[:, :], ps[:, u % 4, :], start=(n == 0), stop=(n == ST - 1)).then_inc(p_used, 1)

            def output(c):
                pe.wait_ge(out_free, c + 1)
                pe.wait_ge(gated, 2 * c + 2)
                for t in range(BT):
                    for h in range(2):
                        mm = pe.matmul(out_bank[:, t * P:(t + 1) * P], yg[:, h, t * P:(t + 1) * P], w_out[:, h * D:(h + 1) * D],
                                       start=(h == 0), stop=(h == 1))
                mm.then_inc(out_full, 1)

            def body(c, q, front, back):
                for u in range(UN):
                    spread_c(c, q, u)
                    if u >= PE_LAG:
                        add_state(c, u - PE_LAG)
                    elif back:
                        add_state(c - 1, UN + u - PE_LAG)
                    if back and u == 9:
                        output(c - 1)
                    if front:
                        front_step(c + 1, 1 - q, u)

            for u in range(UN):
                front_step(0, 0, u)
            chunks(pe, body)
            for u in range(UN - PE_LAG, UN):
                add_state(NB - 1, u)
            output(NB - 1)


def hyperbolic_in(nc, m, a, tag):
    with ExitStack() as ctx:
        sem = lambda name: ctx.enter_context(nc.semaphore(f"{name}_{tag}"))
        sb = lambda name, shape: ctx.enter_context(nc.sbuf_tensor(f"{name}_{tag}", shape, FP32))
        names = ("at_x", "at_h", "lp", "lm", "sq", "poly", "mask", "alpha", "x2", "xy", "num_a", "num_b", "den", "c1", "c2",
                 "hn2", "cross", "h_y0", "h_tmp", "rs_h", "n_h")
        s = {n: sb(f"l2_{n}", [P, T]) for n in names}
        norm2, lnv, y0, tmp, rs, norm = (sb(f"l2_{n}", [P, 2 * T + 1]) for n in ("norm2", "lnv", "y0", "tmp", "rs", "norm"))
        OF_X, OF_M, OF_B = slice(0, T), slice(T, 2 * T), slice(2 * T, 2 * T + 1)
        dot, arg, th = sb("l2_dot", [P, T]), sb("l2_arg", [P, T + 1]), sb("l2_th", [P, T + 1])
        beta, y2 = sb("l2_beta", [P, 1]), sb("l2_y2", [P, 1])
        mx, bias_part = sb("l2_mx", [P, T, D]), sb("l2_bias_part", [P, T, D])
        w_t, bias, b_sq = sb("l2_w", [P, D]), sb("l2_bias", [P, D]), sb("l2_bsq", [P, D])
        blk_t, h_sq, mx_sq, mx_b = sb("l2_blk_t", [P, 2, W]), sb("l2_h_sq", [P, 2, BT, D]), sb("l2_mx_sq", [P, 2, BT, D]), sb("l2_mx_b", [P, 2, BT, D])
        w_in_, step, for_act, for_dve = sem("l2_w_in"), sem("l2_step"), sem("l2_for_act"), sem("l2_for_dve")
        t_full, t_free, mx_full, mx_copied = sem("t_full"), sem("t_free"), sem("mx_full"), sem("mx_copied")
        h_sq_ready, mx_sq_ready, mx_b_ready, reduced = sem("h_sq_ready"), sem("mx_sq_ready"), sem("mx_b_ready"), sem("reduced")
        c_ready, bias_part_ready, sum_step, high_ready, halves_ready = (
            sem("c_ready"), sem("bias_part_ready"), sem("sum_step"), sem("high_ready"), sem("halves_ready"))
        norm_on_vector, norm_on_scalar, h_ready = layernorm(nc, ctx, m, f"hyper_{tag}", halves=False)
        block = ctx.enter_context(nc.Block())
        S = lambda n: s[n][:, :]
        rows = lambda ib: slice(ib * BT, (ib + 1) * BT)
        by_tile = lambda ap: ap.rearrange("p (t d) -> p t d", d=D)
        bias_on = lambda n: bias[:, :].unsqueeze(1).to_broadcast([P, n, D])
        HAS = BT * NB // GT
        PER = NB // HAS

        @block.sync
        def _(sp):
            sp.dma_start(w_t[:, :], a["L2_gnn_weight"]).then_inc(w_in_, 16)
            sp.dma_start(bias[:, :], a["L2_gnn_bias"]).then_inc(w_in_, 16)

        @block.tensor
        def _(pe):
            pe.wait_ge(w_in_, 32)

            def transposes(ib):
                pe.wait_ge(h_ready, ib // PER + 1)
                if ib >= 2:
                    pe.wait_ge(t_free, ib - 1)
                for t in range(BT):
                    mm = pe.transpose(m.acc[0][:, ib % 2, t * P:(t + 1) * P], m.agg[:, ib * BT + t, :], m.ident[:, :])
                mm.then_inc(t_full, 1)

            transposes(0)
            for ib in range(NB):
                r = ib % 2
                if ib + 1 < NB:
                    transposes(ib + 1)
                pe.wait_ge(t_free, ib + 1)
                if ib >= 2:
                    pe.wait_ge(mx_copied, ib - 1)
                for t in range(BT):
                    mm = pe.matmul(m.acc[1][:, r, t * P:(t + 1) * P], blk_t[:, r, t * P:(t + 1) * P], w_t[:, :], start=True, stop=True)
                mm.then_inc(mx_full, 1)

        @block.gpsimd
        def _(pool):
            def squares(ib):
                pool.wait_ge(h_ready, ib // PER + 1)
                if ib >= 2:
                    pool.wait_ge(reduced, 3 * (ib - 2) + 1)
                pool.tensor_tensor(h_sq[:, ib % 2, :, :], m.agg[:, rows(ib), :], m.agg[:, rows(ib), :], ALU.mult).then_inc(h_sq_ready, 1)

            pool.wait_ge(w_in_, 32)
            squares(0)
            for ib in range(NB):
                if ib + 1 < NB:
                    squares(ib + 1)
                pool.wait_ge(mx_copied, ib + 1)
                if ib >= 2:
                    pool.wait_ge(reduced, 3 * (ib - 2) + 3)
                pool.tensor_tensor(mx_b[:, ib % 2, :, :], mx[:, rows(ib), :], bias_on(BT), ALU.mult).then_inc(mx_b_ready, 1)
            pool.wait_ge(c_ready, 1)
            for g in range(T // GT):
                at = slice(g * GT, (g + 1) * GT)
                pool.tensor_tensor(bias_part[:, at, :], bias_on(GT), s["c2"][:, at].unsqueeze(2).to_broadcast([P, GT, D]),
                                   ALU.mult).then_inc(bias_part_ready, 1)

        @block.scalar
        def _(act):
            def products(g):
                for ib in range(g * PER, (g + 1) * PER):
                    act.wait_ge(t_full, ib + 1)
                    if ib >= 2:
                        act.wait_ge(mx_full, ib - 1)
                    act.activation(blk_t[:, ib % 2, :], m.acc[0][:, ib % 2, :], ACT.Copy, scale=1.0 / HS).then_inc(t_free, 1)
                for ib in range(g * PER, (g + 1) * PER):
                    act.wait_ge(mx_copied, ib + 1)
                    if ib >= 2:
                        act.wait_ge(reduced, 3 * (ib - 2) + 2)
                    act.activation(mx_sq[:, ib % 2, :, :], mx[:, rows(ib), :], ACT.Square).then_inc(mx_sq_ready, 1)

            norm_on_scalar(act, lambda g: products(g - 1) if g else None)
            products(HAS - 1)

            def give(ins, n):
                ins.then_inc(for_dve, 1)
                act.wait_ge(for_dve, n)

            act.wait_ge(for_act, 1)
            give(act.activation(lnv[:, :], norm2[:, :], ACT.Ln, scale=ROOT_SCALE), 1)
            give(act.activation(y0[:, :], lnv[:, :], ACT.Exp, scale=-0.5), 2)
            act.wait_ge(for_act, 2)
            give(act.activation(S("lp"), norm[:, OF_X], ACT.Ln, bias=1.0), 3)
            give(act.activation(S("lm"), norm[:, OF_X], ACT.Ln, scale=-1.0, bias=1.0), 4)
            act.wait_ge(for_act, 3)
            give(act.activation(th[:, :], arg[:, :], ACT.Tanh), 5)
            act.wait_ge(for_act, 4)
            give(act.activation(S("lp"), S("hn2"), ACT.Ln, scale=ROOT_SCALE), 6)
            give(act.activation(S("h_y0"), S("lp"), ACT.Exp, scale=-0.5), 7)
            act.wait_ge(for_act, 5)
            give(act.activation(S("lp"), S("n_h"), ACT.Ln, bias=1.0), 8)
            give(act.activation(S("lm"), S("n_h"), ACT.Ln, scale=-1.0, bias=1.0), 9)
            for g in range(T // GT):
                at = slice(g * GT, (g + 1) * GT)
                act.wait_ge(sum_step, 2 * g + 2)
                act.activation(m.hh[:, at, 0:D], m.agg[:, at, :], ACT.Copy).then_inc(high_ready, 1)

        @block.vector
        def _(dve):
            norm_on_vector(dve)
            link = chain(dve, step)

            def tt(out, x, y, op):
                link(dve.tensor_tensor(out, x, y, op))

            def ts(out, x, s1, op0, s2=None, op1=ALU.bypass):
                link(dve.tensor_scalar(out, x, s1, s2, op0, op1) if s2 is not None else dve.tensor_scalar(out, x, s1, None, op0))

            def hand(ins, n):
                ins.then_inc(for_act, 1)
                dve.wait_ge(for_act, n)

            def artanh(n, out):
                tt(out, S("lp"), S("lm"), ALU.subtract)
                ts(out, out, 0.5, ALU.mult)
                tt(S("sq"), n, n, ALU.mult)
                ts(S("poly"), S("sq"), 1 / 15, ALU.mult, 1 / 13, ALU.add)
                for k in (11, 9, 7, 5, 3, 1):
                    tt(S("poly"), S("poly"), S("sq"), ALU.mult)
                    ts(S("poly"), S("poly"), 1 / k, ALU.add)
                tt(S("poly"), S("poly"), n, ALU.mult)
                tt(S("poly"), S("poly"), out, ALU.subtract)
                ts(S("mask"), n, 0.25, ALU.is_lt)
                tt(S("poly"), S("poly"), S("mask"), ALU.mult)
                tt(out, out, S("poly"), ALU.add)

            def reduce(ib):
                to = slice(T + ib * BT, T + (ib + 1) * BT)
                dve.wait_ge(h_sq_ready, ib + 1)
                dve.reduce_sum(norm2[:, rows(ib)], h_sq[:, ib % 2, :, :], axis=AX.X).then_inc(reduced, 1)
                dve.wait_ge(mx_sq_ready, ib + 1)
                dve.reduce_sum(norm2[:, to], mx_sq[:, ib % 2, :, :], axis=AX.X).then_inc(reduced, 1)
                dve.wait_ge(mx_b_ready, ib + 1)
                dve.reduce_sum(dot[:, rows(ib)], mx_b[:, ib % 2, :, :], axis=AX.X).then_inc(reduced, 1)

            dve.wait_ge(w_in_, 32)
            tt(b_sq[:, :], bias[:, :], bias[:, :], ALU.mult)
            link(dve.reduce_sum(norm2[:, OF_B], b_sq[:, :], axis=AX.X))
            for ib in range(NB):
                dve.wait_ge(mx_full, ib + 1)
                dve.tensor_copy(mx[:, rows(ib), :], by_tile(m.acc[1][:, ib % 2, :])).then_inc(mx_copied, 1)
                if ib:
                    reduce(ib - 1)
            reduce(NB - 1)
            dve.wait_ge(reduced, 3 * NB)
            ts(norm2[:, OF_X], norm2[:, OF_X], 1.0 / HS ** 2, ALU.mult)
            hand(dve.tensor_scalar(norm2[:, :], norm2[:, :], TINY, None, ALU.max), 1)
            dve.wait_ge(for_dve, 2)
            ts(y0[:, :], y0[:, :], ROOT_SCALE ** 0.5, ALU.mult)
            rsqrt_newton(dve, link, rs[:, :], y0[:, :], norm2[:, :], tmp[:, :], 1.0)
            tt(norm[:, :], norm2[:, :], rs[:, :], ALU.mult)
            hand(dve.tensor_scalar(norm[:, OF_X], norm[:, OF_X], 1.0 - 1e-7, None, ALU.min), 2)
            dve.wait_ge(for_dve, 4)
            artanh(norm[:, OF_X], S("at_x"))
            tt(arg[:, OF_X], norm[:, OF_M], rs[:, OF_X], ALU.mult)
            tt(arg[:, OF_X], arg[:, OF_X], S("at_x"), ALU.mult)
            hand(dve.tensor_copy(arg[:, T:T + 1], norm[:, OF_B]), 3)
            dve.wait_ge(for_dve, 5)
            ts(th[:, :], th[:, :], MAXNORM, ALU.min)
            tt(S("alpha"), th[:, OF_X], rs[:, OF_M], ALU.mult)
            tt(beta[:, :], th[:, T:T + 1], rs[:, OF_B], ALU.mult)
            tt(y2[:, :], beta[:, :], beta[:, :], ALU.mult)
            tt(y2[:, :], y2[:, :], norm2[:, OF_B], ALU.mult)
            tt(S("x2"), S("alpha"), S("alpha"), ALU.mult)
            tt(S("x2"), S("x2"), norm2[:, OF_M], ALU.mult)
            tt(S("xy"), S("alpha"), dot[:, :], ALU.mult)
            ts(S("xy"), S("xy"), beta[:, :], ALU.mult, 2.0, ALU.mult)
            ts(S("num_a"), S("xy"), y2[:, :], ALU.add, 1.0, ALU.add)
            ts(S("num_b"), S("x2"), -1.0, ALU.mult, 1.0, ALU.add)
            ts(S("den"), S("x2"), y2[:, :], ALU.mult, 1.0, ALU.add)
            tt(S("den"), S("den"), S("xy"), ALU.add)
            ts(S("den"), S("den"), 1e-15, ALU.max)
            link(dve.reciprocal(S("den"), S("den")))
            tt(S("c1"), S("num_a"), S("alpha"), ALU.mult)
            tt(S("c1"), S("c1"), S("den"), ALU.mult)
            ts(S("c2"), S("num_b"), beta[:, :], ALU.mult)
            tt(S("c2"), S("c2"), S("den"), ALU.mult)
            tt(S("hn2"), S("c1"), norm2[:, OF_M], ALU.mult)
            tt(S("cross"), S("c2"), dot[:, :], ALU.mult)
            ts(S("cross"), S("cross"), 2.0, ALU.mult)
            tt(S("hn2"), S("hn2"), S("cross"), ALU.add)
            tt(S("hn2"), S("hn2"), S("c1"), ALU.mult)
            tt(S("cross"), S("c2"), S("c2"), ALU.mult)
            ts(S("cross"), S("cross"), norm2[:, OF_B], ALU.mult)
            tt(S("hn2"), S("hn2"), S("cross"), ALU.add)
            hand(dve.tensor_scalar(S("hn2"), S("hn2"), TINY, None, ALU.max), 4)
            dve.wait_ge(for_dve, 7)
            ts(S("h_y0"), S("h_y0"), ROOT_SCALE ** 0.5, ALU.mult)
            rsqrt_newton(dve, link, S("rs_h"), S("h_y0"), S("hn2"), S("h_tmp"), 1.0)
            tt(S("n_h"), S("hn2"), S("rs_h"), ALU.mult)
            hand(dve.tensor_scalar(S("n_h"), S("n_h"), MAXNORM, None, ALU.min), 5)
            dve.wait_ge(for_dve, 9)
            artanh(S("n_h"), S("at_h"))
            tt(S("at_h"), S("at_h"), S("rs_h"), ALU.mult)
            ts(S("at_h"), S("at_h"), HS, ALU.mult)
            tt(S("c2"), S("c2"), S("at_h"), ALU.mult)
            dve.tensor_tensor(S("c1"), S("c1"), S("at_h"), ALU.mult).then_inc(c_ready, 1)
            dve.wait_ge(c_ready, 1)

            def low_half(g):
                at = slice(g * GT, (g + 1) * GT)
                dve.wait_ge(high_ready, g + 1)
                dve.tensor_tensor(m.hh[:, at, D:2 * D], m.agg[:, at, :], m.hh[:, at, 0:D], ALU.subtract).then_inc(halves_ready, 1)

            for g in range(T // GT):
                at = slice(g * GT, (g + 1) * GT)
                dve.tensor_tensor(m.agg[:, at, :], mx[:, at, :], s["c1"][:, at].unsqueeze(2).to_broadcast([P, GT, D]),
                                  ALU.mult).then_inc(sum_step, 1)
                dve.wait_ge(sum_step, 2 * g + 1)
                dve.wait_ge(bias_part_ready, g + 1)
                dve.tensor_tensor(m.agg[:, at, :], m.agg[:, at, :], bias_part[:, at, :], ALU.add).then_inc(sum_step, 1)
                if g:
                    low_half(g - 1)
            low_half(T // GT - 1)


def hyperbolic_out(nc, m, scale):
    with ExitStack() as ctx:
        sb = lambda name: ctx.enter_context(nc.sbuf_tensor(f"o_{name}", [P, T], FP32))
        sem = lambda name: ctx.enter_context(nc.semaphore(f"o_{name}"))
        v2, r2, lnv, y0, tmp, rs_v, n_v, rs_r, n_r, th = (sb(n) for n in ("v2", "r2", "lnv", "y0", "tmp", "rsv", "nv", "rsr", "nr", "th"))
        big = ctx.enter_context(nc.sbuf_tensor("o_big", [P, T, D], FP32))
        step, for_act, for_dve = sem("step"), sem("for_act"), sem("for_dve")
        block = ctx.enter_context(nc.Block())

        @block.scalar
        def _(act):
            act.activation(big[:, :, :], m.agg[:, :, :], ACT.Square, scale=scale).then_inc(for_dve, 1)
            act.wait_ge(for_act, 1)
            act.activation(m.agg[:, :, :], m.agg[:, :, :], ACT.Relu, scale=scale).then_inc(for_dve, 1)
            act.wait_ge(for_dve, 2)
            act.activation(big[:, :, :], m.agg[:, :, :], ACT.Square).then_inc(for_dve, 1)
            for k, v in enumerate((v2, r2)):
                act.wait_ge(for_act, 2 + k)
                act.activation(lnv[:, :], v[:, :], ACT.Ln, scale=ROOT_SCALE).then_inc(for_dve, 1)
                act.wait_ge(for_dve, 4 + 2 * k)
                act.activation(y0[:, :], lnv[:, :], ACT.Exp, scale=-0.5).then_inc(for_dve, 1)
            act.wait_ge(for_act, 4)
            act.activation(th[:, :], n_r[:, :], ACT.Tanh).then_inc(for_dve, 1)

        @block.vector
        def _(dve):
            link = chain(dve, step)
            dve.wait_ge(for_dve, 1)
            dve.reduce_sum(v2[:, :], big[:, :, :], axis=AX.X).then_inc(for_act, 1)
            dve.wait_ge(for_dve, 3)
            link(dve.reduce_sum(r2[:, :], big[:, :, :], axis=AX.X))
            for k, (v, rs, n) in enumerate(((v2, rs_v, n_v), (r2, rs_r, n_r))):
                dve.tensor_scalar(v[:, :], v[:, :], TINY, None, ALU.max).then_inc(for_act, 1)
                dve.wait_ge(for_dve, 5 + 2 * k)
                link(dve.tensor_scalar(y0[:, :], y0[:, :], ROOT_SCALE ** 0.5, None, ALU.mult))
                rsqrt_newton(dve, link, rs[:, :], y0[:, :], v[:, :], tmp[:, :], 1.0)
                link(dve.tensor_tensor(n[:, :], v[:, :], rs[:, :], ALU.mult))
            link(dve.tensor_scalar(rs_v[:, :], rs_v[:, :], ATANH_MAX, 1.0, ALU.mult, ALU.min))
            dve.tensor_tensor(n_r[:, :], n_r[:, :], rs_v[:, :], ALU.mult).then_inc(for_act, 1)
            dve.wait_ge(for_dve, 8)
            link(dve.tensor_scalar(th[:, :], th[:, :], MAXNORM, None, ALU.min))
            link(dve.tensor_tensor(th[:, :], th[:, :], rs_r[:, :], ALU.mult))
            link(dve.tensor_tensor(m.agg[:, :, :], m.agg[:, :, :], th[:, :].unsqueeze(2).to_broadcast([P, T, D]), ALU.mult))
            link(dve.tensor_tensor(m.x[:, :, :], m.x[:, :, :], m.agg[:, :, :], ALU.add))


def judge(nc, ctx, m):
    sb = lambda name, shape: ctx.enter_context(nc.sbuf_tensor(name, shape, FP32))
    sem = lambda name: ctx.enter_context(nc.semaphore(name))
    n1, n0, tot, odd = sb("n_one", [P, NB]), sb("n_nonzero", [P, NB]), sb("tot_row", [1, NB + 1]), sb("odd", [1, 1])
    step, diff_ready, summed = sem("j_step"), sem("diff_ready"), sem("summed")

    def on_vector(dve):
        link = chain(dve, step)
        link(dve.reduce_sum(n0[:, :], m.nz[:, :].rearrange("p (b k) -> p b k", k=NCH), axis=AX.X))
        link(dve.reduce_sum(n1[:, :], m.cnt1[:, :].rearrange("p (b k) -> p b k", k=BT), axis=AX.X))
        dve.tensor_tensor(n0[:, :], n0[:, :], n1[:, :], ALU.subtract).then_inc(diff_ready, 1)
        dve.wait_ge(summed, 1)
        link(dve.tensor_copy(tot[:, :], m.acc[3][0:1, 0, 0:NB + 1]))
        link(dve.reduce_sum(odd[:, :], tot[:, :], axis=AX.X))
        link(dve.tensor_scalar(odd[:, :], odd[:, :], 0.5, None, ALU.is_gt))
        link(dve.tensor_copy(m.flag[:, :], odd[:, :]))

    def on_tensor(pe):
        pe.wait_ge(diff_ready, 1)
        pe.matmul(m.acc[3][0:1, 0, 0:NB], m.ones[:, :], n0[:, :], start=True, stop=True)
        pe.matmul(m.acc[3][0:1, 0, NB:NB + 1], m.ones[0:CLS, :], m.ybad[:, :], start=True, stop=True).then_inc(summed, 1)

    return on_vector, on_tensor


def store_x(nc, m, out):
    with ExitStack() as ctx:
        stored = ctx.enter_context(nc.semaphore("stored"))
        block = ctx.enter_context(nc.Block())

        @block.sync
        def _(sp):
            sp.dma_start(out.rearrange("p (t d) -> p t d", d=D), m.x[:, :, :]).then_inc(stored, 16)
            sp.wait_ge(stored, 16)


MASKED, PLAIN, SENSITIVE = "masked", "plain", "sensitive"


def aggregate_any(nc, m, a, mode, tag):
    KC = CH * W
    with ExitStack() as ctx:
        sem = lambda name: ctx.enter_context(nc.semaphore(f"{name}_{tag}"))
        sb = lambda name, shape: ctx.enter_context(nc.sbuf_tensor(f"{name}_{tag}", shape, FP32))
        src = sb("src", [P, T, D])
        adj = sb("adj_any", [P, 2, KC])
        wts = sb("wts", [P, 2, KC]) if mode != PLAIN else adj
        if mode == MASKED:
            yt, yb, abs_sum, magnitude = (sb("yt_any", [CLS, NP]), sb("yb_any", [CLS, W]), sb("abs_sum", [P, W]),
                                          sb("magnitude", [P, W]))
        if mode == SENSITIVE:
            inv = sb("inv", [P, KC])
        adj_in = [sem(f"adj_in{k}") for k in range(2)]
        y_in, yb_ready, labels_ready, labels_used = sem("y_in"), sem("yb_ready"), sem("labels_ready"), sem("labels_used")
        src_ready, adj_used, wts_ready, wts_used = sem("src_ready"), sem("adj_used"), sem("wts_ready"), sem("wts_used")
        abs_step, acc_free, rows_ready, inv_ready, exp_ready, sens_step = (
            sem("abs_step"), sem("acc_free"), sem("rows_ready"), sem("inv_ready"), sem("exp_ready"), sem("sens_step"))
        block = ctx.enter_context(nc.Block())

        @block.sync
        def _(sp):
            if mode == MASKED:
                sp.dma_start(yt[:, :], a["L0_gnn_y"]).then_inc(y_in, 16)
            with sp.Fori(0, NB) as ib:
                for k in range(NCH):
                    sp.wait_ge(wts_used if mode == PLAIN else adj_used, ib * NCH + (k + 1))
                    sp.dma_start(adj[:, k % 2, :], a["adj"][bass.ds(ib, 1), :, k * KC:(k + 1) * KC]
                                 .rearrange("b p n -> (b p) n")).then_inc(adj_in[k % 2], 16)

        @block.tensor
        def _(pe):
            pe.sem_inc(wts_used, 2)
            pe.wait_ge(src_ready, 1)
            with pe.Fori(0, NB) as ib:
                pe.wait_ge(acc_free, ib + 1)
                for k in range(NCH):
                    if mode == MASKED:
                        if k == 0:
                            pe.wait_ge(yb_ready, ib + 1)
                        for j in range(CH // 2):
                            pe.wait_ge(labels_used, ib * (T // 2) + (k * CH // 2 + j + 1))
                            for s in range(2):
                                t = k * CH + 2 * j + s
                                mm = pe.matmul(m.acc[2 + j][:, s, :], yt[:, t * P:(t + 1) * P], yb[:, :], start=True, stop=True)
                            mm.then_inc(labels_ready, 1)
                    if mode == PLAIN:
                        pe.wait_ge(adj_in[k % 2], (ib * (NCH // 2) + (k // 2 + 1)) * 16)
                    else:
                        pe.wait_ge(wts_ready, ib * NCH + (k + 1))
                    for j in range(CH):
                        for it in range(BT):
                            at = j * W + it * P
                            mm = pe.matmul(m.acc[it // 2][:, it % 2, 0:D], wts[:, k % 2, at:at + P], src[:, k * CH + j, :],
                                           start=(k + j == 0), stop=(k == NCH - 1 and j == CH - 1))
                    mm.then_inc(wts_used, 1)
                if mode == MASKED:
                    pe.wait_ge(labels_used, ib * (T // 2) + (T // 2 + 2))
                    pe.wait_ge(abs_step, ib * (2 * NCH * CH + 1) + (2 * NCH * CH + 1))
                    for it in range(BT):
                        mm = pe.matmul(m.acc[2][:, 0, it:it + 1], abs_sum[:, it * P:(it + 1) * P], m.ones[:, :], start=True, stop=True)
                    mm.then_inc(rows_ready, 1)

        @block.scalar
        def _(act):
            act.activation(src[:, :, :], m.agg[:, :, :], ACT.Copy).then_inc(src_ready, 1)
            if mode == MASKED:
                act.wait_ge(y_in, 16)
                with act.Fori(0, NB) as ib:
                    act.wait_ge(labels_ready, ib * (T // 2) + 1)
                    act.activation(yb[:, :], yt[:, bass.ds(ib * W, W)], ACT.Copy).then_inc(yb_ready, 1)
            if mode == SENSITIVE:
                with act.Fori(0, NB) as ib:
                    for k in range(NCH):
                        act.wait_ge(inv_ready, ib * NCH + (k + 1))
                        act.activation(inv[:, :], inv[:, :], ACT.Square).then_inc(exp_ready, 1)
                        act.wait_ge(exp_ready, ib * 2 * NCH + (2 * k + 1))
                        act.activation(inv[:, :], inv[:, :], ACT.Exp, scale=-2.0).then_inc(exp_ready, 1)

        @block.vector
        def _(dve):
            dve.sem_inc(adj_used, 2)
            dve.sem_inc(labels_used, 2)
            dve.sem_inc(acc_free, 1)
            if mode == MASKED:
                dve.sem_inc(labels_ready, 1)
                dve.wait_ge(y_in, 16)
            dve.wait_ge(src_ready, 1)
            with dve.Fori(0, NB) as ib:
                if mode == MASKED:
                    dve.memset(abs_sum[:, :], 0.0).then_inc(abs_step, 1)
                for k in range(NCH) if mode != PLAIN else ():
                    dve.wait_ge(adj_in[k % 2], (ib * (NCH // 2) + (k // 2 + 1)) * 16)
                    dve.wait_ge(wts_used, ib * NCH + (k + 1))
                    if mode == MASKED:
                        for j in range(CH // 2):
                            dve.wait_ge(labels_ready, ib * (T // 2) + (k * CH // 2 + j + 2))
                            at = slice(2 * j * W, 2 * (j + 1) * W)
                            dve.tensor_tensor(wts[:, k % 2, at].rearrange("p (s n) -> p s n", s=2),
                                              adj[:, k % 2, at].rearrange("p (s n) -> p s n", s=2),
                                              m.acc[2 + j][:, :, :], ALU.mult).then_inc(labels_used, 1)
                        dve.wait_ge(labels_used, ib * (T // 2) + ((k + 1) * CH // 2 + 2))
                        dve.nop(nofuse=True)
                        dve.engine_nop().then_inc(adj_used, 1)
                        dve.engine_nop().then_inc(wts_ready, 1)
                        for j in range(CH):
                            step = 2 * (k * CH + j)
                            dve.wait_ge(abs_step, ib * (2 * NCH * CH + 1) + (step + 1))
                            part = wts[:, k % 2, j * W:(j + 1) * W]
                            dve.scalar_tensor_tensor(out=magnitude[:, :], in0=part, scalar=-1.0, in1=part,
                                                     op0=ALU.mult, op1=ALU.max).then_inc(abs_step, 1)
                            dve.wait_ge(abs_step, ib * (2 * NCH * CH + 1) + (step + 2))
                            dve.tensor_tensor(abs_sum[:, :], abs_sum[:, :], magnitude[:, :], ALU.add).then_inc(abs_step, 1)
                    else:
                        n = 3 * k
                        dve.tensor_scalar(wts[:, k % 2, :], adj[:, k % 2, :], 0.0, 1e-18, ALU.is_equal, ALU.mult).then_inc(sens_step, 1)
                        dve.wait_ge(sens_step, ib * 3 * NCH + (n + 1))
                        dve.tensor_tensor(wts[:, k % 2, :], wts[:, k % 2, :], adj[:, k % 2, :], ALU.add).then_inc(sens_step, 1)
                        dve.wait_ge(sens_step, ib * 3 * NCH + (n + 2))
                        dve.reciprocal(inv[:, :], wts[:, k % 2, :]).then_inc(sens_step, 1)
                        dve.wait_ge(sens_step, ib * 3 * NCH + (n + 3))
                        dve.tensor_scalar(inv[:, :], inv[:, :], -1.0, None, ALU.add).then_inc(inv_ready, 1)
                        dve.wait_ge(exp_ready, ib * 2 * NCH + (2 * k + 2))
                        dve.scalar_tensor_tensor(out=wts[:, k % 2, :], in0=adj[:, k % 2, :], scalar=1.0, in1=inv[:, :],
                                                 op0=ALU.is_lt, op1=ALU.mult).then_inc(wts_ready, 1)
                        dve.wait_ge(wts_ready, ib * NCH + (k + 1))
                        dve.nop(nofuse=True)
                        dve.engine_nop().then_inc(adj_used, 1)
                dve.wait_ge(wts_used, ib * NCH + (NCH + 2))
                for b in range(2):
                    last = dve.tensor_copy(m.agg[:, bass.ds(ib * BT + 2 * b, 2), :], m.acc[b][:, :, 0:D])
                if mode == MASKED:
                    dve.wait_ge(rows_ready, ib + 1)
                    last = dve.tensor_copy(m.rows[:, bass.ds(ib * BT, BT)], m.acc[2][:, 0, 0:BT])
                last.then_inc(acc_free, 1)


def message(nc, m, a):
    with ExitStack() as ctx:
        sem = lambda name: ctx.enter_context(nc.semaphore(name))
        sb = lambda name, shape: ctx.enter_context(nc.sbuf_tensor(name, shape, FP32))
        w3, b3 = sb("l3_w", [P, D]), sb("l3_b", [P, D])
        blk, blk_t = sb("l3_blk", [P, BT * D]), sb("l3_blk_t", [P, W])
        w3_in, blk_ready, t_full, t_free, mx_full, mx_free = (
            sem("w3_in"), sem("l3_blk_ready"), sem("l3_t_full"), sem("l3_t_free"), sem("l3_mx_full"), sem("l3_mx_free"))
        block = ctx.enter_context(nc.Block())

        @block.sync
        def _(sp):
            sp.dma_start(w3[:, :], a["L3_gnn_W"]).then_inc(w3_in, 16)
            sp.dma_start(b3[:, :], a["L3_gnn_B"]).then_inc(w3_in, 16)

        @block.scalar
        def _(act):
            with act.Fori(0, NB) as ib:
                act.wait_ge(mx_free, ib + 1)
                act.activation(blk[:, :], m.agg[:, bass.ds(ib * BT, BT), :], ACT.Copy, scale=1.0 / HS).then_inc(blk_ready, 1)
                act.wait_ge(t_full, ib + 1)
                act.activation(blk_t[:, :], m.acc[0][:, 0, :], ACT.Copy).then_inc(t_free, 1)

        @block.tensor
        def _(pe):
            pe.wait_ge(w3_in, 32)
            with pe.Fori(0, NB) as ib:
                pe.wait_ge(blk_ready, ib + 1)
                for t in range(BT):
                    mm = pe.transpose(m.acc[0][:, 0, t * P:(t + 1) * P], blk[:, t * D:(t + 1) * D], m.ident[:, :])
                mm.then_inc(t_full, 1)
                pe.wait_ge(t_free, ib + 1)
                for t in range(BT):
                    mm = pe.matmul(m.acc[1][:, 0, t * P:(t + 1) * P], blk_t[:, t * P:(t + 1) * P], w3[:, :], start=True, stop=True)
                mm.then_inc(mx_full, 1)

        @block.vector
        def _(dve):
            dve.sem_inc(mx_free, 1)
            dve.wait_ge(w3_in, 32)
            with dve.Fori(0, NB) as ib:
                dve.wait_ge(mx_full, ib + 1)
                dve.tensor_tensor(m.agg[:, bass.ds(ib * BT, BT), :], m.acc[1][:, 0, :].rearrange("p (t d) -> p t d", d=D),
                                  b3[:, :].unsqueeze(1).to_broadcast([P, BT, D]), ALU.add).then_inc(mx_free, 1)


def add_agg(nc, m):
    with ExitStack() as ctx:
        added = ctx.enter_context(nc.semaphore("added"))
        block = ctx.enter_context(nc.Block())

        @block.vector
        def _(dve):
            dve.tensor_tensor(m.x[:, :, :], m.x[:, :, :], m.agg[:, :, :], ALU.add).then_inc(added, 1)
            dve.wait_ge(added, 1)


def clear_semaphores(nc):
    used = sorted(nc.released_uncleared_semaphores)
    block = nc.Block()
    with block:
        @block.gpsimd
        def _(pool):
            pool.sem_clear(range(used[0], used[-1] + 1))

        @block.scalar
        def _(act):
            act.nop()

        @block.tensor
        def _(pe):
            pe.nop()

        @block.vector
        def _(dve):
            dve.nop()

        @block.sync
        def _(sp):
            sp.nop()


def reload_x(nc, m, a):
    with ExitStack() as ctx:
        x_again = ctx.enter_context(nc.semaphore("x_again"))
        block = ctx.enter_context(nc.Block())

        @block.sync
        def _(sp):
            sp.dma_start(m.x[:, :, :], a["x"].rearrange("p (t d) -> p t d", d=D)).then_inc(x_again, 16)
            sp.wait_ge(x_again, 16)


def binary_path(nc, m, a, out):
    setup(nc, m, a)
    aggregate_masked(nc, m, a)
    with ExitStack() as ctx:
        weights = MambaWeights(nc, ctx, "fast")
        aggregate_compact(nc, m, a, True, "l1", weights=weights)
        mamba(nc, m, a, weights, 1.0 / HS, "fast")
    hyperbolic_in(nc, m, a, "fast")
    aggregate_compact(nc, m, a, False, "l2", out=out)


def general_path(nc, m, a):
    clear_semaphores(nc)
    reload_x(nc, m, a)
    layernorm_phase(nc, m, "g0")
    aggregate_any(nc, m, a, MASKED, "g0")
    after_l0(nc, m, a)
    clear_semaphores(nc)
    layernorm_phase(nc, m, "g1")
    aggregate_any(nc, m, a, PLAIN, "g1")
    with ExitStack() as ctx:
        weights = MambaWeights(nc, ctx, "any")
        load_weights(nc, a, weights)
        mamba(nc, m, a, weights, 1.0 / HS, "any")
    clear_semaphores(nc)
    hyperbolic_in(nc, m, a, "any")
    aggregate_any(nc, m, a, PLAIN, "g2")
    hyperbolic_out(nc, m, 1.0 / HS)
    clear_semaphores(nc)
    layernorm_phase(nc, m, "g3")
    message(nc, m, a)
    aggregate_any(nc, m, a, SENSITIVE, "g3")
    add_agg(nc, m)


def load_weights(nc, a, weights):
    with nc.Block() as block:
        @block.sync
        def _(sp):
            weights.load(sp, a)


def program(nc, a, out):
    with ExitStack() as ctx:
        m = Memory(nc, ctx)
        binary_path(nc, m, a, out)
        other = nc.values_load(m.flag[0:1, 0:1], min_val=0, max_val=1)
        with nc.If(other > 0):
            general_path(nc, m, a)
            store_x(nc, m, out)


def laid_out(x):
    import numpy as np
    rows = np.zeros((NP, x.shape[1]), x.dtype)
    rows[:N] = x
    return np.ascontiguousarray(rows.reshape(T, P, x.shape[1]).transpose(1, 0, 2).reshape(P, -1))


def halves(v):
    import numpy as np
    return np.ascontiguousarray(v.reshape(2, P, -1).transpose(1, 0, 2).reshape(P, -1))


def on_all(v):
    import numpy as np
    return np.ascontiguousarray(np.broadcast_to(v.reshape(1, -1), (P, v.size)))


def kernel(**inputs):
    import numpy as np
    import concourse.bacc as bacc
    from concourse.bass_utils import run_bass_kernel_spmd as run

    g = {k: np.asarray(v) for k, v in inputs.items()}
    adj = np.zeros((NP, NP), g["adj"].dtype)
    adj[:N, :N] = g["adj"]
    adj = np.ascontiguousarray(adj.reshape(NB, W, T, P).transpose(0, 3, 2, 1).reshape(NB, P, T * W))
    y = np.zeros((CLS, NP), g["L0_gnn_y"].dtype)
    y[:, :N] = g["L0_gnn_y"].T
    w_xp = g["L1_gnn_w_xp"]
    dt_cols, b_cols, c_cols = w_xp[:, :RANK], w_xp[:, RANK:RANK + ST], w_xp[:, RANK + ST:]
    arrays = {
        "x": laid_out(g["x"]), "adj": adj, "L0_gnn_h0": laid_out(g["L0_gnn_h0"]), "L0_gnn_y": y,
        "L1_gnn_gcn_w": g["L1_gnn_gcn_w"], "L1_gnn_gcn_b": on_all(g["L1_gnn_gcn_b"]),
        "L1_gnn_ln_g": g["L1_gnn_ln_g"].reshape(P, 1), "L1_gnn_ln_b": g["L1_gnn_ln_b"].reshape(P, 1),
        "L1_gnn_w_in": g["L1_gnn_w_in"], "L1_gnn_conv_w": halves(g["L1_gnn_conv_w"]), "L1_gnn_conv_b": halves(g["L1_gnn_conv_b"]),
        "w_cb": halves(np.concatenate([c_cols, b_cols] * 3, axis=1)), "w_r": halves(dt_cols),
        "L1_gnn_w_dt": g["L1_gnn_w_dt"], "L1_gnn_b_dt": halves(g["L1_gnn_b_dt"]), "L1_gnn_A_log": halves(g["L1_gnn_A_log"]),
        "L1_gnn_D_skip": halves(g["L1_gnn_D_skip"]), "L1_gnn_w_out": halves(g["L1_gnn_w_out"]),
        "L2_gnn_weight": np.ascontiguousarray(g["L2_gnn_weight"].T), "L2_gnn_bias": on_all(g["L2_gnn_bias"]),
        "L3_gnn_W": g["L3_gnn_W"], "L3_gnn_B": on_all(g["L3_gnn_B"]),
    }
    nc = bacc.Bacc("TRN2", target_bir_lowering=False, num_devices=1)
    a = {k: nc.dram_tensor(f"in_{k}", v.shape, mybir.dt.from_np(v.dtype), kind="ExternalInput").ap() for k, v in arrays.items()}
    out = nc.dram_tensor("out_0", (P, T * D), FP32, kind="ExternalOutput").ap()
    program(nc, a, out)
    r = run(nc, [{f"in_{k}": np.ascontiguousarray(v) for k, v in arrays.items()}], core_ids=[0])
    return np.ascontiguousarray(r.results[0]["out_0"].reshape(P, T, D).transpose(1, 0, 2).reshape(NP, D)[:N])
```
